# Optimizing a Trainium2 kernel written in Bass

```python
import numpy as np
import jax
import jax.numpy as jnp

def _softmax(x, axis=-1):
    return jax.nn.softmax(x, axis=axis)

def _gelu(x):
    return jax.nn.gelu(x, approximate=True)

def _silu(x):
    return jax.nn.silu(x)

def _sigmoid(x):
    return jax.nn.sigmoid(x)

def _layernorm(x, axis=-1, eps=1e-05):
    m = jnp.mean(x, axis=axis, keepdims=True)
    v = jnp.var(x, axis=axis, keepdims=True)
    return (x - m) / jnp.sqrt(v + eps)

def _scatter_add(tgt, idx, src, axis=0):
    return tgt.at[idx].add(src)

def _segment_sum(src, seg, n):
    return jax.ops.segment_sum(src, seg, n)
kernel_name = 'mk_adj_ffn_d2_adj_r2_d947f9'

def setup_inputs(seed: int=0):
    np.random.seed(seed)
    _w = jnp.asarray

    def _rec_inputs():
        import jax
        import jax.numpy as jnp
        _gk = jax.random.key(seed)
        x = -0.0005207 + 1.001 * jax.random.normal(jax.random.fold_in(_gk, 1), (128, 128, 128), jnp.float32)
        _a = jax.random.bernoulli(jax.random.fold_in(_gk, 2), 0.0625, (128, 128, 128))
        _a = jnp.logical_or(_a, jnp.swapaxes(_a, -1, -2))
        _a = jnp.logical_or(_a, jnp.eye(128, dtype=bool))
        adj = _a.astype(jnp.int32)
        return (x, adj)
    x, adj = _rec_inputs()

    def _L0_gnn_setup():
        import jax, jax.numpy as jnp
        import numpy as np
        B, N, F_IN, F_OUT = (1, 4096, 128, 128)
        ALPHA = 0.2
        NEG_INF = -9000000000000000.0
        key = jax.random.key(seed)
        ks = jax.random.split(key, 8)
        feat = jax.random.normal(ks[0], (B, N, F_IN), dtype=jnp.float32)
        adj = jax.random.randint(ks[1], (B, N, N), 0, 2, dtype=jnp.int32)
        s = 1.414 * (6.0 / (F_IN + F_OUT)) ** 0.5
        W = jax.random.uniform(ks[2], (F_IN, F_OUT), minval=-s, maxval=s, dtype=jnp.float32)
        a_1 = jax.random.normal(ks[3], (F_OUT, 1), dtype=jnp.float32) * 0.1
        a_2 = jax.random.normal(ks[4], (F_OUT, 1), dtype=jnp.float32) * 0.1
        a_12 = jax.random.normal(ks[5], (F_OUT, F_OUT), dtype=jnp.float32) * (1.0 / F_OUT ** 0.5)
        W_1 = jax.random.uniform(ks[6], (F_IN, F_OUT), minval=-s, maxval=s, dtype=jnp.float32)
        W_2 = jax.random.uniform(ks[7], (F_IN, F_OUT), minval=-s, maxval=s, dtype=jnp.float32)
        return {'feat': feat, 'adj': adj, 'W': W, 'a_1': a_1, 'a_2': a_2, 'a_12': a_12, 'W_1': W_1, 'W_2': W_2}
    _L0_gnn_all = _L0_gnn_setup()
    _L0_gnn_in = {k: v for k, v in _L0_gnn_all.items() if k in ('W', 'a_1', 'a_2', 'a_12', 'W_1', 'W_2')}
    del _L0_gnn_all

    def _L0_ffn_setup():
        import jax, jax.numpy as jnp
        import numpy as np
        B, N, D = (16, 2048, 128)
        NUM_EXPERTS, TOP_K, HEADS = (4, 2, 4)
        N_EDGES = 524288
        LN_EPS = 1e-05

        def _layernorm(x, g, b):
            mu = x.mean(-1, keepdims=True)
            var = ((x - mu) ** 2).mean(-1, keepdims=True)
            return (x - mu) * jax.lax.rsqrt(var + LN_EPS) * g + b

        def _forward(x, edge_index, W_gat, att_src, att_dst, b_gat, ln_gamma, ln_beta, W1, b1, W2, b2):
            Bc, Nc, Dc = x.shape
            M = Bc * Nc
            x_flat = x.reshape(M, Dc)
            h = (x_flat @ W_gat).reshape(M, HEADS, NUM_EXPERTS)
            loops = jnp.arange(M, dtype=edge_index.dtype)
            src = jnp.concatenate([edge_index[0], loops])
            dst = jnp.concatenate([edge_index[1], loops])
            a_src = (h * att_src).sum(-1)
            a_dst = (h * att_dst).sum(-1)
            e = jax.nn.leaky_relu(a_src[src] + a_dst[dst], negative_slope=0.2)
            e_max = jax.ops.segment_max(e, dst, num_segments=M)
            ee = jnp.exp(e - e_max[dst])
            denom = jax.ops.segment_sum(ee, dst, num_segments=M)
            alpha = ee / (denom[dst] + 1e-16)
            msg = h[src] * alpha[:, :, None]
            agg = jax.ops.segment_sum(msg, dst, num_segments=M).reshape(M, HEADS * NUM_EXPERTS) + b_gat
            scores = _layernorm(agg, ln_gamma, ln_beta).reshape(M, HEADS, NUM_EXPERTS).mean(1)
            scores = scores.reshape(Bc, Nc, NUM_EXPERTS)
            topk_s, topk_i = jax.lax.top_k(scores, TOP_K)
            w = jax.nn.softmax(topk_s, axis=-1)
            out = jnp.zeros_like(x)
            for ei in range(NUM_EXPERTS):
                g = jnp.where(topk_i == ei, w, 0.0).sum(-1)
                hh = jax.nn.gelu(x @ W1[ei] + b1[ei], approximate=False)
                out = out + g[..., None] * (hh @ W2[ei] + b2[ei])
            return out
        key = jax.random.key(seed)
        ks = jax.random.split(key, 8)
        s = 0.05
        return {'x': jax.random.normal(ks[0], (B, N, D), jnp.float32), 'W_gat': jax.random.normal(ks[1], (D, HEADS * NUM_EXPERTS), jnp.float32) * s, 'att_src': jax.random.normal(ks[2], (HEADS, NUM_EXPERTS), jnp.float32) * s, 'att_dst': jax.random.normal(ks[3], (HEADS, NUM_EXPERTS), jnp.float32) * s, 'b_gat': jnp.zeros((HEADS * NUM_EXPERTS,), jnp.float32), 'ln_gamma': jnp.ones((HEADS * NUM_EXPERTS,), jnp.float32), 'ln_beta': jnp.zeros((HEADS * NUM_EXPERTS,), jnp.float32), 'W1': jax.random.normal(ks[4], (NUM_EXPERTS, D, 2 * D), jnp.float32) * s, 'b1': jnp.zeros((NUM_EXPERTS, 2 * D), jnp.float32), 'W2': jax.random.normal(ks[5], (NUM_EXPERTS, 2 * D, D), jnp.float32) * s, 'b2': jnp.zeros((NUM_EXPERTS, D), jnp.float32), 'edge_index': jax.random.randint(ks[6], (2, N_EDGES), 0, B * N, jnp.int32)}
    _L0_ffn_all = _L0_ffn_setup()
    _L0_ffn_in = {k: v for k, v in _L0_ffn_all.items() if k in ('W_gat', 'att_src', 'att_dst', 'b_gat', 'ln_gamma', 'ln_beta', 'W1', 'b1', 'W2', 'b2', 'edge_index')}
    del _L0_ffn_all

    def _L1_gnn_setup():
        import jax, jax.numpy as jnp
        import numpy as np
        DIM = 128
        HEADS = 8
        HEAD_DIM = DIM // HEADS
        DFF = 4 * DIM
        EPS = 1e-05

        def _layernorm(x, g, b):
            m = jnp.mean(x, axis=-1, keepdims=True)
            v = jnp.mean(jnp.square(x - m), axis=-1, keepdims=True)
            return (x - m) * jax.lax.rsqrt(v + EPS) * g + b
        key = jax.random.key(seed)
        ks = jax.random.split(key, 12)
        B, N = (8, 512)
        s = 1.0 / np.sqrt(DIM)
        x = jax.random.normal(ks[0], (B, N, DIM), dtype=jnp.float32)
        adj = jax.random.randint(ks[1], (B, N, N), 0, 2, dtype=jnp.int32)
        return {'x': x, 'adj': adj, 'Wqkv': jax.random.normal(ks[2], (3 * DIM, DIM), jnp.float32) * s, 'bqkv': jnp.zeros((3 * DIM,), jnp.float32), 'Wo': jax.random.normal(ks[3], (DIM, DIM), jnp.float32) * s, 'bo': jnp.zeros((DIM,), jnp.float32), 'ln1_g': jnp.ones((DIM,), jnp.float32), 'ln1_b': jnp.zeros((DIM,), jnp.float32), 'W1': jax.random.normal(ks[4], (DFF, DIM), jnp.float32) * s, 'b1': jnp.zeros((DFF,), jnp.float32), 'W2': jax.random.normal(ks[5], (DIM, DFF), jnp.float32) * (1.0 / np.sqrt(DFF)), 'b2': jnp.zeros((DIM,), jnp.float32), 'ln2_g': jnp.ones((DIM,), jnp.float32), 'ln2_b': jnp.zeros((DIM,), jnp.float32)}
    _L1_gnn_all = _L1_gnn_setup()
    _L1_gnn_in = {k: v for k, v in _L1_gnn_all.items() if k in ('Wqkv', 'bqkv', 'Wo', 'bo', 'ln1_g', 'ln1_b', 'W1', 'b1', 'W2', 'b2', 'ln2_g', 'ln2_b')}
    del _L1_gnn_all

    def _L1_ffn_setup():
        import jax, jax.numpy as jnp
        import numpy as np
        B, S, D, F, E, K = (8, 1024, 128, 512, 8, 2)
        key = jax.random.key(seed)
        ks = jax.random.split(key, 10)
        s = 0.02
        return {'x': jax.random.normal(ks[0], (B, S, D), dtype=jnp.float32), 'Wr': jax.random.normal(ks[1], (D, E), dtype=jnp.float32) * s, 'W1s': jax.random.normal(ks[2], (D, F), dtype=jnp.float32) * s, 'b1s': jnp.zeros((F,), dtype=jnp.float32), 'W2s': jax.random.normal(ks[3], (F, D), dtype=jnp.float32) * s, 'b2s': jnp.zeros((D,), dtype=jnp.float32), 'W1p': jax.random.normal(ks[4], (E, D, F), dtype=jnp.float32) * s, 'b1p': jnp.zeros((E, F), dtype=jnp.float32), 'W2p': jax.random.normal(ks[5], (E, F, D), dtype=jnp.float32) * s, 'b2p': jnp.zeros((E, D), dtype=jnp.float32)}
    _L1_ffn_all = _L1_ffn_setup()
    _L1_ffn_in = {k: v for k, v in _L1_ffn_all.items() if k in ('Wr', 'W1s', 'b1s', 'W2s', 'b2s', 'W1p', 'b1p', 'W2p', 'b2p')}
    del _L1_ffn_all
    return {'x': x, 'adj': adj, 'L0_gnn_W': _L0_gnn_in['W'], 'L0_gnn_a_1': _L0_gnn_in['a_1'], 'L0_gnn_a_2': _L0_gnn_in['a_2'], 'L0_gnn_a_12': _L0_gnn_in['a_12'], 'L0_gnn_W_1': _L0_gnn_in['W_1'], 'L0_gnn_W_2': _L0_gnn_in['W_2'], 'L0_ffn_W_gat': _L0_ffn_in['W_gat'], 'L0_ffn_att_src': _L0_ffn_in['att_src'], 'L0_ffn_att_dst': _L0_ffn_in['att_dst'], 'L0_ffn_b_gat': _L0_ffn_in['b_gat'], 'L0_ffn_ln_gamma': _L0_ffn_in['ln_gamma'], 'L0_ffn_ln_beta': _L0_ffn_in['ln_beta'], 'L0_ffn_W1': _L0_ffn_in['W1'], 'L0_ffn_b1': _L0_ffn_in['b1'], 'L0_ffn_W2': _L0_ffn_in['W2'], 'L0_ffn_b2': _L0_ffn_in['b2'], 'L0_ffn_edge_index': _L0_ffn_in['edge_index'], 'L1_gnn_Wqkv': _L1_gnn_in['Wqkv'], 'L1_gnn_bqkv': _L1_gnn_in['bqkv'], 'L1_gnn_Wo': _L1_gnn_in['Wo'], 'L1_gnn_bo': _L1_gnn_in['bo'], 'L1_gnn_ln1_g': _L1_gnn_in['ln1_g'], 'L1_gnn_ln1_b': _L1_gnn_in['ln1_b'], 'L1_gnn_W1': _L1_gnn_in['W1'], 'L1_gnn_b1': _L1_gnn_in['b1'], 'L1_gnn_W2': _L1_gnn_in['W2'], 'L1_gnn_b2': _L1_gnn_in['b2'], 'L1_gnn_ln2_g': _L1_gnn_in['ln2_g'], 'L1_gnn_ln2_b': _L1_gnn_in['ln2_b'], 'L1_ffn_Wr': _L1_ffn_in['Wr'], 'L1_ffn_W1s': _L1_ffn_in['W1s'], 'L1_ffn_b1s': _L1_ffn_in['b1s'], 'L1_ffn_W2s': _L1_ffn_in['W2s'], 'L1_ffn_b2s': _L1_ffn_in['b2s'], 'L1_ffn_W1p': _L1_ffn_in['W1p'], 'L1_ffn_b1p': _L1_ffn_in['b1p'], 'L1_ffn_W2p': _L1_ffn_in['W2p'], 'L1_ffn_b2p': _L1_ffn_in['b2p']}

def reference(x, adj, L0_gnn_W, L0_gnn_a_1, L0_gnn_a_2, L0_gnn_a_12, L0_gnn_W_1, L0_gnn_W_2, L0_ffn_W_gat, L0_ffn_att_src, L0_ffn_att_dst, L0_ffn_b_gat, L0_ffn_ln_gamma, L0_ffn_ln_beta, L0_ffn_W1, L0_ffn_b1, L0_ffn_W2, L0_ffn_b2, L0_ffn_edge_index, L1_gnn_Wqkv, L1_gnn_bqkv, L1_gnn_Wo, L1_gnn_bo, L1_gnn_ln1_g, L1_gnn_ln1_b, L1_gnn_W1, L1_gnn_b1, L1_gnn_W2, L1_gnn_b2, L1_gnn_ln2_g, L1_gnn_ln2_b, L1_ffn_Wr, L1_ffn_W1s, L1_ffn_b1s, L1_ffn_W2s, L1_ffn_b2s, L1_ffn_W1p, L1_ffn_b1p, L1_ffn_W2p, L1_ffn_b2p):
    import jax
    import jax.numpy as jnp

    def _L0_gnn_ref(feat, adj, W, a_1, a_2, a_12, W_1, W_2):
        import jax, jax.numpy as jnp
        import numpy as np
        B, N, F_IN, F_OUT = (1, 4096, 128, 128)
        ALPHA = 0.2
        NEG_INF = -9000000000000000.0
        h = jnp.matmul(feat, W)
        Ax = jnp.matmul(h, a_1)
        Ay = jnp.matmul(h, a_2)
        A_xy = jnp.matmul(jnp.matmul(h, a_12), jnp.swapaxes(h, 1, 2))
        logits = jnp.swapaxes(Ax, 1, 2) + Ay + A_xy
        e = jax.nn.leaky_relu(logits, negative_slope=ALPHA)
        e = jnp.where(adj > 0, e, NEG_INF)
        attention = jax.nn.softmax(e, axis=-1)
        h_prime = jnp.matmul(attention, feat)
        h_out = jnp.matmul(feat, W_1) + jnp.matmul(h_prime, W_2)
        return jax.nn.elu(h_out)

    def _L0_ffn_ref(x, W_gat, att_src, att_dst, b_gat, ln_gamma, ln_beta, W1, b1, W2, b2, edge_index):
        import jax, jax.numpy as jnp
        import numpy as np
        B, N, D = (16, 2048, 128)
        NUM_EXPERTS, TOP_K, HEADS = (4, 2, 4)
        N_EDGES = 524288
        LN_EPS = 1e-05

        def _layernorm(x, g, b):
            mu = x.mean(-1, keepdims=True)
            var = ((x - mu) ** 2).mean(-1, keepdims=True)
            return (x - mu) * jax.lax.rsqrt(var + LN_EPS) * g + b

        def _forward(x, edge_index, W_gat, att_src, att_dst, b_gat, ln_gamma, ln_beta, W1, b1, W2, b2):
            Bc, Nc, Dc = x.shape
            M = Bc * Nc
            x_flat = x.reshape(M, Dc)
            h = (x_flat @ W_gat).reshape(M, HEADS, NUM_EXPERTS)
            loops = jnp.arange(M, dtype=edge_index.dtype)
            src = jnp.concatenate([edge_index[0], loops])
            dst = jnp.concatenate([edge_index[1], loops])
            a_src = (h * att_src).sum(-1)
            a_dst = (h * att_dst).sum(-1)
            e = jax.nn.leaky_relu(a_src[src] + a_dst[dst], negative_slope=0.2)
            e_max = jax.ops.segment_max(e, dst, num_segments=M)
            ee = jnp.exp(e - e_max[dst])
            denom = jax.ops.segment_sum(ee, dst, num_segments=M)
            alpha = ee / (denom[dst] + 1e-16)
            msg = h[src] * alpha[:, :, None]
            agg = jax.ops.segment_sum(msg, dst, num_segments=M).reshape(M, HEADS * NUM_EXPERTS) + b_gat
            scores = _layernorm(agg, ln_gamma, ln_beta).reshape(M, HEADS, NUM_EXPERTS).mean(1)
            scores = scores.reshape(Bc, Nc, NUM_EXPERTS)
            topk_s, topk_i = jax.lax.top_k(scores, TOP_K)
            w = jax.nn.softmax(topk_s, axis=-1)
            out = jnp.zeros_like(x)
            for ei in range(NUM_EXPERTS):
                g = jnp.where(topk_i == ei, w, 0.0).sum(-1)
                hh = jax.nn.gelu(x @ W1[ei] + b1[ei], approximate=False)
                out = out + g[..., None] * (hh @ W2[ei] + b2[ei])
            return out
        return _forward(x, edge_index, W_gat, att_src, att_dst, b_gat, ln_gamma, ln_beta, W1, b1, W2, b2)

    def _L1_gnn_ref(x, adj, Wqkv, bqkv, Wo, bo, ln1_g, ln1_b, W1, b1, W2, b2, ln2_g, ln2_b):
        import jax, jax.numpy as jnp
        import numpy as np
        DIM = 128
        HEADS = 8
        HEAD_DIM = DIM // HEADS
        DFF = 4 * DIM
        EPS = 1e-05

        def _layernorm(x, g, b):
            m = jnp.mean(x, axis=-1, keepdims=True)
            v = jnp.mean(jnp.square(x - m), axis=-1, keepdims=True)
            return (x - m) * jax.lax.rsqrt(v + EPS) * g + b
        B, N, _ = x.shape
        eye = jnp.eye(N, dtype=bool)[None]
        allowed = (adj > 0) | (jnp.swapaxes(adj, 1, 2) > 0) | eye
        qkv = x @ Wqkv.T + bqkv
        q, k, v = jnp.split(qkv, 3, axis=-1)

        def heads(t):
            return t.reshape(B, N, HEADS, HEAD_DIM).transpose(0, 2, 1, 3)
        q, k, v = (heads(q), heads(k), heads(v))
        scale = 1.0 / np.sqrt(HEAD_DIM)
        scores = jnp.einsum('bhqd,bhkd->bhqk', q * scale, k)
        scores = jnp.where(allowed[:, None], scores, -jnp.inf)
        attn = jax.nn.softmax(scores, axis=-1)
        ctx = jnp.einsum('bhqk,bhkd->bhqd', attn, v)
        ctx = ctx.transpose(0, 2, 1, 3).reshape(B, N, DIM)
        attn_out = ctx @ Wo.T + bo
        x = _layernorm(x + attn_out, ln1_g, ln1_b)
        ff = jax.nn.relu(x @ W1.T + b1) @ W2.T + b2
        x = _layernorm(x + ff, ln2_g, ln2_b)
        return x

    def _L1_ffn_ref(x, Wr, W1s, b1s, W2s, b2s, W1p, b1p, W2p, b2p):
        import jax, jax.numpy as jnp
        import numpy as np
        B, S, D, F, E, K = (8, 1024, 128, 512, 8, 2)
        gelu = lambda t: jax.nn.gelu(t, approximate=False)
        shared = gelu(x @ W1s + b1s) @ W2s + b2s
        rw = jax.nn.softmax(x @ Wr, axis=-1)
        topw, topi = jax.lax.top_k(rw, K)
        topw = topw / jnp.sum(topw, axis=-1, keepdims=True)
        mask = jnp.sum(jax.nn.one_hot(topi, E, dtype=topw.dtype) * topw[..., None], axis=-2)
        h = gelu(jnp.einsum('bsd,edf->bsef', x, W1p) + b1p)
        priv = jnp.einsum('bsef,efd->bsed', h, W2p) + b2p
        routed = jnp.einsum('bsed,bse->bsd', priv, mask)
        return shared + routed
    x = x + _L0_gnn_ref(_layernorm(x, axis=-1), adj, L0_gnn_W, L0_gnn_a_1, L0_gnn_a_2, L0_gnn_a_12, L0_gnn_W_1, L0_gnn_W_2)
    x = x + _L0_ffn_ref(_layernorm(x, axis=-1), L0_ffn_W_gat, L0_ffn_att_src, L0_ffn_att_dst, L0_ffn_b_gat, L0_ffn_ln_gamma, L0_ffn_ln_beta, L0_ffn_W1, L0_ffn_b1, L0_ffn_W2, L0_ffn_b2, L0_ffn_edge_index)
    x = x + _L1_gnn_ref(_layernorm(x, axis=-1), adj, L1_gnn_Wqkv, L1_gnn_bqkv, L1_gnn_Wo, L1_gnn_bo, L1_gnn_ln1_g, L1_gnn_ln1_b, L1_gnn_W1, L1_gnn_b1, L1_gnn_W2, L1_gnn_b2, L1_gnn_ln2_g, L1_gnn_ln2_b)
    x = x + _L1_ffn_ref(_layernorm(x, axis=-1), L1_ffn_Wr, L1_ffn_W1s, L1_ffn_b1s, L1_ffn_W2s, L1_ffn_b2s, L1_ffn_W1p, L1_ffn_b1p, L1_ffn_W2p, L1_ffn_b2p)
    return x

_drawn_inputs = setup_inputs


def setup_inputs(seed=0):
    import zlib

    import numpy as np

    out = dict(_drawn_inputs(seed))
    spreads = {'L0_ffn_b_gat': (0.0, 0.1),
     'L0_ffn_ln_gamma': (1.0, 0.6),
     'L0_ffn_ln_beta': (0.0, 0.412),
     'L0_ffn_b1': (0.0, 0.403),
     'L0_ffn_b2': (0.0, 0.1),
     'L1_gnn_bqkv': (0.0, 0.1),
     'L1_gnn_bo': (0.0, 0.1),
     'L1_gnn_ln1_g': (1.0, 0.2),
     'L1_gnn_ln1_b': (0.0, 0.1),
     'L1_gnn_b1': (0.0, 0.381),
     'L1_gnn_b2': (0.0, 0.1),
     'L1_gnn_ln2_g': (1.0, 0.2),
     'L1_gnn_ln2_b': (0.0, 0.1),
     'L1_ffn_b1s': (0.0, 0.8),
     'L1_ffn_b2s': (0.0, 0.1),
     'L1_ffn_b1p': (0.0, 0.8),
     'L1_ffn_b2p': (0.0, 0.295)}
    factors = {'L0_gnn_a_2': 8.0,
     'L0_ffn_att_src': 8.0,
     'L0_ffn_att_dst': 8.0,
     'L1_ffn_W1s': 2.752,
     'L1_ffn_W1p': 3.939,
     'L1_ffn_W2p': 3.546}
    for name, (base, spread) in spreads.items():
        noise = np.random.default_rng([zlib.crc32(name.encode()), seed]).standard_normal(out[name].shape)
        drawn = base * np.exp(spread * noise) if base else spread * noise
        out[name] = jnp.asarray(drawn.astype(out[name].dtype))
    for name, factor in factors.items():
        out[name] = (out[name] * factor).astype(out[name].dtype)
    return out
```

```python
from contextlib import ExitStack

import numpy as np
import concourse.bass as bass
from concourse import mybir
from concourse.alu_op_type import AluOpType as ALU

ACT = mybir.ActivationFunctionType
AX = mybir.AxisListType.X
F32 = mybir.dt.float32
BF16 = mybir.dt.bfloat16
I32 = mybir.dt.int32
U32 = mybir.dt.uint32

P = 128
Q = 4
T = Q * P
GT = 4
GE = GT * P
ST = 8
RING = 32
H0, E0 = 4, 4
PW = H0 + H0 * (1 + E0)
H1 = 8
HD = P // H1
E1 = 8
FC = 4
EPS = 1e-5
NEG = 9e15
FAR = 1e30
SKIP = float(2**23)


PER = (106, 220)


class Steps:

    def __init__(self, sem, names):
        self.sem, self.names, self.n = sem, {s: k + 1 for k, s in enumerate(names)}, len(names)
        assert len(self.names) == len(names)

    def at(self, i, name):
        return (i + 1) * self.n + self.names[name]


class Chain:

    def __init__(self, sem, per):
        self.sem, self.per, self.n, self.i = sem, per, 0, 0

    def turn(self, i):
        self.i, self.n = i, 0

    def count(self, ins):
        self.n += 1
        ins.then_inc(self.sem, 1)

    def wait(self, eng):
        eng.wait_ge(self.sem, self.i * self.per + self.n)

    def end(self):
        assert self.n == self.per, (self.n, self.per)


def program(nc, a, NB, NE):
    NCH = NB // Q
    M = NB * P
    CE = NE // P // NCH
    SG = CE // ST
    assert SG * ST == CE and SG % 2 == 0
    FR = P * P * 4
    FILLS = 2 * -(-(NE + (NB + 8) * GE) // (2 * FR))
    CAP = FILLS * FR
    TURNS = -(-(NE // GE + NB) // 4)
    FILLED = 16 * FILLS // 2
    sorted_edges = nc.dram_tensor("sorted_edges", (CAP, 2), U32, kind="Internal").ap()
    node_rows = nc.dram_tensor("node_rows", (M, PW), F32, kind="Internal").ap()
    expert_rows = nc.dram_tensor("expert_rows", (M, E0, P), F32, kind="Internal").ap()

    with ExitStack() as ctx:
        def sb(name, shape, dt=F32):
            return ctx.enter_context(nc.sbuf_tensor(name, shape, dt))

        def psum(name, shape, dt=F32):
            return ctx.enter_context(nc.psum_tensor(name, shape, dt))

        def sem(name):
            return ctx.enter_context(nc.semaphore(name))

        X = sb("X", [P, NB, P])
        pay = sb("pay", [P, NB, PW])
        dn = sb("dn", [P, NB, H0])
        dm = sb("dm", [P, NB, 2 * H0])
        ring = sb("ring", [P, RING, GT, PW])
        ringf = ring[:, :, :, :].rearrange("p r k f -> p (r k f)")
        place = {"f_W1": ringf[:, 0:1024].rearrange("p (e f m) -> p e f m", e=E0, f=2),
                 "f_W2": ringf[:, 1024:2048].rearrange("p (e f m) -> p e f m", e=E0, f=2),
                 "g_W": ringf[:, 2048:2176], "g_a12": ringf[:, 2176:2304], "g_W1": ringf[:, 2304:2432],
                 "g_W2": ringf[:, 2432:2560], "f_b2": ringf[0:1, 2560:3072]}
        w = {}
        wl = []
        for name, shape in (
            ("g_W", [P, P]), ("g_a12", [P, P]), ("g_W1", [P, P]), ("g_W2", [P, P]), ("g_a1", [P, 1]), ("g_a2", [P, 1]),
            ("f_Wgat", [P, H0 * E0]), ("f_asrc", [P, H0 * E0]), ("f_adst", [P, H0 * E0]), ("f_bgat", [P, H0 * E0]),
            ("f_gam", [P, H0 * E0]), ("f_bet", [P, H0 * E0]),
            ("f_W1", [P, E0, 2, P]), ("f_b1", [P, E0, 2]), ("f_W2", [P, E0, 2, P]), ("f_b2", [1, E0 * P]),
            ("a_Wqkv", [P, 3 * P]), ("a_bqk", [P, 2]), ("a_bv", [1, P]), ("a_Wo", [P, P]), ("a_bo", [1, P]),
            ("a_g1", [P, P]), ("a_b1", [P, P]), ("a_g2", [P, P]), ("a_b2", [P, P]),
            ("a_W1", [P, FC, P]), ("a_c1", [P, FC]), ("a_W2", [P, FC, P]), ("a_c2", [1, P]),
            ("m_Wr", [P, E1]), ("m_W1", [P, E1 + 1, FC, P]), ("m_b1", [P, E1 + 1, FC]),
            ("m_W2", [P, E1 + 1, FC, P]), ("m_b2", [1, (E1 + 1) * P]),
        ):
            w[name] = place.get(name)
            if w[name] is None:
                w[name] = sb(name, shape)[tuple(slice(None) for _ in shape)]
            wl.append((w[name], a[name]))

        ident = sb("ident", [P, P])
        iota = sb("iota", [P, P], BF16)
        before = sb("before", [P, P], BF16)
        notbefore = sb("notbefore", [P, P], BF16)
        onesb = sb("onesb", [P, P], BF16)
        zerob = sb("zerob", [P, 4 * P], BF16)
        zero = sb("zero", [P, P])
        ones1 = sb("ones1", [1, P])
        headmask = sb("headmask", [P, H1])
        lower = sb("lower", [P, E1, E1])

        adjc = sb("adjc", [P, Q, P], I32)
        srcc = sb("srcc", [P, CE], I32)
        dstc = sb("dstc", [P, CE], I32)
        tmpi = sb("tmpi", [P, CE], I32)
        dhi = sb("dhi", [P, CE])
        far = sb("far", [P, CE])
        rec = sb("rec", [P, CE, 2], U32)
        pos = sb("pos", [P, ST])
        idx = sb("idx", [P, 2, ST], U32)
        recs = sb("recs", [P, 2, ST, 2], U32)
        starts = sb("starts", [P, NB + 1])
        tot = sb("tot", [P, NB])
        toti = sb("toti", [P, NB + 2], I32)
        gstart = sb("gstart", [1, NB + 2], I32)
        bst = sb("bst", [P, Q, 6])
        mv = sb("mv", [P, Q, 2])
        nb_ = sb("nb_", [P, Q, 4])
        nbi = sb("nbi", [P, Q], I32)
        rstd = sb("rstd", [P, Q])
        xn = sb("xn", [P, Q, P])
        xT = sb("xT", [P, T])
        bufA = sb("bufA", [P, T])
        bufB = sb("bufB", [P, T])
        bufC = sb("bufC", [P, T])
        bufD = sb("bufD", [P, T])
        sm = sb("sm", [P, 16])
        small = sb("small", [P, Q * H0 * E0])
        small2 = sb("small2", [P, Q * H0 * E0])
        gmx = sb("gmx", [P, H0])
        gmall = sb("gmall", [P, H0])
        yb = sb("yb", [P, Q, E0, P])
        big1 = sb("big1", [P, 8, P])
        big2 = sb("big2", [P, 8, P])
        big3 = sb("big3", [P, 8, P])

        stage = sb("stage", [P, 2, 2, GT, PW])
        gidx = sb("gidx", [P, 2, 2, GT, 2], U32)
        ring_dst = sb("ring_dst", [P, RING, GT, 2], U32)
        Og = big3[:, 0:GT, :]
        OT = big3[:, GT:2 * GT, :]
        iotaf = sb("iotaf", [P, P])
        zg = sb("zg", [P, GT, H0])
        eg = sb("eg", [P, GT, H0])
        Vg = sb("Vg", [P, GT, H0 * (1 + E0)])
        dmc = sb("dmc", [P, Q, 2 * H0])
        selfc = sb("selfc", [P, Q, H0 * (1 + E0)])
        agg = sb("agg", [P, Q, H0 * (1 + E0)])
        mixw = sb("mixw", [P, Q, E1 + 1])
        gates = sb("gates", [P, Q, E1])
        pairs = big1[:, 0:4, :].rearrange("p a (b c) -> p (a b) c", c=E1)
        cmp1 = pairs[:, 0:Q * E1, :].rearrange("p (q a) c -> p q a c", q=Q)
        cmp2 = pairs[:, Q * E1:2 * Q * E1, :].rearrange("p (q a) c -> p q a c", q=Q)
        vext = sb("vext", [P, Q, H1, HD + 1])
        cden = sb("cden", [P, H1])
        neg = sb("neg", [P, Q, P])
        mxh = sb("mxh", [P, H1])
        hid1 = sb("hid1", [P, FC, T])
        hid = hid1[:, 0:2, :]
        O = hid1[:, 2:4, :].bitcast(BF16).rearrange("p o (k b) -> p o k b", k=ST)

        pR = psum("pR", [P, 8, P])
        pS = psum("pS", [P, 8, P])
        p4 = psum("p4", [P, T])
        p5 = psum("p5", [P, T])
        p6 = psum("p6", [P, T])
        p7 = psum("p7", [P, T])

        weights_in = sem("weights_in")
        edges_in = sem("edges_in")
        x_in = sem("x_in")
        consts = sem("consts")
        counted_onehot = sem("counted_onehot")
        counted = sem("counted")
        bases_ready = sem("bases_ready")
        chunk_in = sem("chunk_in")
        scattered = [sem("scattered0"), sem("scattered1")]
        rows_out = sem("rows_out")
        experts_out = sem("experts_out")
        stores_done = sem("stores_done")
        guard_ready = sem("guard_ready")
        tables_ready = sem("tables_ready")
        passed = sem("passed")
        setup_chain = sem("setup_chain")
        chain1 = sem("chain1")
        chain2 = sem("chain2")
        chaing = sem("chaing")
        chainm = sem("chainm")
        gidx_in = [sem("gidx_in0"), sem("gidx_in1")]
        gathered = [sem("gathered0"), sem("gathered1")]
        ring_out = sem("ring_out")
        ring_filled = sem("ring_filled")
        ring_freed = sem("ring_freed")
        y_in = sem("y_in")
        adj_in = sem("adj_in")
        result_out = sem("result_out")

        vwork = {0: ["xn"], 4: ["masked"], 5: ["prob"], 7: ["zmin", "x1"], 8: ["xn1"], 9: ["pay"]}
        twork = {1: ["xT"], 2: ["hT"], 3: ["gT", "ay"], 4: ["logits"], 6: ["PT", "hpT"], 7: ["hout"], 9: ["xT1", "hrow"]}
        twork |= {10 + e: [f"up0_{e}", f"up1_{e}", f"down{e}"] for e in range(E0)}
        V1 = Steps(sem("vector_1"), [s for g in range(SG) for s in [f"onehot{g}", f"prod{g}", f"idx{g}"] + vwork.get(g, [])])
        T1 = Steps(sem("tensor_1"), [s for g in range(SG) for s in [f"rank{g}", f"ranked{g}"] + twork.get(g, [])])
        A1 = Steps(sem("scalar_1"), ["xT", "hT", "gT", "ay", "exp", "PT", "hpT", "elu", "xT1"]
                   + [f"{s}{e}" for e in range(E0) for s in ("gelu0_", "gelu1_", "y")])
        VG = Steps(sem("vector_g"), ["onehot", "z"])
        TG = Steps(sem("tensor_g"), ["onehotT", "dstscore", "sums"])
        AG = Steps(sem("scalar_g"), ["onehotT", "exp"])
        qs = range(Q)
        V2 = Steps(sem("vector_2"), ["self", "agg", "gexp0", "x2", "xn", "mask", "allowed"]
                   + [f"{s}{q}" for q in qs for s in ("keys", "max", "ctx")]
                   + ["y1", "xn3", "gexp", "gate"] + [f"mix{e}" for e in range(E1 + 1)])
        T2 = Steps(sem("tensor_2"), ["self", "xT", "qT", "kT", "v", "maskT"]
                   + [f"{s}{q}" for q in qs for s in ("scores", "PT", "ctx")]
                   + ["ctxT", "attn", "y1T"] + [f"ffup{f}" for f in range(FC)] + ["ff", "xT3", "router"]
                   + [f"{s}{e}" for e in range(E1 + 1) for s in ("up0_", "up1_", "up2_", "up3_", "down")])
        A2 = Steps(sem("scalar_2"), ["gate0", "xT", "qT", "kT", "v"]
                   + [f"{s}{q}" for q in qs for s in ("exp", "PT")]
                   + ["ctxT", "y1T"] + [f"relu{f}" for f in range(FC)] + ["xT3", "rexp"]
                   + [f"gelu{f}_{e}" for e in range(E1 + 1) for f in range(FC)])

        block = ctx.enter_context(nc.Block())

        sorted_tiles = sorted_edges.rearrange("(g p k) w -> p g k w", p=P, k=GT)

        CH1, CH2 = PER

        @block.sync
        def _(sp):
            def wait(sm_, value):
                sp.wait_ge(sm_, value)
                sp.sem_inc(passed, 1)

            sp.dma_start(X[:, :, :].bitcast(I32).rearrange("p b f -> p (b f)")[:, 0:NE // P],
                         a["edges"][1].rearrange("(p c) -> p c", p=P)).then_inc(edges_in, 16)
            for tile, src in wl:
                sp.dma_start(tile, src).then_inc(weights_in, 16)

            e_view = [a["edges"][r].rearrange("(p c) -> p c", p=P) for r in range(2)]

            def load_chunk(c):
                sp.dma_start(adjc[:, :, :], a["adj"].rearrange("b i j -> i b j")[:, bass.ds(c * Q, Q), :]).then_inc(chunk_in, 16)
                sp.dma_start(srcc[:, :], e_view[0][:, bass.ds(c * CE, CE)]).then_inc(chunk_in, 16)
                sp.dma_start(dstc[:, :], e_view[1][:, bass.ds(c * CE, CE)]).then_inc(chunk_in, 16)

            sp.wait_ge(bases_ready, 1)
            sp.dma_start(X[:, :, :], a["x"].rearrange("b n f -> n b f")).then_inc(x_in, 16)
            load_chunk(0)
            sp.sem_inc(stores_done, 1)
            with sp.Fori(0, NCH) as c:
                wait(V1.sem, V1.at(c, "pay"))
                sp.dma_start(node_rows.rearrange("(b n) w -> n b w", n=P)[:, bass.ds(c * Q, Q), :],
                             pay[:, bass.ds(c * Q, Q), :]).then_inc(rows_out, 16)
                wait(A1.sem, A1.at(c, f"y{E0 - 1}"))
                sp.dma_start(expert_rows.rearrange("(b n) e f -> n b e f", n=P)[:, bass.ds(c * Q, Q), :, :],
                             yb[:, :, :, :]).then_inc(experts_out, 16)
                wait(V1.sem, V1.at(c, f"idx{SG - 1}"))
                load_chunk((c + 1) % NCH)
                wait(rows_out, 16 * (c + 1))
                wait(experts_out, 16 * (c + 1))
                sp.sem_inc(stores_done, 1)
            wait(chunk_in, 48 * (NCH + 1))

            for h in range(2):
                wait(scattered[h], FILLED + 128 * (NCH * SG // 2))

            def load_idx(it, h):
                sp.dma_start(gidx[:, h, :, :, :], sorted_tiles[:, bass.ds(it * 4 + h * 2, 2), :, :]).then_inc(gidx_in[h], 16)

            for h in range(2):
                load_idx(0, h)
            turns = sp.value_load(gstart[0:1, NB + 1:NB + 2], min_val=1, max_val=TURNS)
            with sp.Fori(0, turns) as it:
                for h in range(2):
                    slot = (it % (RING // 4)) * 4 + 2 * h
                    wait(gathered[h], 128 * (it + 1))
                    wait(ring_freed, it * 4 + 2 * h + 2)
                    sp.dma_start(ring[:, bass.ds(slot, 2), :, :], stage[:, h, :, :, :]).then_inc(ring_out, 16)
                    sp.dma_start(ring_dst[:, bass.ds(slot, 2), :, :], gidx[:, h, :, :, :]).then_inc(ring_out, 16)
                    wait(ring_out, 64 * it + 32 * (h + 1))
                    sp.sem_inc(ring_filled, 2)
                    load_idx(it + 1, h)
            for h in range(2):
                wait(gidx_in[h], 16 * turns + 16)
            sp.wait_ge(result_out, 16 * NCH)


        @block.gpsimd
        def _(pool):
            pool.iota(iota[:, :], pattern=[[1, P]], base=0, channel_multiplier=0,
                      allow_small_or_imprecise_dtypes=True).then_inc(consts, 1)
            pool.iota(iotaf[:, :], pattern=[[1, P]], base=0, channel_multiplier=0,
                      allow_small_or_imprecise_dtypes=True).then_inc(consts, 1)
            pool.memset(onesb[:, :], 1.0).then_inc(consts, 1)
            pool.memset(zero[:, :], 0.0).then_inc(consts, 1)
            pool.memset(zerob[:, :], 0.0).then_inc(consts, 1)
            pool.memset(ones1[:, :], 1.0).then_inc(consts, 1)
            pool.memset(big3[:, :, :], 1.0).then_inc(consts, 1)
            pool.memset(pay[:, :, :], 1.0).then_inc(consts, 1)
            pool.memset(vext[:, :, :, :], 1.0).then_inc(consts, 1)
            fill = big2[:, :, :].rearrange("p a b -> p (a b)").bitcast(U32).rearrange("p (c w) -> p c w", w=2)
            pool.memset(fill[:, :, 0], 0).then_inc(consts, 1)
            pool.memset(fill[:, :, 1].bitcast(F32), -1.0).then_inc(consts, 1)
            pool.wait_ge(consts, 11)
            pool.affine_select(out=before[:, :], in_=onesb[:, :], compare_op=ALU.is_gt, fill=0.0, base=0,
                               pattern=[[1, P]], channel_multiplier=-1).then_inc(consts, 1)
            pool.affine_select(out=notbefore[:, :], in_=onesb[:, :], compare_op=ALU.is_ge, fill=0.0, base=0,
                               pattern=[[-1, P]], channel_multiplier=1).then_inc(consts, 1)
            pool.affine_select(out=ident[:, :], in_=zero[:, :], compare_op=ALU.not_equal, fill=1.0, base=0,
                               pattern=[[-1, P]], channel_multiplier=1).then_inc(consts, 1)
            pool.affine_select(out=headmask[:, :], in_=big3[:, 0, 0:H1], compare_op=ALU.is_ge, fill=0.0, base=0,
                               pattern=[[-HD, H1]], channel_multiplier=1).then_inc(consts, 1)
            pool.affine_select(out=lower[:, :, :], in_=big3[:, 0, 0:E1 * E1].rearrange("p (a b) -> p a b", a=E1),
                               compare_op=ALU.is_gt, fill=0.0, base=0,
                               pattern=[[1, E1], [-1, E1]], channel_multiplier=0).then_inc(consts, 1)
            pool.wait_ge(consts, 16)
            pool.affine_select(out=headmask[:, :], in_=headmask[:, :], compare_op=ALU.is_ge, fill=0.0, base=HD - 1,
                               pattern=[[HD, H1]], channel_multiplier=-1).then_inc(consts, 1)
            fills = sorted_edges.rearrange("(r p c) w -> r p c w", p=P, c=4 * P)
            for r in range(FILLS):
                pool.dma_start(fills[r], fill).then_inc(scattered[r % 2], 16)
            for h in range(2):
                pool.wait_ge(scattered[h], FILLED)

            last = pool.to_reg(CAP - 1)
            with pool.Fori(0, NCH) as c:
                for g in range(SG):
                    pool.wait_ge(V1.sem, V1.at(c, f"idx{g}"))
                    pool.sem_inc(passed, 1)
                    for k in range(ST):
                        pool.indirect_dma_start(
                            out=sorted_edges, out_offset=bass.IndirectOffsetOnAxis(ap=idx[:, g % 2, k:k + 1], axis=0),
                            in_=recs[:, g % 2, k, :], in_offset=None, bounds_check=last, oob_is_err=False,
                        ).then_inc(scattered[g % 2], 16)

            pool.wait_ge(V1.sem, V1.at(NCH - 1, "pay"))
            pool.partition_all_reduce(gmall[:, :], gmx[:, :], P, bass.bass_isa.ReduceOp.max).then_inc(guard_ready, 1)

            turns = pool.value_load(gstart[0:1, NB + 1:NB + 2], min_val=1, max_val=TURNS)
            with pool.Fori(0, turns) as it:
                for h in range(2):
                    pool.wait_ge(gidx_in[h], 16 * (it + 1))
                    pool.sem_inc(passed, 1)
                    for g in range(2):
                        for k in range(GT):
                            pool.indirect_dma_start(
                                out=stage[:, h, g, k, :], out_offset=None, in_=node_rows,
                                in_offset=bass.IndirectOffsetOnAxis(ap=gidx[:, h, g, k, 0:1], axis=0),
                            ).then_inc(gathered[h], 16)

        @block.scalar
        def _(act):
            act.wait_ge(weights_in, 16 * len(wl))
            act.wait_ge(consts, 17)
            act.activation(sm[:, 15:16], zero[:, 0:1], ACT.Copy).then_inc(A1.sem, A1.n)

            def copy(steps, i, name, dst, src, *waits):
                for st, what in waits:
                    act.wait_ge(st.sem, st.at(i, what))
                act.activation(dst, src, ACT.Copy).then_inc(steps.sem, 1)

            with act.Fori(0, NCH) as c:
                copy(A1, c, "xT", xT[:, :], p4[:, :], (T1, "xT"))
                copy(A1, c, "hT", bufA[:, :], p5[:, :], (T1, "hT"))
                act.wait_ge(T1.sem, T1.at(c, "gT"))
                act.activation(bufB[:, :], p4[:, :], ACT.Identity, bias=w["g_a1"][:, 0:1]).then_inc(A1.sem, 1)
                copy(A1, c, "ay", sm[:, 0:Q], p6[:, 0:Q], (T1, "ay"))
                act.wait_ge(V1.sem, V1.at(c, "masked"))
                act.activation(bufC[:, :], bufC[:, :], ACT.Exp).then_inc(A1.sem, 1)
                copy(A1, c, "PT", bufD[:, :], p4[:, :], (T1, "PT"))
                copy(A1, c, "hpT", bufB[:, :], p5[:, :], (T1, "hpT"))
                act.wait_ge(V1.sem, V1.at(c, "zmin"))
                act.activation(bufC[:, :], bufC[:, :], ACT.Exp).then_inc(A1.sem, 1)
                copy(A1, c, "xT1", xT[:, :], p5[:, :], (T1, "xT1"))
                for e in range(E0):
                    for f in range(2):
                        act.wait_ge(T1.sem, T1.at(c, f"up{f}_{e}"))
                        act.activation(hid[:, f, :], pS[:, 4 * f:4 * f + 4, :], ACT.Gelu,
                                       bias=w["f_b1"][:, e, f:f + 1]).then_inc(A1.sem, 1)
                    act.wait_ge(T1.sem, T1.at(c, f"down{e}"))
                    if e == 0:
                        act.wait_ge(stores_done, c + 1)
                    act.activation(yb[:, :, e, :], p7[:, :].rearrange("p (q f) -> p q f", q=Q), ACT.Copy).then_inc(A1.sem, 1)

            act.wait_ge(stores_done, NCH + 1)
            act.wait_ge(chunk_in, 48 * (NCH + 1))
            act.activation(sm[:, 15:16], zero[:, 0:1], ACT.Copy).then_inc(A2.sem, A2.n)
            act.wait_ge(tables_ready, 1)
            act.activation(dn[:, :, :], dn[:, :, :], ACT.Exp).then_inc(guard_ready, 1)
            act.activation(sm[:, 14:15], zero[:, 0:1], ACT.Copy).then_inc(AG.sem, AG.n)

            def load_y(c):
                act.dma_start(yb[:, :, :, :], expert_rows.rearrange("(b n) e f -> n b e f", n=P)[:, bass.ds(c * Q, Q), :, :]).then_inc(y_in, 16)

            def load_adj(c):
                act.dma_start(adjc[:, :, :], a["adj"].rearrange("b i j -> i b j")[:, bass.ds(c * Q, Q), :]).then_inc(adj_in, 16)

            load_y(0)
            load_adj(0)
            with act.Fori(0, NCH) as c:
                for q in qs:
                    g0 = act.value_load(gstart[0:1, bass.ds(c * Q + q, 1)], min_val=0, max_val=CAP // GE)
                    g1 = act.value_load(gstart[0:1, bass.ds(c * Q + q + 1, 1)], min_val=1, max_val=CAP // GE)
                    with act.Fori(g0, g1) as g:
                        act.wait_ge(TG.sem, TG.at(g, "onehotT"))
                        act.activation(OT[:, :, :], p4[:, :].rearrange("p (k e) -> p k e", k=GT), ACT.Copy).then_inc(AG.sem, 1)
                        act.wait_ge(VG.sem, VG.at(g, "z"))
                        act.activation(eg[:, :, :], zg[:, :, :], ACT.Exp).then_inc(AG.sem, 1)
                act.wait_ge(V2.sem, V2.at(c, "gexp0"))
                act.activation(small2[:, 0:Q * E0], small[:, 0:Q * E0], ACT.Exp).then_inc(A2.sem, 1)
                act.wait_ge(V2.sem, V2.at(c, "x2"))
                load_y((c + 1) % NCH)
                copy(A2, c, "xT", xT[:, :], p4[:, :], (T2, "xT"))
                act.wait_ge(V2.sem, V2.at(c, "mask"))
                load_adj((c + 1) % NCH)
                act.wait_ge(T2.sem, T2.at(c, "qT"))
                act.activation(bufA[:, :], p5[:, :], ACT.Identity, bias=w["a_bqk"][:, 0:1]).then_inc(A2.sem, 1)
                act.wait_ge(T2.sem, T2.at(c, "kT"))
                act.activation(bufB[:, :], p4[:, :], ACT.Identity, bias=w["a_bqk"][:, 1:2]).then_inc(A2.sem, 1)
                act.wait_ge(T2.sem, T2.at(c, "v"))
                act.activation(vext[:, :, :, 0:HD].rearrange("p q h d -> p (q h) d"),
                               p5[:, :].rearrange("p (q d) -> p q d", d=HD), ACT.Copy).then_inc(A2.sem, 1)
                for q in qs:
                    act.wait_ge(V2.sem, V2.at(c, f"max{q}"))
                    act.activation(big2[:, :, :], big2[:, :, :], ACT.Exp, scale=HD ** -0.5).then_inc(A2.sem, 1)
                    act.wait_ge(T2.sem, T2.at(c, f"PT{q}"))
                    act.activation(big3[:, :, :], pS[:, :, :], ACT.Copy).then_inc(A2.sem, 1)
                copy(A2, c, "ctxT", bufA[:, :], p4[:, :], (T2, "ctxT"))
                copy(A2, c, "y1T", xT[:, :], p4[:, :], (T2, "y1T"))
                for f in range(FC):
                    act.wait_ge(T2.sem, T2.at(c, f"ffup{f}"))
                    act.activation(hid1[:, f, :], pR[:, 4 * (f % 2):4 * (f % 2) + 4, :], ACT.Relu,
                                   bias=w["a_c1"][:, f:f + 1]).then_inc(A2.sem, 1)
                copy(A2, c, "xT3", xT[:, :], p4[:, :], (T2, "xT3"))
                act.wait_ge(V2.sem, V2.at(c, "gexp"))
                act.activation(gates[:, :, :], gates[:, :, :], ACT.Exp).then_inc(A2.sem, 1)
                for e in range(E1 + 1):
                    for f in range(FC):
                        act.wait_ge(T2.sem, T2.at(c, f"up{f}_{e}"))
                        act.activation(hid1[:, f, :], pR[:, 4 * (f % 2):4 * (f % 2) + 4, :], ACT.Gelu,
                                       bias=w["m_b1"][:, e, f:f + 1]).then_inc(A2.sem, 1)
                act.wait_ge(V2.sem, V2.at(c, f"mix{E1}"))
                act.dma_start(a["out"].rearrange("b n f -> n b f")[:, bass.ds(c * Q, Q), :],
                              X[:, bass.ds(c * Q, Q), :]).then_inc(result_out, 16)
            act.wait_ge(y_in, 16 * (NCH + 1))
            act.wait_ge(adj_in, 16 * (NCH + 1))

        @block.tensor
        def _(pe):
            pe.wait_ge(weights_in, 16 * len(wl))
            pe.wait_ge(consts, 17)
            for h in range(2):
                m = pe.matmul(pS[:, 4 * h:4 * h + 4, :], onesb[:, :], zerob[:, :], start=True, stop=False, skip_group_check=True)
            m.then_inc(counted, 2)
            with pe.Fori(0, NCH * SG // 2) as i:
                for o in range(2):
                    pe.wait_ge(counted_onehot, 2 * i + o + 1)
                    for h in range(2):
                        m = pe.matmul(pS[:, 4 * h:4 * h + 4, 0:NB], onesb[:, :], O[:, o, 4 * h:4 * h + 4, 0:NB],
                                      start=False, stop=False, skip_group_check=True)
                    m.then_inc(counted, 1)
            pe.wait_ge(bases_ready, 1)
            for h in range(2):
                m = pe.matmul(pR[:, 4 * h:4 * h + 4, 0:NB], ident[:, :], big1[:, 4 * h:4 * h + 4, 0:NB],
                              start=True, stop=False, skip_group_check=True)
            m.then_inc(T1.sem, T1.n)

            def scatter_step(c, g):
                pe.wait_ge(V1.sem, V1.at(c, f"onehot{g}"))
                for h in range(2):
                    m = pe.matmul(pR[:, 4 * h:4 * h + 4, 0:NB], before[:, :], O[:, g % 2, 4 * h:4 * h + 4, 0:NB],
                                  start=False, stop=False, skip_group_check=True)
                m.then_inc(T1.sem, 1)
                pe.wait_ge(V1.sem, V1.at(c, f"prod{g}"))
                for h in range(2):
                    m = pe.matmul(pR[:, 4 * h:4 * h + 4, 0:NB], notbefore[:, :], O[:, g % 2, 4 * h:4 * h + 4, 0:NB],
                                  start=False, stop=False, skip_group_check=True)
                m.then_inc(T1.sem, 1)

            def turn(dst, src, inc, who=ident):
                for q in qs:
                    m = pe.transpose(dst[:, q * P:(q + 1) * P], src[:, q * P:(q + 1) * P], ident[:, :])
                m.then_inc(inc.sem, 1)

            def flat(t):
                return t[:, :, :].rearrange("p q f -> p (q f)")

            def rows_bias(dst, q, bias, start=False):
                return pe.matmul(dst[:, q * P:(q + 1) * P], ones1[:, :], bias, start=start, stop=True)

            def slices(c):
                def s_xT():
                    pe.wait_ge(V1.sem, V1.at(c, "xn"))
                    turn(p4, flat(xn), T1)

                def s_hT():
                    pe.wait_ge(A1.sem, A1.at(c, "xT"))
                    pe.matmul(p5[:, :], w["g_W"][:, :], xT[:, :], start=True, stop=True).then_inc(T1.sem, 1)

                def s_gT():
                    pe.wait_ge(A1.sem, A1.at(c, "hT"))
                    pe.matmul(p4[:, :], w["g_a12"][:, :], bufA[:, :], start=True, stop=True).then_inc(T1.sem, 1)
                    for q in qs:
                        m = pe.matmul(p6[:, q:q + 1], bufA[:, q * P:(q + 1) * P], w["g_a2"][:, :], start=True, stop=True)
                    m.then_inc(T1.sem, 1)

                def s_logits():
                    pe.wait_ge(A1.sem, A1.at(c, "gT"))
                    for q in qs:
                        m = pe.matmul(p5[:, q * P:(q + 1) * P], bufB[:, q * P:(q + 1) * P], bufA[:, q * P:(q + 1) * P],
                                      start=True, stop=True)
                    m.then_inc(T1.sem, 1)

                def s_PT():
                    pe.wait_ge(V1.sem, V1.at(c, "prob"))
                    turn(p4, bufC, T1)
                    pe.wait_ge(A1.sem, A1.at(c, "PT"))
                    for q in qs:
                        m = pe.matmul(p5[:, q * P:(q + 1) * P], xn[:, q, :], bufD[:, q * P:(q + 1) * P], start=True, stop=True)
                    m.then_inc(T1.sem, 1)

                def s_hout():
                    pe.wait_ge(A1.sem, A1.at(c, "hpT"))
                    for q in qs:
                        pe.matmul(p4[:, q * P:(q + 1) * P], xT[:, q * P:(q + 1) * P], w["g_W1"][:, :], start=True, stop=False)
                        m = pe.matmul(p4[:, q * P:(q + 1) * P], bufB[:, q * P:(q + 1) * P], w["g_W2"][:, :], start=False, stop=True)
                    m.then_inc(T1.sem, 1)

                def s_hrow():
                    pe.wait_ge(V1.sem, V1.at(c, "xn1"))
                    turn(p5, flat(xn), T1)
                    pe.wait_ge(A1.sem, A1.at(c, "xT1"))
                    for q in qs:
                        m = pe.matmul(p6[:, q * 16:(q + 1) * 16], xT[:, q * P:(q + 1) * P], w["f_Wgat"][:, :], start=True, stop=True)
                    m.then_inc(T1.sem, 1)

                def s_expert(e):
                    for f in range(2):
                        if e > 0:
                            pe.wait_ge(A1.sem, A1.at(c, f"gelu{f}_{e - 1}"))
                        pe.matmul(pS[:, 4 * f:4 * f + 4, :], w["f_W1"][:, e, f, :], xT[:, :], start=True, stop=True).then_inc(T1.sem, 1)
                    for f in range(2):
                        pe.wait_ge(A1.sem, A1.at(c, f"gelu{f}_{e}"))
                    if e > 0:
                        pe.wait_ge(A1.sem, A1.at(c, f"y{e - 1}"))
                    for q in qs:
                        for f in range(2):
                            pe.matmul(p7[:, q * P:(q + 1) * P], hid[:, f, q * P:(q + 1) * P], w["f_W2"][:, e, f, :],
                                      start=(f == 0), stop=False)
                        m = rows_bias(p7, q, w["f_b2"][0:1, e * P:(e + 1) * P])
                    m.then_inc(T1.sem, 1)

                return [lambda: None, s_xT, s_hT, s_gT, s_logits, lambda: None, s_PT, s_hout, lambda: None, s_hrow] \
                    + [lambda e=e: s_expert(e) for e in range(E0)]

            with pe.Fori(0, NCH) as c:
                work = slices(c)
                for g in range(SG):
                    scatter_step(c, g)
                    if g < len(work):
                        work[g]()
            pe.wait_ge(A1.sem, A1.at(NCH - 1, f"y{E0 - 1}"))
            m = pe.matmul(p7[:, 0:P], ident[:, :], ident[:, :], start=True, stop=True)
            m.then_inc(T2.sem, T2.n)
            m = pe.matmul(p7[:, 0:P], ident[:, :], ident[:, :], start=True, stop=True)
            m.then_inc(TG.sem, TG.n)
            with pe.Fori(0, NCH) as c:
                for q in qs:
                    if q == 0:
                        pe.wait_ge(V2.sem, V2.at(c, "self"))
                    m = pe.matmul(p6[:, q * 20:(q + 1) * 20], ident[:, :], selfc[:, q, :], start=True, stop=False, skip_group_check=True)
                    if q == 0:
                        m.then_inc(T2.sem, 1)
                    g0 = pe.value_load(gstart[0:1, bass.ds(c * Q + q, 1)], min_val=0, max_val=CAP // GE)
                    g1 = pe.value_load(gstart[0:1, bass.ds(c * Q + q + 1, 1)], min_val=1, max_val=CAP // GE)
                    with pe.Fori(g0, g1) as g:
                        pe.wait_ge(VG.sem, VG.at(g, "onehot"))
                        for k in range(GT):
                            m = pe.transpose(p4[:, k * P:(k + 1) * P], Og[:, k, :], ident[:, :])
                        m.then_inc(TG.sem, 1)
                        pe.wait_ge(AG.sem, AG.at(g, "onehotT"))
                        for k in range(GT):
                            m = pe.matmul(p5[:, k * 8:(k + 1) * 8], OT[:, k, :], dmc[:, q, :], start=True, stop=True)
                        m.then_inc(TG.sem, 1)
                        pe.wait_ge(ring_freed, g + RING + 1)
                        for k in range(GT):
                            m = pe.matmul(p6[:, q * 20:(q + 1) * 20], Og[:, k, :], Vg[:, k, :], start=False, stop=False,
                                          skip_group_check=True)
                        m.then_inc(TG.sem, 1)
                pe.wait_ge(V2.sem, V2.at(c, "xn"))
                turn(p4, flat(xn), T2)
                pe.wait_ge(A2.sem, A2.at(c, "xT"))
                pe.matmul(p5[:, :], w["a_Wqkv"][:, 0:P], xT[:, :], start=True, stop=True).then_inc(T2.sem, 1)
                pe.matmul(p4[:, :], w["a_Wqkv"][:, P:2 * P], xT[:, :], start=True, stop=True).then_inc(T2.sem, 1)
                pe.wait_ge(A2.sem, A2.at(c, "qT"))
                for q in qs:
                    pe.matmul(p5[:, q * P:(q + 1) * P], xT[:, q * P:(q + 1) * P], w["a_Wqkv"][:, 2 * P:3 * P], start=True, stop=False)
                    m = rows_bias(p5, q, w["a_bv"][:, :])
                m.then_inc(T2.sem, 1)
                pe.wait_ge(V2.sem, V2.at(c, "mask"))
                turn(p6, bufC, T2)
                for q in qs:
                    pe.wait_ge(V2.sem, V2.at(c, f"keys{q}"))
                    for h in range(2):
                        m = pe.matmul(pS[:, 4 * h:4 * h + 4, :], bufA[:, q * P:(q + 1) * P], big1[:, 4 * h:4 * h + 4, :],
                                      start=True, stop=True)
                    m.then_inc(T2.sem, 1)
                    pe.wait_ge(A2.sem, A2.at(c, f"exp{q}"))
                    for h in range(H1):
                        m = pe.transpose(pS[:, h, :], big2[:, h, :], ident[:, :])
                    m.then_inc(T2.sem, 1)
                    pe.wait_ge(A2.sem, A2.at(c, f"PT{q}"))
                    if q > 0:
                        pe.wait_ge(V2.sem, V2.at(c, f"ctx{q - 1}"))
                    for h in range(H1):
                        m = pe.matmul(p5[:, h * 17:(h + 1) * 17], big3[:, h, :], vext[:, q, h, :], start=True, stop=True)
                    m.then_inc(T2.sem, 1)
                pe.wait_ge(V2.sem, V2.at(c, f"ctx{Q - 1}"))
                turn(p4, bufC, T2)
                pe.wait_ge(A2.sem, A2.at(c, "ctxT"))
                for q in qs:
                    pe.matmul(p5[:, q * P:(q + 1) * P], bufA[:, q * P:(q + 1) * P], w["a_Wo"][:, :], start=True, stop=False)
                    m = rows_bias(p5, q, w["a_bo"][:, :])
                m.then_inc(T2.sem, 1)
                pe.wait_ge(V2.sem, V2.at(c, "y1"))
                turn(p4, bufD, T2)
                pe.wait_ge(A2.sem, A2.at(c, "y1T"))
                for f in range(FC):
                    if f >= 2:
                        pe.wait_ge(A2.sem, A2.at(c, f"relu{f - 2}"))
                    pe.matmul(pR[:, 4 * (f % 2):4 * (f % 2) + 4, :], w["a_W1"][:, f, :], xT[:, :], start=True, stop=True).then_inc(T2.sem, 1)
                pe.wait_ge(A2.sem, A2.at(c, f"relu{FC - 1}"))
                for q in qs:
                    for f in range(FC):
                        pe.matmul(p5[:, q * P:(q + 1) * P], hid1[:, f, q * P:(q + 1) * P], w["a_W2"][:, f, :], start=(f == 0), stop=False)
                    m = rows_bias(p5, q, w["a_c2"][:, :])
                m.then_inc(T2.sem, 1)
                pe.wait_ge(V2.sem, V2.at(c, "xn3"))
                turn(p4, flat(xn), T2)
                pe.wait_ge(A2.sem, A2.at(c, "xT3"))
                for q in qs:
                    m = pe.matmul(p5[:, q * E1:(q + 1) * E1], xT[:, q * P:(q + 1) * P], w["m_Wr"][:, :], start=True, stop=True)
                m.then_inc(T2.sem, 1)
                for e in range(E1 + 1):
                    for f in range(FC):
                        if f >= 2:
                            pe.wait_ge(A2.sem, A2.at(c, f"gelu{f - 2}_{e}"))
                        elif e > 0:
                            pe.wait_ge(A2.sem, A2.at(c, f"gelu{f + 2}_{e - 1}"))
                        pe.matmul(pR[:, 4 * (f % 2):4 * (f % 2) + 4, :], w["m_W1"][:, e, f, :], xT[:, :], start=True, stop=True).then_inc(T2.sem, 1)
                    pe.wait_ge(A2.sem, A2.at(c, f"gelu{FC - 1}_{e}"))
                    if e > 0:
                        pe.wait_ge(V2.sem, V2.at(c, f"mix{e - 1}"))
                    for q in qs:
                        for f in range(FC):
                            pe.matmul(p7[:, q * P:(q + 1) * P], hid1[:, f, q * P:(q + 1) * P], w["m_W2"][:, e, f, :],
                                      start=(f == 0), stop=False)
                        m = rows_bias(p7, q, w["m_b2"][0:1, e * P:(e + 1) * P])
                    m.then_inc(T2.sem, 1)

        @block.vector
        def _(vec):
            def cols(t):
                return t[:, :].rearrange("p (q f) -> p q f", q=Q)

            setup, c1, c2, cg, cm = (Chain(x, per) for x, per in ((setup_chain, 0), (chain1, CH1), (chain2, CH2), (chaing, 2), (chainm, 0)))
            vec.wait_ge(consts, 17)

            def do(chain, ins, bare=False):
                chain.count(ins)
                chain.wait(vec)
                if bare:
                    vec.sem_inc(passed, 1)

            def sig(steps, i, name, ins, bare=False):
                ins.then_inc(steps.sem, 1)
                vec.wait_ge(steps.sem, steps.at(i, name))
                if bare:
                    vec.sem_inc(passed, 1)

            NT = NE // P
            xi = X[:, :, :].bitcast(I32).rearrange("p b f -> p (b f)")
            xf = X[:, :, :].rearrange("p b f -> p (b f)")
            vec.wait_ge(edges_in, 16)
            do(setup, vec.tensor_single_scalar(xi[:, NT:2 * NT], xi[:, 0:NT], 7, op=ALU.arith_shift_right))
            do(setup, vec.tensor_copy(xf[:, 2 * NT:3 * NT], xi[:, NT:2 * NT]))
            with vec.Fori(0, NCH * SG // 2) as i:
                for o in range(2):
                    vec.wait_ge(counted, 2 * i + o + 1)
                    for k in range(ST):
                        m = vec.tensor_scalar(O[:, o, k, 0:NB], iota[:, 0:NB], xf[:, bass.ds(2 * NT + (2 * i + o) * ST + k, 1)],
                                              None, op0=ALU.is_equal)
                    m.then_inc(counted_onehot, 1)
            vec.wait_ge(counted, 2 + NCH * SG)
            cnt = yb[:, :, :, :].rearrange("p q e f -> p (q e) f")[:, 0:ST, 0:NB]
            do(setup, vec.tensor_copy(cnt, pS[:, :, 0:NB]))
            do(setup, vec.tensor_reduce(tot[:, :], cnt.rearrange("p k b -> p b k"), AX, ALU.add))
            do(setup, vec.tensor_scalar(toti[:, 0:NB], tot[:, :], float(GE - 1), None, op0=ALU.add))
            do(setup, vec.tensor_single_scalar(toti[:, 0:NB], toti[:, 0:NB], GE.bit_length() - 1, op=ALU.arith_shift_right))
            do(setup, vec.tensor_copy(tot[:, :], toti[:, 0:NB]))
            do(setup, vec.tensor_scalar(tot[:, :], tot[:, :], 1.0, None, op0=ALU.max))
            do(setup, vec.memset(starts[:, 0:1], 0.0))
            do(setup, vec.tensor_tensor_scan(starts[:, 1:NB + 1], tot[:, :], zero[:, 0:NB], 0.0, ALU.add, ALU.add))
            do(setup, vec.tensor_copy(gstart[0:1, 0:NB + 1], starts[0:1, :]))
            do(setup, vec.tensor_scalar(toti[0:1, 0:1], starts[0:1, NB:NB + 1], 3.0, None, op0=ALU.add))
            do(setup, vec.tensor_single_scalar(gstart[0:1, NB + 1:NB + 2], toti[0:1, 0:1], 2, op=ALU.arith_shift_right))
            do(setup, vec.tensor_scalar(big1[:, 0, 0:NB], starts[:, 0:NB], float(GE), None, op0=ALU.mult))
            for k in range(1, ST):
                do(setup, vec.tensor_tensor(big1[:, k, 0:NB], big1[:, k - 1, 0:NB], cnt[:, k - 1, :], ALU.add))
            do(setup, vec.memset(gmx[:, :], -3e38))
            vec.memset(sm[:, 12:13], 0.0).then_inc(V1.sem, V1.n)
            vec.memset(sm[:, 13:14], 0.0).then_inc(bases_ready, 1)

            def inv_sqrt(chain, var, n=Q):
                v, y, t = nb_[:, 0:n, 0], nb_[:, 0:n, 1], nb_[:, 0:n, 2]
                do(chain, vec.tensor_scalar(v, var, EPS, None, op0=ALU.add))
                do(chain, vec.tensor_single_scalar(nbi[:, 0:n], nb_[:, 0:n, 0].bitcast(I32), 1, op=ALU.arith_shift_right))
                do(chain, vec.tensor_scalar(y.bitcast(I32), nbi[:, 0:n], -1.0, float(0x5F3759DF), op0=ALU.mult, op1=ALU.add))
                for r in range(4):
                    do(chain, vec.tensor_tensor(t, y, y, ALU.mult))
                    do(chain, vec.scalar_tensor_tensor(t, t, -0.5, v, ALU.mult, ALU.mult))
                    do(chain, vec.scalar_tensor_tensor(y if r < 3 else rstd[:, 0:n], t, 1.5, y, ALU.add, ALU.mult))

            def norm(chain, src, dst, last=None):
                for q in qs:
                    chain.count(vec.bn_stats(bst[:, q, :], src(q)))
                chain.wait(vec)
                vec.sem_inc(passed, 1)
                for q in qs:
                    chain.count(vec.bn_aggr(mv[:, q, :], bst[:, q, :]))
                chain.wait(vec)
                inv_sqrt(chain, mv[:, :, 1])
                for q in qs:
                    m = vec.tensor_scalar(dst(q), src(q), mv[:, q, 0:1], rstd[:, q:q + 1], op0=ALU.subtract, op1=ALU.mult)
                    if q < Q - 1:
                        chain.count(m)
                    elif last is None:
                        do(chain, m)
                    else:
                        sig(*last, m)

            def over(t, n):
                return t.unsqueeze(2)

            def stage1(c):
                xq = lambda q: X[:, bass.ds(c * Q + q, 1), :].rearrange("p o f -> p (o f)")
                xc = X[:, bass.ds(c * Q, Q), :]

                def w_xn():
                    vec.sem_inc(passed, 1)
                    norm(c1, xq, lambda q: xn[:, q, :], (V1, c, "xn"))

                def w_masked():
                    vec.wait_ge(T1.sem, T1.at(c, "logits"))
                    vec.wait_ge(A1.sem, A1.at(c, "ay"))
                    do(c1, vec.tensor_tensor(cols(bufC), cols(p5), sm[:, 0:Q].unsqueeze(2).broadcast_to([P, Q, P]), ALU.add))
                    do(c1, vec.scalar_tensor_tensor(bufC[:, :], bufC[:, :], 0.2, bufC[:, :], ALU.mult, ALU.max))
                    do(c1, vec.tensor_scalar(cols(bufD), adjc[:, :, :], 0.0, None, op0=ALU.is_gt))
                    do(c1, vec.tensor_tensor(bufC[:, :], bufC[:, :], bufD[:, :], ALU.mult))
                    do(c1, vec.tensor_scalar(bufD[:, :], bufD[:, :], NEG, -NEG, op0=ALU.mult, op1=ALU.add))
                    do(c1, vec.tensor_tensor(bufC[:, :], bufC[:, :], bufD[:, :], ALU.add))
                    do(c1, vec.tensor_reduce(sm[:, 4:8], cols(bufC), AX, ALU.max))
                    sig(V1, c, "masked", vec.tensor_tensor(cols(bufC), cols(bufC), sm[:, 4:8].unsqueeze(2).broadcast_to([P, Q, P]), ALU.subtract))

                def w_prob():
                    vec.wait_ge(A1.sem, A1.at(c, "exp"))
                    do(c1, vec.tensor_reduce(sm[:, 4:8], cols(bufC), AX, ALU.add))
                    do(c1, vec.reciprocal(sm[:, 8:12], sm[:, 4:8]))
                    sig(V1, c, "prob", vec.tensor_tensor(cols(bufC), cols(bufC), sm[:, 8:12].unsqueeze(2).broadcast_to([P, Q, P]), ALU.mult))

                def w_x1():
                    vec.wait_ge(T1.sem, T1.at(c, "hout"))
                    sig(V1, c, "zmin", vec.tensor_scalar(bufC[:, :], p4[:, :], 0.0, None, op0=ALU.min))
                    vec.wait_ge(A1.sem, A1.at(c, "elu"))
                    do(c1, vec.scalar_tensor_tensor(bufC[:, :], p4[:, :], 0.0, bufC[:, :], ALU.max, ALU.add))
                    sig(V1, c, "x1", vec.scalar_tensor_tensor(xc, cols(bufC), -1.0, xc, ALU.add, ALU.add))

                def w_xn1():
                    vec.sem_inc(passed, 1)
                    norm(c1, xq, lambda q: xn[:, q, :], (V1, c, "xn1"))

                def w_pay():
                    vec.wait_ge(T1.sem, T1.at(c, "hrow"))
                    pc = pay[:, bass.ds(c * Q, Q), :]
                    h = p6[:, 0:Q * 16].rearrange("p (q h) -> p q h", q=Q)
                    h4 = p6[:, 0:Q * 16].rearrange("p (q h e) -> p q h e", q=Q, h=H0)
                    s3 = small[:, :].rearrange("p (q h) -> p q h", q=Q)
                    s4 = small[:, :].rearrange("p (q h e) -> p q h e", q=Q, h=H0)
                    do(c1, vec.tensor_copy(pc[:, :, H0:PW].rearrange("p q (h f) -> p q h f", h=H0)[:, :, :, 1:1 + E0], h4))
                    do(c1, vec.tensor_tensor(s3, h, w["f_asrc"][:, :].unsqueeze(1).broadcast_to([P, Q, H0 * E0]), ALU.mult), bare=True)
                    do(c1, vec.tensor_reduce(pc[:, :, 0:H0], s4, AX, ALU.add))
                    do(c1, vec.tensor_tensor(s3, h, w["f_adst"][:, :].unsqueeze(1).broadcast_to([P, Q, H0 * E0]), ALU.mult), bare=True)
                    do(c1, vec.tensor_reduce(dn[:, bass.ds(c * Q, Q), :], s4, AX, ALU.add), bare=True)
                    do(c1, vec.tensor_reduce(sm[:, 4:8], pc[:, :, 0:H0].rearrange("p q h -> p h q"), AX, ALU.max))
                    sig(V1, c, "pay", vec.tensor_tensor(gmx[:, :], gmx[:, :], sm[:, 4:8], ALU.max))

                return {0: w_xn, 4: w_masked, 5: w_prob, 7: w_x1, 8: w_xn1, 9: w_pay}

            vec.wait_ge(x_in, 16)
            with vec.Fori(0, NCH) as c:
                c1.turn(c)
                vec.wait_ge(chunk_in, 48 * (c + 1))
                do(c1, vec.tensor_single_scalar(tmpi[:, :], dstc[:, :], 7, op=ALU.arith_shift_right))
                do(c1, vec.tensor_copy(dhi[:, :], tmpi[:, :]))
                do(c1, vec.tensor_single_scalar(tmpi[:, :], dstc[:, :], P - 1, op=ALU.bitwise_and))
                do(c1, vec.tensor_copy(rec[:, :, 1].bitcast(F32), tmpi[:, :]))
                do(c1, vec.tensor_scalar(rec[:, :, 0], srcc[:, :], float(M - 1), None, op0=ALU.min))
                do(c1, vec.tensor_scalar(far[:, :], dhi[:, :], NB - 0.5, SKIP, op0=ALU.is_gt, op1=ALU.mult))
                work = stage1(c)
                for g in range(SG):
                    prev = T1.at(c, f"ranked{g - 2}") if g >= 2 else T1.at(c - 1, f"ranked{SG - 2 + g}")
                    vec.wait_ge(T1.sem, prev)
                    for k in range(ST):
                        m = vec.tensor_scalar(O[:, g % 2, k, 0:NB], iota[:, 0:NB], dhi[:, g * ST + k:g * ST + k + 1], None, op0=ALU.is_equal)
                    sig(V1, c, f"onehot{g}", m)
                    vec.wait_ge(T1.sem, T1.at(c, f"rank{g}"))
                    sig(V1, c, f"prod{g}", vec.tensor_tensor(big1[:, :, 0:NB], pR[:, :, 0:NB], O[:, g % 2, :, 0:NB], ALU.mult))
                    do(c1, vec.tensor_reduce(pos[:, :], big1[:, :, 0:NB], AX, ALU.add))
                    vec.wait_ge(scattered[g % 2], FILLED + 128 * (c * (SG // 2) + g // 2))
                    do(c1, vec.tensor_tensor(idx[:, g % 2, :], pos[:, :], far[:, g * ST:(g + 1) * ST], ALU.add))
                    sig(V1, c, f"idx{g}", vec.tensor_copy(recs[:, g % 2, :, :], rec[:, g * ST:(g + 1) * ST, :]))
                    if g in work:
                        work[g]()
                c1.end()

            vec.wait_ge(guard_ready, 1)
            do(cm, vec.tensor_copy(dm[:, :, 0:H0], dn[:, :, :]))
            guard = dm[:, :, H0:2 * H0]
            do(cm, vec.tensor_tensor(guard, dn[:, :, :], gmall[:, :].unsqueeze(1).broadcast_to([P, NB, H0]), ALU.add))
            do(cm, vec.scalar_tensor_tensor(guard, guard, 0.2, guard, ALU.mult, ALU.max))
            do(cm, vec.tensor_scalar(guard, guard, -1.0, None, op0=ALU.mult))
            do(cm, vec.tensor_tensor(dn[:, :, :], dn[:, :, :], pay[:, :, 0:H0], ALU.add))
            do(cm, vec.scalar_tensor_tensor(dn[:, :, :], dn[:, :, :], 0.2, dn[:, :, :], ALU.mult, ALU.max))
            vec.tensor_tensor(dn[:, :, :], dn[:, :, :], dm[:, :, H0:2 * H0], ALU.add).then_inc(tables_ready, 1)
            vec.wait_ge(guard_ready, 2)
            weighted = pay[:, :, H0:PW].rearrange("p b (h f) -> p b h f", h=H0)
            do(cm, vec.tensor_tensor(weighted, weighted, dn[:, :, :].unsqueeze(3).broadcast_to([P, NB, H0, 1 + E0]), ALU.mult))
            vec.memset(sm[:, 12:13], 0.0).then_inc(V2.sem, V2.n)
            vec.memset(sm[:, 13:14], 0.0).then_inc(VG.sem, VG.n)
            vec.memset(small2[:, 0:1], 0.0).then_inc(ring_freed, RING)

            def top2(v, n, sel):
                a, b = cmp1[:, :, 0:n, 0:n], cmp2[:, :, 0:n, 0:n]
                other, own = v.unsqueeze(2).broadcast_to([P, Q, n, n]), v.unsqueeze(3).broadcast_to([P, Q, n, n])
                do(c2, vec.tensor_tensor(a, other, own, ALU.is_gt))
                do(c2, vec.tensor_tensor(b, other, own, ALU.is_equal))
                do(c2, vec.tensor_tensor(b, b, lower[:, 0:n, 0:n].unsqueeze(1).broadcast_to([P, Q, n, n]), ALU.mult))
                do(c2, vec.tensor_tensor(a, a, b, ALU.add))
                do(c2, vec.tensor_reduce(sel, a, AX, ALU.add))
                do(c2, vec.tensor_scalar(sel, sel, 1.5, None, op0=ALU.is_lt))

            def per_q(t):
                return t.unsqueeze(2)

            with vec.Fori(0, NCH) as c:
                c2.turn(c)
                xq = lambda q: X[:, bass.ds(c * Q + q, 1), :].rearrange("p o f -> p (o f)")
                xc = X[:, bass.ds(c * Q, Q), :]
                do(c2, vec.tensor_copy(dmc[:, :, :], dm[:, bass.ds(c * Q, Q), :]))
                sig(V2, c, "self", vec.tensor_copy(selfc[:, :, :], pay[:, bass.ds(c * Q, Q), H0:PW]))
                for q in qs:
                    g0 = vec.value_load(gstart[0:1, bass.ds(c * Q + q, 1)], min_val=0, max_val=CAP // GE)
                    g1 = vec.value_load(gstart[0:1, bass.ds(c * Q + q + 1, 1)], min_val=1, max_val=CAP // GE)
                    with vec.Fori(g0, g1) as g:
                        cg.turn(g)
                        slot = g % RING
                        rows = ring[:, bass.ds(slot, 1), :, :].rearrange("p o k f -> p (o k) f")
                        dst = ring_dst[:, bass.ds(slot, 1), :, :].rearrange("p o k w -> p (o k) w").bitcast(F32)[:, :, 1:2]
                        vec.wait_ge(ring_filled, g + 1)
                        vec.wait_ge(TG.sem, TG.at(g - 1, "sums"))
                        sig(VG, g, "onehot", vec.tensor_tensor(Og[:, :, :], iotaf[:, :].unsqueeze(1).broadcast_to([P, GT, P]),
                                                               dst.broadcast_to([P, GT, P]), ALU.is_equal))
                        vec.wait_ge(TG.sem, TG.at(g, "dstscore"))
                        d8 = p5[:, 0:GT * 8].rearrange("p (k f) -> p k f", k=GT)
                        do(cg, vec.tensor_tensor(zg[:, :, :], rows[:, :, 0:H0], d8[:, :, 0:H0], ALU.add))
                        do(cg, vec.scalar_tensor_tensor(zg[:, :, :], zg[:, :, :], 0.2, zg[:, :, :], ALU.mult, ALU.max))
                        sig(VG, g, "z", vec.tensor_tensor(zg[:, :, :], zg[:, :, :], d8[:, :, H0:2 * H0], ALU.add))
                        vec.wait_ge(AG.sem, AG.at(g, "exp"))
                        vec.tensor_tensor(Vg[:, :, :].rearrange("p k (h f) -> p k h f", h=H0),
                                          rows[:, :, H0:PW].rearrange("p k (h f) -> p k h f", h=H0),
                                          eg[:, :, :].unsqueeze(3).broadcast_to([P, GT, H0, 1 + E0]), ALU.mult).then_inc(ring_freed, 1)
                        cg.end()
                vec.wait_ge(TG.sem, TG.at(g1 - 1, "sums"))
                sig(V2, c, "agg", vec.tensor_copy(agg[:, :, :], p6[:, 0:Q * 20].rearrange("p (q f) -> p q f", q=Q)))
                a5 = agg[:, :, :].rearrange("p q (h f) -> p q h f", h=H0)
                s3 = small[:, :].rearrange("p (q h) -> p q h", q=Q)
                t3 = small2[:, :].rearrange("p (q h) -> p q h", q=Q)
                s4 = small[:, :].rearrange("p (q h e) -> p q h e", q=Q, h=H0)
                den = sm[:, 0:16].rearrange("p (q h) -> p q h", q=Q)
                do(c2, vec.tensor_scalar(den, a5[:, :, :, 0], 1e-16, None, op0=ALU.add))
                do(c2, vec.reciprocal(den, den))
                do(c2, vec.tensor_tensor(s4, a5[:, :, :, 1:1 + E0], den.unsqueeze(3).broadcast_to([P, Q, H0, E0]), ALU.mult))
                do(c2, vec.tensor_tensor(s3, s3, w["f_bgat"][:, :].unsqueeze(1).broadcast_to([P, Q, 16]), ALU.add))
                do(c2, vec.tensor_reduce(sm[:, 0:Q], s3, AX, ALU.add))
                do(c2, vec.tensor_scalar(sm[:, 0:Q], sm[:, 0:Q], 1.0 / 16, None, op0=ALU.mult))
                do(c2, vec.tensor_tensor(s3, s3, sm[:, 0:Q].unsqueeze(2).broadcast_to([P, Q, 16]), ALU.subtract))
                do(c2, vec.tensor_tensor(t3, s3, s3, ALU.mult))
                do(c2, vec.tensor_reduce(sm[:, 0:Q], t3, AX, ALU.add))
                do(c2, vec.tensor_scalar(sm[:, 0:Q], sm[:, 0:Q], 1.0 / 16, None, op0=ALU.mult))
                inv_sqrt(c2, sm[:, 0:Q])
                do(c2, vec.tensor_tensor(s3, s3, rstd[:, :].unsqueeze(2).broadcast_to([P, Q, 16]), ALU.mult))
                do(c2, vec.tensor_tensor(s3, s3, w["f_gam"][:, :].unsqueeze(1).broadcast_to([P, Q, 16]), ALU.mult))
                do(c2, vec.tensor_tensor(s3, s3, w["f_bet"][:, :].unsqueeze(1).broadcast_to([P, Q, 16]), ALU.add))
                scr, sel4 = gates[:, :, 0:E0], gates[:, :, E0:2 * E0]
                do(c2, vec.tensor_reduce(scr, small[:, :].rearrange("p (q h e) -> p q e h", q=Q, h=H0), AX, ALU.add))
                do(c2, vec.tensor_scalar(scr, scr, 1.0 / H0, None, op0=ALU.mult))
                top2(scr, E0, sel4)
                do(c2, vec.tensor_reduce(sm[:, 0:Q], scr, AX, ALU.max))
                ex0 = small[:, 0:Q * E0].rearrange("p (q e) -> p q e", q=Q)
                g0_ = small2[:, 0:Q * E0].rearrange("p (q e) -> p q e", q=Q)
                sig(V2, c, "gexp0", vec.tensor_tensor(ex0, scr, sm[:, 0:Q].unsqueeze(2).broadcast_to([P, Q, E0]), ALU.subtract))
                vec.wait_ge(A2.sem, A2.at(c, "gate0"))
                do(c2, vec.tensor_tensor(g0_, g0_, sel4, ALU.mult))
                do(c2, vec.tensor_reduce(sm[:, 0:Q], g0_, AX, ALU.add))
                do(c2, vec.reciprocal(sm[:, 4:8], sm[:, 0:Q]))
                do(c2, vec.tensor_tensor(mixw[:, :, 0:E0], g0_, sm[:, 4:8].unsqueeze(2).broadcast_to([P, Q, E0]), ALU.mult))
                vec.wait_ge(y_in, 16 * (c + 1))
                for e in range(E0):
                    for q in qs:
                        m = vec.scalar_tensor_tensor(xq(q), yb[:, q, e, :], mixw[:, q, e:e + 1], xq(q), ALU.mult, ALU.add)
                        if q < Q - 1:
                            c2.count(m)
                        elif e < E0 - 1:
                            do(c2, m)
                        else:
                            sig(V2, c, "x2", m, bare=True)
                norm(c2, xq, lambda q: xn[:, q, :], (V2, c, "xn"))
                vec.wait_ge(adj_in, 16 * (c + 1))
                sig(V2, c, "mask", vec.tensor_scalar(cols(bufC), adjc[:, :, :], 0.0, None, op0=ALU.is_gt))
                vec.wait_ge(T2.sem, T2.at(c, "maskT"))
                do(c2, vec.tensor_tensor(neg[:, :, :], cols(p6), cols(bufC), ALU.max))
                do(c2, vec.tensor_tensor(neg[:, :, :], neg[:, :, :], ident[:, :].unsqueeze(1).broadcast_to([P, Q, P]), ALU.max))
                sig(V2, c, "allowed", vec.tensor_scalar(neg[:, :, :], neg[:, :, :], FAR, -FAR, op0=ALU.mult, op1=ALU.add))
                for q in qs:
                    if q == 0:
                        vec.wait_ge(A2.sem, A2.at(c, "kT"))
                    sig(V2, c, f"keys{q}", vec.tensor_tensor(big1[:, :, :], bufB[:, q * P:(q + 1) * P].unsqueeze(1).broadcast_to([P, H1, P]),
                                                            headmask[:, :].unsqueeze(2).broadcast_to([P, H1, P]), ALU.mult))
                    vec.wait_ge(T2.sem, T2.at(c, f"scores{q}"))
                    do(c2, vec.tensor_tensor(big2[:, :, :], pS[:, :, :], neg[:, q:q + 1, :].broadcast_to([P, H1, P]), ALU.add))
                    do(c2, vec.tensor_reduce(mxh[:, :], big2[:, :, :], AX, ALU.max))
                    sig(V2, c, f"max{q}", vec.tensor_tensor(big2[:, :, :], big2[:, :, :], mxh[:, :].unsqueeze(2).broadcast_to([P, H1, P]), ALU.subtract))
                    vec.wait_ge(T2.sem, T2.at(c, f"ctx{q}"))
                    cx = p5[:, 0:H1 * 17].rearrange("p (h f) -> p h f", h=H1)
                    do(c2, vec.reciprocal(cden[:, :], cx[:, :, HD]))
                    sig(V2, c, f"ctx{q}", vec.tensor_tensor(bufC[:, q * P:(q + 1) * P].rearrange("p (h f) -> p h f", h=H1), cx[:, :, 0:HD],
                                                           cden[:, :].unsqueeze(2).broadcast_to([P, H1, HD]), ALU.mult))
                vec.wait_ge(T2.sem, T2.at(c, "attn"))
                bq = lambda t: (lambda q: t[:, q * P:(q + 1) * P])
                do(c2, vec.tensor_tensor(bufD[:, :], p5[:, :], xn[:, :, :].rearrange("p q f -> p (q f)"), ALU.add))
                norm(c2, bq(bufD), bq(bufD))
                do(c2, vec.tensor_tensor(cols(bufD), cols(bufD), w["a_g1"][:, :].unsqueeze(1).broadcast_to([P, Q, P]), ALU.mult))
                sig(V2, c, "y1", vec.tensor_tensor(cols(bufD), cols(bufD), w["a_b1"][:, :].unsqueeze(1).broadcast_to([P, Q, P]), ALU.add))
                vec.wait_ge(T2.sem, T2.at(c, "ff"))
                do(c2, vec.tensor_tensor(bufC[:, :], p5[:, :], bufD[:, :], ALU.add))
                norm(c2, bq(bufC), bq(bufC))
                do(c2, vec.tensor_tensor(cols(bufC), cols(bufC), w["a_g2"][:, :].unsqueeze(1).broadcast_to([P, Q, P]), ALU.mult))
                do(c2, vec.tensor_tensor(cols(bufC), cols(bufC), w["a_b2"][:, :].unsqueeze(1).broadcast_to([P, Q, P]), ALU.add))
                do(c2, vec.tensor_tensor(xc, cols(bufC), xc, ALU.add), bare=True)
                norm(c2, xq, lambda q: xn[:, q, :], (V2, c, "xn3"))
                vec.wait_ge(T2.sem, T2.at(c, "router"))
                lg = p5[:, 0:Q * E1].rearrange("p (q e) -> p q e", q=Q)
                do(c2, vec.tensor_reduce(sm[:, 0:Q], lg, AX, ALU.max))
                sig(V2, c, "gexp", vec.tensor_tensor(gates[:, :, :], lg, sm[:, 0:Q].unsqueeze(2).broadcast_to([P, Q, E1]), ALU.subtract))
                vec.wait_ge(A2.sem, A2.at(c, "rexp"))
                do(c2, vec.tensor_reduce(sm[:, 0:Q], gates[:, :, :], AX, ALU.add))
                do(c2, vec.reciprocal(sm[:, 4:8], sm[:, 0:Q]))
                do(c2, vec.tensor_tensor(gates[:, :, :], gates[:, :, :], sm[:, 4:8].unsqueeze(2).broadcast_to([P, Q, E1]), ALU.mult))
                sel8 = small[:, 0:Q * E1].rearrange("p (q e) -> p q e", q=Q)
                top2(gates[:, :, :], E1, sel8)
                do(c2, vec.tensor_tensor(gates[:, :, :], gates[:, :, :], sel8, ALU.mult))
                do(c2, vec.tensor_reduce(sm[:, 0:Q], gates[:, :, :], AX, ALU.add))
                do(c2, vec.reciprocal(sm[:, 4:8], sm[:, 0:Q]))
                sig(V2, c, "gate", vec.tensor_tensor(mixw[:, :, 1:1 + E1], gates[:, :, :], sm[:, 4:8].unsqueeze(2).broadcast_to([P, Q, E1]), ALU.mult))
                for e in range(E1 + 1):
                    vec.wait_ge(T2.sem, T2.at(c, f"down{e}"))
                    if e == 0:
                        sig(V2, c, "mix0", vec.tensor_tensor(xc, cols(p7), xc, ALU.add))
                        continue
                    for q in qs:
                        m = vec.scalar_tensor_tensor(xq(q), p7[:, q * P:(q + 1) * P], mixw[:, q, e:e + 1], xq(q), ALU.mult, ALU.add)
                        if q < Q - 1:
                            c2.count(m)
                        else:
                            sig(V2, c, f"mix{e}", m)
                c2.end()


_OUT = ((128, 128, 128), "float32")


def laid_out(i):
    c = np.ascontiguousarray
    rep = lambda v: c(np.broadcast_to(np.asarray(v).reshape(1, -1), (P, np.asarray(v).size)))
    row = lambda v: c(np.asarray(v).reshape(1, -1))
    col = lambda v: c(np.asarray(v).reshape(-1, P).T)
    n = {k: np.asarray(v) for k, v in i.items()}
    m1 = np.concatenate([n["L1_ffn_W1s"][None], n["L1_ffn_W1p"]])
    m2 = np.concatenate([n["L1_ffn_W2s"][None], n["L1_ffn_W2p"]])
    b1 = np.concatenate([n["L1_ffn_b1s"][None], n["L1_ffn_b1p"]])
    b2 = np.concatenate([n["L1_ffn_b2s"][None], n["L1_ffn_b2p"]])
    return {
        "x": c(n["x"]), "adj": c(n["adj"]), "edges": c(n["L0_ffn_edge_index"]),
        "g_W": c(n["L0_gnn_W"]), "g_a12": c(n["L0_gnn_a_12"]), "g_W1": c(n["L0_gnn_W_1"]), "g_W2": c(n["L0_gnn_W_2"]),
        "g_a1": c(n["L0_gnn_a_1"]), "g_a2": c(n["L0_gnn_a_2"]),
        "f_Wgat": c(n["L0_ffn_W_gat"]), "f_asrc": rep(n["L0_ffn_att_src"]), "f_adst": rep(n["L0_ffn_att_dst"]),
        "f_bgat": rep(n["L0_ffn_b_gat"]), "f_gam": rep(n["L0_ffn_ln_gamma"]), "f_bet": rep(n["L0_ffn_ln_beta"]),
        "f_W1": c(n["L0_ffn_W1"].reshape(E0, P, 2, P).transpose(1, 0, 2, 3)),
        "f_b1": c(n["L0_ffn_b1"].reshape(E0, 2, P).transpose(2, 0, 1)),
        "f_W2": c(n["L0_ffn_W2"].reshape(E0, 2, P, P).transpose(2, 0, 1, 3)), "f_b2": row(n["L0_ffn_b2"]),
        "a_Wqkv": c(n["L1_gnn_Wqkv"].T), "a_bqk": col(n["L1_gnn_bqkv"][:2 * P]), "a_bv": row(n["L1_gnn_bqkv"][2 * P:]),
        "a_Wo": c(n["L1_gnn_Wo"].T), "a_bo": row(n["L1_gnn_bo"]),
        "a_g1": rep(n["L1_gnn_ln1_g"]), "a_b1": rep(n["L1_gnn_ln1_b"]), "a_g2": rep(n["L1_gnn_ln2_g"]), "a_b2": rep(n["L1_gnn_ln2_b"]),
        "a_W1": c(n["L1_gnn_W1"].T.reshape(P, FC, P)), "a_c1": col(n["L1_gnn_b1"]),
        "a_W2": c(n["L1_gnn_W2"].T.reshape(FC, P, P).transpose(1, 0, 2)), "a_c2": row(n["L1_gnn_b2"]),
        "m_Wr": c(n["L1_ffn_Wr"]), "m_W1": c(m1.reshape(E1 + 1, P, FC, P).transpose(1, 0, 2, 3)),
        "m_b1": c(b1.reshape(E1 + 1, FC, P).transpose(2, 0, 1)),
        "m_W2": c(m2.reshape(E1 + 1, FC, P, P).transpose(2, 0, 1, 3)), "m_b2": row(b2),
    }


def kernel(**inputs):
    import concourse.bacc as bacc
    from concourse.bass_utils import run_bass_kernel_spmd

    nc = bacc.Bacc("TRN2", target_bir_lowering=False, num_devices=1)
    arrays, aps = {}, {}
    for name, v in laid_out(inputs).items():
        arrays[f"in_{name}"] = v
        aps[name] = nc.dram_tensor(f"in_{name}", v.shape, mybir.dt.from_np(v.dtype), kind="ExternalInput").ap()
    aps["out"] = nc.dram_tensor("out_x", _OUT[0], F32, kind="ExternalOutput").ap()
    program(nc, aps, NB=arrays["in_x"].shape[0], NE=arrays["in_edges"].shape[1])
    r = run_bass_kernel_spmd(nc, [arrays], core_ids=[0])
    return r.results[0]["out_x"]
```

```python
from contextlib import ExitStack

import numpy as np
import concourse.bass as bass
from concourse import mybir
from concourse.alu_op_type import AluOpType as ALU

ACT = mybir.ActivationFunctionType
AX = mybir.AxisListType.X
F32 = mybir.dt.float32
BF16 = mybir.dt.bfloat16
I32 = mybir.dt.int32
U32 = mybir.dt.uint32

P = 128
Q = 4
T = Q * P
GT = 4
GE = GT * P
ST = 8
RING = 32
H0, E0 = 4, 4
VW = H0 * (1 + E0)
PW = H0 + VW
H1 = 8
HD = P // H1
E1 = 8
FC = 4
EPS = 1e-5
NEG = 9e15
FAR = 1e30
HI, LO = 16, 8
CT = 64
SKIP = float(2**23)


PER = (106, 196)


class Steps:

    def __init__(self, sem, names):
        self.sem, self.names, self.n = sem, {s: k + 1 for k, s in enumerate(names)}, len(names)
        assert len(self.names) == len(names)

    def at(self, i, name):
        return (i + 1) * self.n + self.names[name]


class Chain:

    def __init__(self, sem, per):
        self.sem, self.per, self.n, self.i = sem, per, 0, 0

    def turn(self, i):
        self.i, self.n = i, 0

    def count(self, ins):
        self.n += 1
        ins.then_inc(self.sem, 1)

    def wait(self, eng):
        eng.wait_ge(self.sem, self.i * self.per + self.n)

    def end(self):
        assert self.n == self.per, (self.n, self.per)


def program(nc, a, NB, NE):
    NCH = NB // Q
    M = NB * P
    CE = NE // P // NCH
    SG = CE // ST
    assert SG * ST == CE and SG % 2 == 0
    FR = P * P * 4
    FILLS = 2 * -(-(NE + (NB + 8) * GE) // (2 * FR))
    CAP = FILLS * FR
    TURNS = -(-(NE // GE + NB + 1) // 4)
    FILLED = 16 * FILLS // 2
    sorted_edges = nc.dram_tensor("sorted_edges", (CAP, 2), U32, kind="Internal").ap()
    node_rows = nc.dram_tensor("node_rows", (M, PW), F32, kind="Internal").ap()
    expert_rows = nc.dram_tensor("expert_rows", (M, E0, P), F32, kind="Internal").ap()

    with ExitStack() as ctx:
        def sb(name, shape, dt=F32):
            return ctx.enter_context(nc.sbuf_tensor(name, shape, dt))

        def psum(name, shape, dt=F32):
            return ctx.enter_context(nc.psum_tensor(name, shape, dt))

        def sem(name):
            return ctx.enter_context(nc.semaphore(name))

        X = sb("X", [P, NB, P])
        pay = sb("pay", [P, NB, PW])
        dnf = sb("dn", [P, max(NB * H0, T)])
        dn = dnf[:, 0:NB * H0].rearrange("p (b h) -> p b h", h=H0)
        mixT = dnf[0:E1 + 1, 0:T]
        dm3 = sb("dm3", [P, NB, 3, 2 * H0], BF16)
        ring = sb("ring", [P, RING, GT, PW])
        ringf = ring[:, :, :, :].rearrange("p r k f -> p (r k f)")
        place = {"f_W1": ringf[:, 0:1024].rearrange("p (e f m) -> p e f m", e=E0, f=2),
                 "f_W2": ringf[:, 1024:2048].rearrange("p (e f m) -> p e f m", e=E0, f=2),
                 "g_W": ringf[:, 2048:2176], "g_a12": ringf[:, 2176:2304], "g_W1": ringf[:, 2304:2432],
                 "g_W2": ringf[:, 2432:2560], "f_b2": ringf[0:1, 2560:3072]}
        w = {}
        wl = []
        for name, shape in (
            ("g_W", [P, P]), ("g_a12", [P, P]), ("g_W1", [P, P]), ("g_W2", [P, P]), ("g_a1", [P, 1]), ("g_a2", [P, 1]),
            ("f_Wgat", [P, H0 * E0]), ("f_asrc", [P, H0 * E0]), ("f_adst", [P, H0 * E0]), ("f_bgat", [P, H0 * E0]),
            ("f_gam", [P, H0 * E0]), ("f_bet", [P, H0 * E0]),
            ("f_W1", [P, E0, 2, P]), ("f_b1", [P, E0, 2]), ("f_W2", [P, E0, 2, P]), ("f_b2", [1, E0 * P]),
            ("a_Wqkv", [P, 3 * P]), ("a_bqk", [P, 2]), ("a_bv", [1, P]), ("a_Wo", [P, P]), ("a_bo", [1, P]),
            ("a_g1", [P, P]), ("a_b1", [P, P]), ("a_g2", [P, P]), ("a_b2", [P, P]),
            ("a_W1", [P, FC, P]), ("a_c1", [P, FC]), ("a_W2", [P, FC, P]), ("a_c2", [1, P]),
            ("m_Wr", [P, E1]), ("m_W1", [P, E1 + 1, FC, P]), ("m_b1", [P, E1 + 1, FC]),
            ("m_W2", [P, E1 + 1, FC, P]), ("m_b2", [E1 + 1, P]),
        ):
            w[name] = place.get(name)
            if w[name] is None:
                w[name] = sb(name, shape)[tuple(slice(None) for _ in shape)]
            wl.append((w[name], a[name]))

        ident = sb("ident", [P, P])
        identb = sb("identb", [P, P], BF16)
        iota = sb("iota", [P, P], BF16)
        before = sb("before", [P, P], BF16)
        notbefore = sb("notbefore", [P, P], BF16)
        onesb = sb("onesb", [P, P], BF16)
        zerob = sb("zerob", [P, ST * LO], BF16)
        zero = sb("zero", [P, P])
        ones1 = sb("ones1", [1, P])
        headmask = sb("headmask", [P, H1])
        lower = sb("lower", [P, E1, E1])

        adjc = sb("adjc", [P, Q, P], I32)
        words = sb("words", [P, 4 * CE])
        assert CE == P
        srcc, dstc, tmpi = (words[:, k * CE:(k + 1) * CE].bitcast(I32) for k in range(3))
        far = words[:, 3 * CE:4 * CE]
        dhi = sb("dhi", [P, CE], BF16)
        rec = sb("rec", [P, CE, 2], U32)
        pos = sb("pos", [P, ST])
        idx = sb("idx", [P, 2, ST], U32)
        recs = sb("recs", [P, 2, ST, 2], U32)
        starts = sb("starts", [P, NB + 1])
        tot = sb("tot", [P, NB])
        toti = sb("toti", [P, NB + 2], I32)
        gstart = sb("gstart", [1, NB + 2], I32)
        bst = sb("bst", [P, Q, 6])
        mv = sb("mv", [P, Q, 2])
        nb_ = sb("nb_", [P, Q, 4])
        nbi = sb("nbi", [P, Q], I32)
        rstd = sb("rstd", [P, Q])
        xn = sb("xn", [P, Q, P])
        xT = sb("xT", [P, T])
        bufA = sb("bufA", [P, T])
        bufB = sb("bufB", [P, T])
        bufC = sb("bufC", [P, T])
        bufD = sb("bufD", [P, T])
        sm = sb("sm", [P, 16])
        small = sb("small", [P, Q * H0 * E0])
        small2 = sb("small2", [P, Q * H0 * E0])
        gmx = sb("gmx", [P, H0])
        gmall = sb("gmall", [P, H0])
        yb = sb("yb", [P, Q, E0, P])
        big1 = sb("big1", [P, 8, P])
        big2 = sb("big2", [P, 8, P])
        big3 = sb("big3", [P, 8, P])

        stage = sb("stage", [P, 2, 2, GT, PW])
        gidx = sb("gidx", [P, 2, 2, GT, 2], U32)
        ring_dst = sb("ring_dst", [P, RING, GT, 2], U32)
        Og = sb("Og", [P, 2, GT, P], BF16)
        OT = words[:, :].bitcast(BF16)[:, 0:GT * P].rearrange("p (k e) -> p k e", k=GT)
        zg = sb("zg", [P, GT, H0])
        eg = sb("eg", [P, GT, H0])
        Vg = sb("Vg", [P, GT, VW])
        V3 = sb("V3", [P, GT, 3, VW], BF16)
        agg = sb("agg", [P, Q, VW])
        xTb = sb("xTb", [P, T])
        mix0 = sb("mix0", [P, Q, E0])
        mixw = sb("mixw", [P, Q, E1 + 1])
        ffh = [t[:, 4 * h:4 * h + 4, :].rearrange("p a b -> p (a b)") for t in (big1, big2) for h in range(2)]
        gates = sb("gates", [P, Q, E1])
        pairs = big1[:, 0:4, :].rearrange("p a (b c) -> p (a b) c", c=E1)
        cmp1 = pairs[:, 0:Q * E1, :].rearrange("p (q a) c -> p q a c", q=Q)
        cmp2 = pairs[:, Q * E1:2 * Q * E1, :].rearrange("p (q a) c -> p q a c", q=Q)
        vext = sb("vext", [P, Q, H1, HD + 1])
        cden = sb("cden", [P, H1])
        neg = sb("neg", [P, Q, P])
        mxh = sb("mxh", [P, H1])
        hid1 = sb("hid1", [P, FC, T])
        hid = hid1[:, 0:2, :]
        rows_b = yb[:, :, :, :].bitcast(BF16).rearrange("p q e f -> p (q e f)")
        hi1 = rows_b[:, 0:2 * CT * HI].rearrange("p (o n) -> p o n", o=2)
        lo1 = rows_b[:, 2 * CT * HI:2 * CT * (HI + LO)].rearrange("p (o n) -> p o n", o=2)
        O = hid1[:, 2:4, :].bitcast(BF16).rearrange("p o (k b) -> p o k b", k=ST)

        pR = psum("pR", [P, 8, P])
        pS = psum("pS", [P, 8, P])
        p4 = psum("p4", [P, T])
        p4b = p4[:, :].bitcast(BF16)[:, 0:GT * P]
        p5 = psum("p5", [P, T])
        p6 = psum("p6", [P, T])
        p7 = psum("p7", [P, T])

        weights_in = sem("weights_in")
        edges_in = sem("edges_in")
        x_in = sem("x_in")
        consts = sem("consts")
        counted_onehot = sem("counted_onehot")
        counted = sem("counted")
        bases_ready = sem("bases_ready")
        chunk_in = sem("chunk_in")
        scattered = [sem("scattered0"), sem("scattered1")]
        rows_out = sem("rows_out")
        experts_out = sem("experts_out")
        stores_done = sem("stores_done")
        guard_ready = sem("guard_ready")
        tables_ready = sem("tables_ready")
        passed = sem("passed")
        setup_chain = sem("setup_chain")
        chain1 = sem("chain1")
        chain2 = sem("chain2")
        chaing = sem("chaing")
        chainm = sem("chainm")
        chainb = sem("chainb")
        gidx_in = [sem("gidx_in0"), sem("gidx_in1")]
        gathered = [sem("gathered0"), sem("gathered1")]
        ring_out = sem("ring_out")
        ring_filled = sem("ring_filled")
        ring_freed = sem("ring_freed")
        y_in = sem("y_in")
        adj_in = sem("adj_in")
        result_out = sem("result_out")

        vwork = {0: ["xn"], 5: ["masked"], 6: ["prob"], 9: ["zmin"], 10: ["x1"], 11: ["xn1"], 13: ["pay"]}
        twork = {1: ["xT"], 2: ["hT"], 3: ["gT", "ay"], 4: ["logits"], 7: ["PT", "hpT"], 8: ["hout"], 12: ["xT1", "hrow"]}
        for e in range(E0):
            twork[12 + e] = twork.get(12 + e, []) + [f"up0_{e}", f"up1_{e}", f"down{e}"]
        ahead = lambda name, g: [f"{name}{g + 1}"] if g + 1 < SG else []
        V1 = Steps(sem("vector_1"), ["onehot0"] + [s for g in range(SG) for s in [f"prod{g}", f"idx{g}"] + ahead("onehot", g) + vwork.get(g, [])])
        T1 = Steps(sem("tensor_1"), ["rank0"] + [s for g in range(SG) for s in [f"ranked{g}"] + ahead("rank", g) + twork.get(g, [])])
        A1 = Steps(sem("scalar_1"), ["xT", "hT", "gT", "ay", "exp", "PT", "hpT", "elu", "xT1"]
                   + [f"{s}{e}" for e in range(E0) for s in ("gelu0_", "gelu1_", "y")])
        VG = Steps(sem("vector_g"), ["z", "next_onehot", "parts"])
        TG = Steps(sem("tensor_g"), ["dstscore", "next_T", "sums"])
        AG = Steps(sem("scalar_g"), ["exp", "next_T"])
        qs = range(Q)
        order = list(range(1, E1 + 1)) + [0]
        V2 = Steps(sem("vector_2"), ["agg", "gexp0", "x2", "xn", "mask", "allowed", "keys0"]
                   + [s for q in qs for s in [f"max{q}"] + ([f"keys{q + 1}"] if q < Q - 1 else []) + [f"ctx{q}"]]
                   + ["y1", "xn3", "gexp", "gate"])
        T2 = Steps(sem("tensor_2"), ["xT", "qT", "kT", "v", "maskT"]
                   + [f"{s}{q}" for q in qs for s in ("scores", "PT", "ctx")]
                   + ["ctxT", "attn", "y1T"] + [f"ffup{f}" for f in range(FC)] + ["ff", "xT3", "router", "mixT"])
        A2 = Steps(sem("scalar_2"), ["gate0", "xT", "qT", "kT", "v"]
                   + [f"{s}{q}" for q in qs for s in ("exp", "PT")]
                   + ["ctxT", "y1T"] + [f"relu{f}" for f in range(FC)] + ["xT3", "rexp", "mixT"])
        VB = Steps(sem("vector_b"), [f"mix{e}" for e in order])
        TB = Steps(sem("tensor_b"), [f"{s}{e}" for e in order for s in ("up0_", "up1_", "up2_", "up3_", "down")])
        AB = Steps(sem("scalar_b"), [f"gelu{f}_{e}" for e in order for f in range(FC)])

        block = ctx.enter_context(nc.Block())

        sorted_tiles = sorted_edges.rearrange("(g p k) w -> p g k w", p=P, k=GT)

        CH1, CH2 = PER

        @block.sync
        def _(sp):
            def wait(sm_, value):
                sp.wait_ge(sm_, value)
                sp.sem_inc(passed, 1)

            sp.dma_start(X[:, :, :].bitcast(I32).rearrange("p b f -> p (b f)")[:, 0:NE // P],
                         a["edges"][1].rearrange("(p c) -> p c", p=P)).then_inc(edges_in, 16)
            for tile, src in wl:
                sp.dma_start(tile, src).then_inc(weights_in, 16)

            e_view = [a["edges"][r].rearrange("(p c) -> p c", p=P) for r in range(2)]

            def load_chunk(c):
                sp.dma_start(adjc[:, :, :], a["adj"].rearrange("b i j -> i b j")[:, bass.ds(c * Q, Q), :]).then_inc(chunk_in, 16)
                sp.dma_start(srcc, e_view[0][:, bass.ds(c * CE, CE)]).then_inc(chunk_in, 16)
                sp.dma_start(dstc, e_view[1][:, bass.ds(c * CE, CE)]).then_inc(chunk_in, 16)

            sp.wait_ge(bases_ready, 1)
            sp.dma_start(X[:, :, :], a["x"].rearrange("b n f -> n b f")).then_inc(x_in, 16)
            load_chunk(0)
            sp.sem_inc(stores_done, 1)
            with sp.Fori(0, NCH) as c:
                wait(V1.sem, V1.at(c, "masked"))
                load_chunk((c + 1) % NCH)
                wait(V1.sem, V1.at(c, "pay"))
                sp.dma_start(node_rows.rearrange("(b n) w -> n b w", n=P)[:, bass.ds(c * Q, Q), :],
                             pay[:, bass.ds(c * Q, Q), :]).then_inc(rows_out, 16)
                wait(A1.sem, A1.at(c, f"y{E0 - 1}"))
                sp.dma_start(expert_rows.rearrange("(b n) e f -> n b e f", n=P)[:, bass.ds(c * Q, Q), :, :],
                             yb[:, :, :, :]).then_inc(experts_out, 16)
                wait(rows_out, 16 * (c + 1))
                wait(experts_out, 16 * (c + 1))
                sp.sem_inc(stores_done, 1)
            wait(chunk_in, 48 * (NCH + 1))

            for h in range(2):
                wait(scattered[h], FILLED + 128 * (NCH * SG // 2))

            def load_idx(it, h):
                sp.dma_start(gidx[:, h, :, :, :], sorted_tiles[:, bass.ds(it * 4 + h * 2, 2), :, :]).then_inc(gidx_in[h], 16)

            for h in range(2):
                load_idx(0, h)
            turns = sp.value_load(gstart[0:1, NB + 1:NB + 2], min_val=1, max_val=TURNS)
            with sp.Fori(0, turns) as it:
                for h in range(2):
                    slot = (it % (RING // 4)) * 4 + 2 * h
                    wait(gathered[h], 128 * (it + 1))
                    wait(ring_freed, it * 4 + 2 * h + 2)
                    sp.dma_start(ring[:, bass.ds(slot, 2), :, :], stage[:, h, :, :, :]).then_inc(ring_out, 16)
                    sp.dma_start(ring_dst[:, bass.ds(slot, 2), :, :], gidx[:, h, :, :, :]).then_inc(ring_out, 16)
                    wait(ring_out, 64 * it + 32 * (h + 1))
                    sp.sem_inc(ring_filled, 2)
                    load_idx(it + 1, h)
            for h in range(2):
                wait(gidx_in[h], 16 * turns + 16)
            sp.wait_ge(result_out, 16 * NCH)


        @block.gpsimd
        def _(pool):
            pool.iota(iota[:, :], pattern=[[1, P]], base=0, channel_multiplier=0,
                      allow_small_or_imprecise_dtypes=True).then_inc(consts, 1)
            pool.memset(onesb[:, :], 1.0).then_inc(consts, 1)
            pool.memset(zero[:, :], 0.0).then_inc(consts, 1)
            pool.memset(zerob[:, :], 0.0).then_inc(consts, 1)
            pool.memset(ones1[:, :], 1.0).then_inc(consts, 1)
            pool.memset(big3[:, :, :], 1.0).then_inc(consts, 1)
            pool.memset(pay[:, :, :], 1.0).then_inc(consts, 1)
            pool.memset(vext[:, :, :, :], 1.0).then_inc(consts, 1)
            fill = big2[:, :, :].rearrange("p a b -> p (a b)").bitcast(U32).rearrange("p (c w) -> p c w", w=2)
            pool.memset(fill[:, :, 0], 0).then_inc(consts, 1)
            pool.memset(fill[:, :, 1].bitcast(F32), -1.0).then_inc(consts, 1)
            pool.wait_ge(consts, 10)
            pool.affine_select(out=before[:, :], in_=onesb[:, :], compare_op=ALU.is_gt, fill=0.0, base=0,
                               pattern=[[1, P]], channel_multiplier=-1).then_inc(consts, 1)
            pool.affine_select(out=notbefore[:, :], in_=onesb[:, :], compare_op=ALU.is_ge, fill=0.0, base=0,
                               pattern=[[-1, P]], channel_multiplier=1).then_inc(consts, 1)
            pool.affine_select(out=ident[:, :], in_=zero[:, :], compare_op=ALU.not_equal, fill=1.0, base=0,
                               pattern=[[-1, P]], channel_multiplier=1).then_inc(consts, 1)
            pool.affine_select(out=headmask[:, :], in_=big3[:, 0, 0:H1], compare_op=ALU.is_ge, fill=0.0, base=0,
                               pattern=[[-HD, H1]], channel_multiplier=1).then_inc(consts, 1)
            pool.affine_select(out=lower[:, :, :], in_=big3[:, 0, 0:E1 * E1].rearrange("p (a b) -> p a b", a=E1),
                               compare_op=ALU.is_gt, fill=0.0, base=0,
                               pattern=[[1, E1], [-1, E1]], channel_multiplier=0).then_inc(consts, 1)
            pool.wait_ge(consts, 15)
            pool.tensor_copy(identb[:, :], ident[:, :]).then_inc(consts, 1)
            pool.affine_select(out=headmask[:, :], in_=headmask[:, :], compare_op=ALU.is_ge, fill=0.0, base=HD - 1,
                               pattern=[[HD, H1]], channel_multiplier=-1).then_inc(consts, 1)
            fills = sorted_edges.rearrange("(r p c) w -> r p c w", p=P, c=4 * P)
            for r in range(FILLS):
                pool.dma_start(fills[r], fill).then_inc(scattered[r % 2], 16)
            for h in range(2):
                pool.wait_ge(scattered[h], FILLED)

            last = pool.to_reg(CAP - 1)
            with pool.Fori(0, NCH) as c:
                for g in range(SG):
                    pool.wait_ge(V1.sem, V1.at(c, f"idx{g}"))
                    pool.sem_inc(passed, 1)
                    for k in range(ST):
                        pool.indirect_dma_start(
                            out=sorted_edges, out_offset=bass.IndirectOffsetOnAxis(ap=idx[:, g % 2, k:k + 1], axis=0),
                            in_=recs[:, g % 2, k, :], in_offset=None, bounds_check=last, oob_is_err=False,
                        ).then_inc(scattered[g % 2], 16)

            pool.wait_ge(V1.sem, V1.at(NCH - 1, "pay"))
            pool.partition_all_reduce(gmall[:, :], gmx[:, :], P, bass.bass_isa.ReduceOp.max).then_inc(guard_ready, 1)

            turns = pool.value_load(gstart[0:1, NB + 1:NB + 2], min_val=1, max_val=TURNS)
            with pool.Fori(0, turns) as it:
                for h in range(2):
                    pool.wait_ge(gidx_in[h], 16 * (it + 1))
                    pool.sem_inc(passed, 1)
                    for g in range(2):
                        for k in range(GT):
                            pool.indirect_dma_start(
                                out=stage[:, h, g, k, :], out_offset=None, in_=node_rows,
                                in_offset=bass.IndirectOffsetOnAxis(ap=gidx[:, h, g, k, 0:1], axis=0),
                            ).then_inc(gathered[h], 16)

        @block.scalar
        def _(act):
            act.wait_ge(weights_in, 16 * len(wl))
            act.wait_ge(consts, 17)
            act.activation(sm[:, 15:16], zero[:, 0:1], ACT.Copy).then_inc(A1.sem, A1.n)

            def copy(steps, i, name, dst, src, *waits):
                for st, what in waits:
                    act.wait_ge(st.sem, st.at(i, what))
                act.activation(dst, src, ACT.Copy).then_inc(steps.sem, 1)

            with act.Fori(0, NCH) as c:
                copy(A1, c, "xT", xT[:, :], p4[:, :], (T1, "xT"))
                copy(A1, c, "hT", bufA[:, :], p5[:, :], (T1, "hT"))
                act.wait_ge(T1.sem, T1.at(c, "gT"))
                act.activation(bufB[:, :], p4[:, :], ACT.Identity, bias=w["g_a1"][:, 0:1]).then_inc(A1.sem, 1)
                copy(A1, c, "ay", sm[:, 0:Q], p6[:, 0:Q], (T1, "ay"))
                act.wait_ge(V1.sem, V1.at(c, "masked"))
                act.activation(bufC[:, :], bufC[:, :], ACT.Exp).then_inc(A1.sem, 1)
                copy(A1, c, "PT", bufD[:, :], p4[:, :], (T1, "PT"))
                copy(A1, c, "hpT", bufB[:, :], p5[:, :], (T1, "hpT"))
                act.wait_ge(V1.sem, V1.at(c, "zmin"))
                act.activation(bufC[:, :], bufC[:, :], ACT.Exp).then_inc(A1.sem, 1)
                copy(A1, c, "xT1", xT[:, :], p5[:, :], (T1, "xT1"))
                for e in range(E0):
                    for f in range(2):
                        act.wait_ge(T1.sem, T1.at(c, f"up{f}_{e}"))
                        act.activation(hid[:, f, :], pS[:, 4 * f:4 * f + 4, :], ACT.Gelu,
                                       bias=w["f_b1"][:, e, f:f + 1]).then_inc(A1.sem, 1)
                    act.wait_ge(T1.sem, T1.at(c, f"down{e}"))
                    if e == 0:
                        act.wait_ge(stores_done, c + 1)
                    act.activation(yb[:, :, e, :], p7[:, :].rearrange("p (q f) -> p q f", q=Q), ACT.Copy).then_inc(A1.sem, 1)

            act.wait_ge(stores_done, NCH + 1)
            act.wait_ge(chunk_in, 48 * (NCH + 1))
            act.activation(sm[:, 15:16], zero[:, 0:1], ACT.Copy).then_inc(A2.sem, A2.n)
            act.wait_ge(tables_ready, 1)
            act.activation(dn, dn, ACT.Exp).then_inc(guard_ready, 1)
            act.activation(sm[:, 14:15], zero[:, 0:1], ACT.Copy).then_inc(AB.sem, AB.n)

            def transposed_rows():
                return act.activation(OT[:, :, :], p4b[:, :].rearrange("p (k e) -> p k e", k=GT), ACT.Copy)

            act.wait_ge(TG.sem, TG.at(-1, "next_T"))
            transposed_rows().then_inc(AG.sem, AG.n)

            def load_y(c):
                act.dma_start(yb[:, :, :, :], expert_rows.rearrange("(b n) e f -> n b e f", n=P)[:, bass.ds(c * Q, Q), :, :]).then_inc(y_in, 16)

            def load_adj(c):
                act.dma_start(adjc[:, :, :], a["adj"].rearrange("b i j -> i b j")[:, bass.ds(c * Q, Q), :]).then_inc(adj_in, 16)

            load_y(0)
            load_adj(0)

            def back(c, s):
                e = order[s]
                for f in range(FC):
                    act.wait_ge(TB.sem, TB.at(c, f"up{f}_{e}"))
                    act.activation(hid1[:, f, :], pR[:, 4 * (f % 2):4 * (f % 2) + 4, :], ACT.Gelu,
                                   bias=w["m_b1"][:, e, f:f + 1]).then_inc(AB.sem, 1)

            def store(c):
                act.wait_ge(VB.sem, VB.at(c, "mix0"))
                act.dma_start(a["out"].rearrange("b n f -> n b f")[:, bass.ds(c * Q, Q), :],
                              X[:, bass.ds(c * Q, Q), :]).then_inc(result_out, 16)

            def front(c, behind):
                for q in qs:
                    g0 = act.value_load(gstart[0:1, bass.ds(c * Q + q, 1)], min_val=0, max_val=CAP // GE)
                    g1 = act.value_load(gstart[0:1, bass.ds(c * Q + q + 1, 1)], min_val=1, max_val=CAP // GE)
                    with act.Fori(g0, g1) as g:
                        act.wait_ge(VG.sem, VG.at(g, "z"))
                        act.activation(eg[:, :, :], zg[:, :, :], ACT.Exp).then_inc(AG.sem, 1)
                        act.wait_ge(TG.sem, TG.at(g, "next_T"))
                        transposed_rows().then_inc(AG.sem, 1)
                behind(0)
                act.wait_ge(V2.sem, V2.at(c, "gexp0"))
                act.activation(small2[:, 0:Q * E0], small[:, 0:Q * E0], ACT.Exp).then_inc(A2.sem, 1)
                behind(1)
                behind(2)
                act.wait_ge(V2.sem, V2.at(c, "x2"))
                load_y((c + 1) % NCH)
                copy(A2, c, "xT", xT[:, :], p4[:, :], (T2, "xT"))
                act.wait_ge(V2.sem, V2.at(c, "mask"))
                load_adj((c + 1) % NCH)
                act.wait_ge(T2.sem, T2.at(c, "qT"))
                act.activation(bufA[:, :], p5[:, :], ACT.Identity, bias=w["a_bqk"][:, 0:1]).then_inc(A2.sem, 1)
                act.wait_ge(T2.sem, T2.at(c, "kT"))
                act.activation(bufB[:, :], p4[:, :], ACT.Identity, bias=w["a_bqk"][:, 1:2]).then_inc(A2.sem, 1)
                act.wait_ge(T2.sem, T2.at(c, "v"))
                act.activation(vext[:, :, :, 0:HD].rearrange("p q h d -> p (q h) d"),
                               p5[:, :].rearrange("p (q d) -> p q d", d=HD), ACT.Copy).then_inc(A2.sem, 1)
                for q in qs:
                    behind(3 + q)
                    act.wait_ge(V2.sem, V2.at(c, f"max{q}"))
                    act.activation(big2[:, :, :], big2[:, :, :], ACT.Exp, scale=HD ** -0.5).then_inc(A2.sem, 1)
                    act.wait_ge(T2.sem, T2.at(c, f"PT{q}"))
                    act.activation(big3[:, :, :], pS[:, :, :], ACT.Copy).then_inc(A2.sem, 1)
                copy(A2, c, "ctxT", bufA[:, :], p4[:, :], (T2, "ctxT"))
                behind(7)
                copy(A2, c, "y1T", xT[:, :], p4[:, :], (T2, "y1T"))
                for f in range(FC):
                    act.wait_ge(T2.sem, T2.at(c, f"ffup{f}"))
                    act.activation(ffh[f], pS[:, 4 * (f % 2):4 * (f % 2) + 4, :], ACT.Relu,
                                   bias=w["a_c1"][:, f:f + 1]).then_inc(A2.sem, 1)
                behind(8)
                copy(A2, c, "xT3", xTb[:, :], p4[:, :], (T2, "xT3"))
                act.wait_ge(V2.sem, V2.at(c, "gexp"))
                act.activation(gates[:, :, :], gates[:, :, :], ACT.Exp).then_inc(A2.sem, 1)
                copy(A2, c, "mixT", mixT, p4[0:E1 + 1, :], (T2, "mixT"))

            front(0, lambda s: None)
            with act.Fori(1, NCH) as c:
                front(c, lambda s: back(c - 1, s))
                store(c - 1)
            for s_ in range(E1 + 1):
                back(NCH - 1, s_)
            store(NCH - 1)
            act.wait_ge(y_in, 16 * (NCH + 1))
            act.wait_ge(adj_in, 16 * (NCH + 1))

        @block.tensor
        def _(pe):
            pe.wait_ge(weights_in, 16 * len(wl))
            pe.wait_ge(consts, 17)
            pe.matmul(p7[:, 0:ST * LO], onesb[:, :], zerob[:, :], start=True, stop=False, skip_group_check=True).then_inc(counted, 2)
            with pe.Fori(0, NE // P // CT // 2) as i:
                for o in range(2):
                    pe.wait_ge(counted_onehot, 2 * i + o + 1)
                    for s in range(CT // ST):
                        m = pe.matmul(p7[:, 0:ST * LO], hi1[:, o, s * ST * HI:(s + 1) * ST * HI], lo1[:, o, s * ST * LO:(s + 1) * ST * LO],
                                      start=False, stop=False, skip_group_check=True)
                    m.then_inc(counted, 1)
            pe.wait_ge(counted_onehot, NE // P // CT + 1)
            for h in range(2):
                m = pe.matmul(pS[:, 4 * h:4 * h + 4, :], big3[:, 0, :], big1[:, 4 * h:4 * h + 4, :], start=True, stop=True)
            m.then_inc(counted, 1)
            pe.wait_ge(bases_ready, 1)
            for h in range(2):
                m = pe.matmul(pR[:, 4 * h:4 * h + 4, 0:NB], ident[:, :], big1[:, 4 * h:4 * h + 4, 0:NB],
                              start=True, stop=False, skip_group_check=True)
            m.then_inc(T1.sem, T1.n)

            def rank(c, g):
                pe.wait_ge(V1.sem, V1.at(c, f"onehot{g}"))
                for h in range(2):
                    m = pe.matmul(pR[:, 4 * h:4 * h + 4, 0:NB], before[:, :], O[:, g % 2, 4 * h:4 * h + 4, 0:NB],
                                  start=False, stop=False, skip_group_check=True)
                m.then_inc(T1.sem, 1)

            def ranked(c, g):
                pe.wait_ge(V1.sem, V1.at(c, f"prod{g}"))
                for h in range(2):
                    m = pe.matmul(pR[:, 4 * h:4 * h + 4, 0:NB], notbefore[:, :], O[:, g % 2, 4 * h:4 * h + 4, 0:NB],
                                  start=False, stop=False, skip_group_check=True)
                m.then_inc(T1.sem, 1)

            def turn(dst, src, inc, who=ident):
                for q in qs:
                    m = pe.transpose(dst[:, q * P:(q + 1) * P], src[:, q * P:(q + 1) * P], ident[:, :])
                m.then_inc(inc.sem, 1)

            def flat(t):
                return t[:, :, :].rearrange("p q f -> p (q f)")

            def rows_bias(dst, q, bias, start=False):
                return pe.matmul(dst[:, q * P:(q + 1) * P], ones1[:, :], bias, start=start, stop=True)

            def slices(c):
                def s_xT():
                    pe.wait_ge(V1.sem, V1.at(c, "xn"))
                    turn(p4, flat(xn), T1)

                def s_hT():
                    pe.wait_ge(A1.sem, A1.at(c, "xT"))
                    pe.matmul(p5[:, :], w["g_W"][:, :], xT[:, :], start=True, stop=True).then_inc(T1.sem, 1)

                def s_gT():
                    pe.wait_ge(A1.sem, A1.at(c, "hT"))
                    pe.matmul(p4[:, :], w["g_a12"][:, :], bufA[:, :], start=True, stop=True).then_inc(T1.sem, 1)
                    for q in qs:
                        m = pe.matmul(p6[:, q:q + 1], bufA[:, q * P:(q + 1) * P], w["g_a2"][:, :], start=True, stop=True)
                    m.then_inc(T1.sem, 1)

                def s_logits():
                    pe.wait_ge(A1.sem, A1.at(c, "gT"))
                    for q in qs:
                        m = pe.matmul(p5[:, q * P:(q + 1) * P], bufB[:, q * P:(q + 1) * P], bufA[:, q * P:(q + 1) * P],
                                      start=True, stop=True)
                    m.then_inc(T1.sem, 1)

                def s_PT():
                    pe.wait_ge(V1.sem, V1.at(c, "prob"))
                    turn(p4, bufC, T1)
                    pe.wait_ge(A1.sem, A1.at(c, "PT"))
                    for q in qs:
                        m = pe.matmul(p5[:, q * P:(q + 1) * P], xn[:, q, :], bufD[:, q * P:(q + 1) * P], start=True, stop=True)
                    m.then_inc(T1.sem, 1)

                def s_hout():
                    pe.wait_ge(A1.sem, A1.at(c, "hpT"))
                    for q in qs:
                        pe.matmul(p4[:, q * P:(q + 1) * P], xT[:, q * P:(q + 1) * P], w["g_W1"][:, :], start=True, stop=False)
                        m = pe.matmul(p4[:, q * P:(q + 1) * P], bufB[:, q * P:(q + 1) * P], w["g_W2"][:, :], start=False, stop=True)
                    m.then_inc(T1.sem, 1)

                def s_hrow():
                    pe.wait_ge(V1.sem, V1.at(c, "xn1"))
                    turn(p5, flat(xn), T1)
                    pe.wait_ge(A1.sem, A1.at(c, "xT1"))
                    for q in qs:
                        m = pe.matmul(p6[:, q * 16:(q + 1) * 16], xT[:, q * P:(q + 1) * P], w["f_Wgat"][:, :], start=True, stop=True)
                    m.then_inc(T1.sem, 1)

                def s_expert(e):
                    for f in range(2):
                        if e > 0:
                            pe.wait_ge(A1.sem, A1.at(c, f"gelu{f}_{e - 1}"))
                        pe.matmul(pS[:, 4 * f:4 * f + 4, :], w["f_W1"][:, e, f, :], xT[:, :], start=True, stop=True).then_inc(T1.sem, 1)
                    for f in range(2):
                        pe.wait_ge(A1.sem, A1.at(c, f"gelu{f}_{e}"))
                    if e > 0:
                        pe.wait_ge(A1.sem, A1.at(c, f"y{e - 1}"))
                    for q in qs:
                        for f in range(2):
                            pe.matmul(p7[:, q * P:(q + 1) * P], hid[:, f, q * P:(q + 1) * P], w["f_W2"][:, e, f, :],
                                      start=(f == 0), stop=False)
                        m = rows_bias(p7, q, w["f_b2"][0:1, e * P:(e + 1) * P])
                    m.then_inc(T1.sem, 1)

                return {1: [s_xT], 2: [s_hT], 3: [s_gT], 4: [s_logits], 7: [s_PT], 8: [s_hout],
                        12: [s_hrow, lambda: s_expert(0)]} | {12 + e: [lambda e=e: s_expert(e)] for e in range(1, E0)}

            with pe.Fori(0, NCH) as c:
                work = slices(c)
                rank(c, 0)
                for g in range(SG):
                    ranked(c, g)
                    if g + 1 < SG:
                        rank(c, g + 1)
                    for slice_ in work.get(g, []):
                        slice_()
            pe.wait_ge(A1.sem, A1.at(NCH - 1, f"y{E0 - 1}"))
            for steps in (T2, TB):
                pe.matmul(p7[:, 0:P], ident[:, :], ident[:, :], start=True, stop=True).then_inc(steps.sem, steps.n)

            def transposed_rows(g):
                for k in range(GT):
                    m = pe.transpose(p4b[:, k * P:(k + 1) * P], og(g)[:, k, :], identb[:, :])
                return m

            def og(g):
                return Og[:, bass.ds(g % 2, 1), :, :].rearrange("p o k e -> p (o k) e")

            pe.wait_ge(VG.sem, VG.at(-1, "next_onehot"))
            transposed_rows(0).then_inc(TG.sem, TG.n)

            def up(c, s):
                e = order[s]
                for f in range(FC):
                    if f >= 2:
                        pe.wait_ge(AB.sem, AB.at(c, f"gelu{f - 2}_{e}"))
                    elif s > 0:
                        pe.wait_ge(AB.sem, AB.at(c, f"gelu{f + 2}_{order[s - 1]}"))
                    pe.matmul(pR[:, 4 * (f % 2):4 * (f % 2) + 4, :], w["m_W1"][:, e, f, :], xTb[:, :], start=True, stop=True).then_inc(TB.sem, 1)

            def down(c, s):
                e = order[s]
                pe.wait_ge(AB.sem, AB.at(c, f"gelu{FC - 1}_{e}"))
                if s > 0:
                    pe.wait_ge(VB.sem, VB.at(c, f"mix{order[s - 1]}"))
                for q in qs:
                    if e == 0:
                        pe.matmul(p7[:, q * P:(q + 1) * P], mixT[:, q * P:(q + 1) * P], w["m_b2"][:, :], start=True, stop=False)
                    for f in range(FC):
                        m = pe.matmul(p7[:, q * P:(q + 1) * P], hid1[:, f, q * P:(q + 1) * P], w["m_W2"][:, e, f, :],
                                      start=(f == 0 and e > 0), stop=(f == FC - 1))
                m.then_inc(TB.sem, 1)

            def front(c, up, down):
                pe.wait_ge(A2.sem, A2.at(c - 1, "mixT"))
                for q in qs:
                    pe.matmul(p6[:, q * 3 * VW:(q + 1) * 3 * VW], onesb[:, :], zerob[:, 0:3 * VW], start=True, stop=False, skip_group_check=True)
                    g0 = pe.value_load(gstart[0:1, bass.ds(c * Q + q, 1)], min_val=0, max_val=CAP // GE)
                    g1 = pe.value_load(gstart[0:1, bass.ds(c * Q + q + 1, 1)], min_val=1, max_val=CAP // GE)
                    with pe.Fori(g0, g1) as g:
                        pe.wait_ge(AG.sem, AG.at(g - 1, "next_T"))
                        for k in range(GT):
                            for part in range(3):
                                m = pe.matmul(p5[:, k * 8:(k + 1) * 8], OT[:, k, :],
                                              dm3[:, bass.ds(c * Q + q, 1), part, :].rearrange("p o f -> p (o f)"),
                                              start=(part == 0), stop=(part == 2))
                        m.then_inc(TG.sem, 1)
                        pe.wait_ge(VG.sem, VG.at(g, "next_onehot"))
                        transposed_rows(g + 1).then_inc(TG.sem, 1)
                        pe.wait_ge(VG.sem, VG.at(g, "parts"))
                        for k in range(GT):
                            m = pe.matmul(p6[:, q * 3 * VW:(q + 1) * 3 * VW], og(g)[:, k, :],
                                          V3[:, k, :, :].rearrange("p s f -> p (s f)"), start=False, stop=False,
                                          skip_group_check=True)
                        m.then_inc(TG.sem, 1)
                for s in range(3):
                    up(s)
                    down(s)
                pe.wait_ge(AG.sem, AG.at(g1 - 1, "next_T"))
                pe.sem_inc(passed, 1)
                pe.wait_ge(V2.sem, V2.at(c, "xn"))
                turn(p4, flat(xn), T2)
                pe.wait_ge(A2.sem, A2.at(c, "xT"))
                pe.matmul(p5[:, :], w["a_Wqkv"][:, 0:P], xT[:, :], start=True, stop=True).then_inc(T2.sem, 1)
                pe.matmul(p4[:, :], w["a_Wqkv"][:, P:2 * P], xT[:, :], start=True, stop=True).then_inc(T2.sem, 1)
                pe.wait_ge(A2.sem, A2.at(c, "qT"))
                for q in qs:
                    pe.matmul(p5[:, q * P:(q + 1) * P], xT[:, q * P:(q + 1) * P], w["a_Wqkv"][:, 2 * P:3 * P], start=True, stop=False)
                    m = rows_bias(p5, q, w["a_bv"][:, :])
                m.then_inc(T2.sem, 1)
                pe.wait_ge(V2.sem, V2.at(c, "mask"))
                turn(p6, bufC, T2)
                for q in qs:
                    pe.wait_ge(V2.sem, V2.at(c, f"keys{q}"))
                    for h in range(2):
                        m = pe.matmul(pS[:, 4 * h:4 * h + 4, :], bufA[:, q * P:(q + 1) * P], big1[:, 4 * h:4 * h + 4, :],
                                      start=True, stop=True)
                    m.then_inc(T2.sem, 1)
                    up(3 + q)
                    pe.wait_ge(A2.sem, A2.at(c, f"exp{q}"))
                    for h in range(H1):
                        m = pe.transpose(pS[:, h, :], big2[:, h, :], ident[:, :])
                    m.then_inc(T2.sem, 1)
                    down(3 + q)
                    pe.wait_ge(A2.sem, A2.at(c, f"PT{q}"))
                    if q > 0:
                        pe.wait_ge(V2.sem, V2.at(c, f"ctx{q - 1}"))
                    for h in range(H1):
                        m = pe.matmul(p5[:, h * 17:(h + 1) * 17], big3[:, h, :], vext[:, q, h, :], start=True, stop=True)
                    m.then_inc(T2.sem, 1)
                pe.wait_ge(V2.sem, V2.at(c, f"ctx{Q - 1}"))
                turn(p4, bufC, T2)
                pe.wait_ge(A2.sem, A2.at(c, "ctxT"))
                for q in qs:
                    pe.matmul(p5[:, q * P:(q + 1) * P], bufA[:, q * P:(q + 1) * P], w["a_Wo"][:, :], start=True, stop=False)
                    m = rows_bias(p5, q, w["a_bo"][:, :])
                m.then_inc(T2.sem, 1)
                up(7)
                down(7)
                pe.wait_ge(V2.sem, V2.at(c, "y1"))
                turn(p4, bufD, T2)
                pe.wait_ge(A2.sem, A2.at(c, "y1T"))
                for f in range(FC):
                    if f >= 2:
                        pe.wait_ge(A2.sem, A2.at(c, f"relu{f - 2}"))
                    pe.matmul(pS[:, 4 * (f % 2):4 * (f % 2) + 4, :], w["a_W1"][:, f, :], xT[:, :], start=True, stop=True).then_inc(T2.sem, 1)
                pe.wait_ge(A2.sem, A2.at(c, f"relu{FC - 1}"))
                for q in qs:
                    for f in range(FC):
                        pe.matmul(p5[:, q * P:(q + 1) * P], ffh[f][:, q * P:(q + 1) * P], w["a_W2"][:, f, :], start=(f == 0), stop=False)
                    m = rows_bias(p5, q, w["a_c2"][:, :])
                m.then_inc(T2.sem, 1)
                up(8)
                pe.wait_ge(V2.sem, V2.at(c, "xn3"))
                turn(p4, flat(xn), T2)
                pe.wait_ge(A2.sem, A2.at(c, "xT3"))
                for q in qs:
                    m = pe.matmul(p5[:, q * E1:(q + 1) * E1], xTb[:, q * P:(q + 1) * P], w["m_Wr"][:, :], start=True, stop=True)
                m.then_inc(T2.sem, 1)
                down(8)
                pe.wait_ge(V2.sem, V2.at(c, "gate"))
                for q in qs:
                    m = pe.transpose(p4[0:E1 + 1, q * P:(q + 1) * P], mixw[:, q, :], ident[:, :])
                m.then_inc(T2.sem, 1)

            front(0, lambda s: None, lambda s: None)
            with pe.Fori(1, NCH) as c:
                front(c, lambda s: up(c - 1, s), lambda s: down(c - 1, s))
            pe.wait_ge(A2.sem, A2.at(NCH - 1, "mixT"))
            for s in range(E1 + 1):
                up(NCH - 1, s)
                down(NCH - 1, s)

        @block.vector
        def _(vec):
            def cols(t):
                return t[:, :].rearrange("p (q f) -> p q f", q=Q)

            setup, c1, c2, cg, cm = (Chain(x, per) for x, per in ((setup_chain, 0), (chain1, CH1), (chain2, CH2), (chaing, 5), (chainm, 0)))
            cb = Chain(chainb, E1 * (Q - 1))
            vec.wait_ge(consts, 17)

            def do(chain, ins, bare=False):
                chain.count(ins)
                chain.wait(vec)
                if bare:
                    vec.sem_inc(passed, 1)

            def sig(steps, i, name, ins, bare=False):
                ins.then_inc(steps.sem, 1)
                vec.wait_ge(steps.sem, steps.at(i, name))
                if bare:
                    vec.sem_inc(passed, 1)

            NT = NE // P
            xi = X[:, :, :].bitcast(I32).rearrange("p b f -> p (b f)")
            xf = X[:, :, :].rearrange("p b f -> p (b f)")
            vec.wait_ge(edges_in, 16)
            do(setup, vec.tensor_single_scalar(xi[:, NT:2 * NT], xi[:, 0:NT], 10, op=ALU.arith_shift_right))
            do(setup, vec.tensor_copy(xf[:, 2 * NT:3 * NT], xi[:, NT:2 * NT]))
            do(setup, vec.tensor_single_scalar(xi[:, NT:2 * NT], xi[:, 0:NT], 7, op=ALU.arith_shift_right))
            do(setup, vec.tensor_single_scalar(xi[:, NT:2 * NT], xi[:, NT:2 * NT], LO - 1, op=ALU.bitwise_and))
            do(setup, vec.tensor_copy(xf[:, 3 * NT:4 * NT], xi[:, NT:2 * NT]))
            with vec.Fori(0, NT // CT // 2) as i:
                for o in range(2):
                    vec.wait_ge(counted, 2 * i + o + 1)
                    for row, n, at in ((hi1, HI, 2 * NT), (lo1, LO, 3 * NT)):
                        m = vec.tensor_tensor(row[:, o, :].rearrange("p (t n) -> p t n", n=n), iota[:, 0:n].unsqueeze(1).broadcast_to([P, CT, n]),
                                              xf[:, bass.ds(at + (2 * i + o) * CT, CT)].unsqueeze(2).broadcast_to([P, CT, n]), ALU.is_equal)
                    m.then_inc(counted_onehot, 1)
            vec.wait_ge(counted, 2 + NT // CT)
            do(setup, vec.tensor_copy(small[:, 0:ST * LO], p7[:, 0:ST * LO]))
            vec.tensor_tensor(big1[:, :, :].rearrange("p k (a b) -> p k a b", a=HI),
                              ident[:, :].rearrange("p (k a) -> p k a", k=ST).unsqueeze(3).broadcast_to([P, ST, HI, LO]),
                              small[:, 0:ST * LO].rearrange("p (k b) -> p k b", k=ST).unsqueeze(2).broadcast_to([P, ST, HI, LO]),
                              ALU.mult).then_inc(counted_onehot, 1)
            vec.wait_ge(counted, 3 + NT // CT)
            cnt = yb[:, :, :, :].rearrange("p q e f -> p (q e) f")[:, 0:ST, 0:NB]
            do(setup, vec.tensor_copy(cnt, pS[:, :, 0:NB]))
            do(setup, vec.tensor_reduce(tot[:, :], cnt.rearrange("p k b -> p b k"), AX, ALU.add))
            do(setup, vec.tensor_scalar(toti[:, 0:NB], tot[:, :], float(GE - 1), None, op0=ALU.add))
            do(setup, vec.tensor_single_scalar(toti[:, 0:NB], toti[:, 0:NB], GE.bit_length() - 1, op=ALU.arith_shift_right))
            do(setup, vec.tensor_copy(tot[:, :], toti[:, 0:NB]))
            do(setup, vec.tensor_scalar(tot[:, :], tot[:, :], 1.0, None, op0=ALU.max))
            do(setup, vec.memset(starts[:, 0:1], 0.0))
            do(setup, vec.tensor_tensor_scan(starts[:, 1:NB + 1], tot[:, :], zero[:, 0:NB], 0.0, ALU.add, ALU.add))
            do(setup, vec.tensor_copy(gstart[0:1, 0:NB + 1], starts[0:1, :]))
            do(setup, vec.tensor_scalar(toti[0:1, 0:1], starts[0:1, NB:NB + 1], 4.0, None, op0=ALU.add))
            do(setup, vec.tensor_single_scalar(gstart[0:1, NB + 1:NB + 2], toti[0:1, 0:1], 2, op=ALU.arith_shift_right))
            do(setup, vec.tensor_scalar(big1[:, 0, 0:NB], starts[:, 0:NB], float(GE), None, op0=ALU.mult))
            for k in range(1, ST):
                do(setup, vec.tensor_tensor(big1[:, k, 0:NB], big1[:, k - 1, 0:NB], cnt[:, k - 1, :], ALU.add))
            do(setup, vec.memset(gmx[:, :], -3e38))
            vec.memset(sm[:, 12:13], 0.0).then_inc(V1.sem, V1.n)
            vec.memset(sm[:, 13:14], 0.0).then_inc(bases_ready, 1)

            def inv_sqrt(chain, var, n=Q):
                v, y, t = nb_[:, 0:n, 0], nb_[:, 0:n, 1], nb_[:, 0:n, 2]
                do(chain, vec.tensor_scalar(v, var, EPS, None, op0=ALU.add))
                do(chain, vec.tensor_single_scalar(nbi[:, 0:n], nb_[:, 0:n, 0].bitcast(I32), 1, op=ALU.arith_shift_right))
                do(chain, vec.tensor_scalar(y.bitcast(I32), nbi[:, 0:n], -1.0, float(0x5F3759DF), op0=ALU.mult, op1=ALU.add))
                for r in range(4):
                    do(chain, vec.tensor_tensor(t, y, y, ALU.mult))
                    do(chain, vec.scalar_tensor_tensor(t, t, -0.5, v, ALU.mult, ALU.mult))
                    do(chain, vec.scalar_tensor_tensor(y if r < 3 else rstd[:, 0:n], t, 1.5, y, ALU.add, ALU.mult))

            def norm(chain, src, dst, last=None):
                for q in qs:
                    chain.count(vec.bn_stats(bst[:, q, :], src(q)))
                chain.wait(vec)
                vec.sem_inc(passed, 1)
                for q in qs:
                    chain.count(vec.bn_aggr(mv[:, q, :], bst[:, q, :]))
                chain.wait(vec)
                inv_sqrt(chain, mv[:, :, 1])
                for q in qs:
                    m = vec.tensor_scalar(dst(q), src(q), mv[:, q, 0:1], rstd[:, q:q + 1], op0=ALU.subtract, op1=ALU.mult)
                    if q < Q - 1:
                        chain.count(m)
                    elif last is None:
                        do(chain, m)
                    else:
                        sig(*last, m)

            def over(t, n):
                return t.unsqueeze(2)

            def stage1(c):
                xq = lambda q: X[:, bass.ds(c * Q + q, 1), :].rearrange("p o f -> p (o f)")
                xc = X[:, bass.ds(c * Q, Q), :]

                def w_xn():
                    vec.sem_inc(passed, 1)
                    norm(c1, xq, lambda q: xn[:, q, :], (V1, c, "xn"))

                def w_masked():
                    vec.wait_ge(T1.sem, T1.at(c, "logits"))
                    vec.wait_ge(A1.sem, A1.at(c, "ay"))
                    do(c1, vec.tensor_tensor(cols(bufC), cols(p5), sm[:, 0:Q].unsqueeze(2).broadcast_to([P, Q, P]), ALU.add))
                    do(c1, vec.scalar_tensor_tensor(bufC[:, :], bufC[:, :], 0.2, bufC[:, :], ALU.mult, ALU.max))
                    do(c1, vec.tensor_scalar(cols(bufD), adjc[:, :, :], 0.0, None, op0=ALU.is_gt))
                    do(c1, vec.tensor_tensor(bufC[:, :], bufC[:, :], bufD[:, :], ALU.mult))
                    do(c1, vec.tensor_scalar(bufD[:, :], bufD[:, :], NEG, -NEG, op0=ALU.mult, op1=ALU.add))
                    do(c1, vec.tensor_tensor(bufC[:, :], bufC[:, :], bufD[:, :], ALU.add))
                    do(c1, vec.tensor_reduce(sm[:, 4:8], cols(bufC), AX, ALU.max))
                    sig(V1, c, "masked", vec.tensor_tensor(cols(bufC), cols(bufC), sm[:, 4:8].unsqueeze(2).broadcast_to([P, Q, P]), ALU.subtract))

                def w_prob():
                    vec.wait_ge(A1.sem, A1.at(c, "exp"))
                    do(c1, vec.tensor_reduce(sm[:, 4:8], cols(bufC), AX, ALU.add))
                    do(c1, vec.reciprocal(sm[:, 8:12], sm[:, 4:8]))
                    sig(V1, c, "prob", vec.tensor_tensor(cols(bufC), cols(bufC), sm[:, 8:12].unsqueeze(2).broadcast_to([P, Q, P]), ALU.mult))

                def w_zmin():
                    vec.wait_ge(T1.sem, T1.at(c, "hout"))
                    sig(V1, c, "zmin", vec.tensor_scalar(bufC[:, :], p4[:, :], 0.0, None, op0=ALU.min))

                def w_x1():
                    vec.wait_ge(A1.sem, A1.at(c, "elu"))
                    do(c1, vec.scalar_tensor_tensor(bufC[:, :], p4[:, :], 0.0, bufC[:, :], ALU.max, ALU.add))
                    sig(V1, c, "x1", vec.scalar_tensor_tensor(xc, cols(bufC), -1.0, xc, ALU.add, ALU.add))

                def w_xn1():
                    vec.sem_inc(passed, 1)
                    norm(c1, xq, lambda q: xn[:, q, :], (V1, c, "xn1"))

                def w_pay():
                    vec.wait_ge(T1.sem, T1.at(c, "hrow"))
                    pc = pay[:, bass.ds(c * Q, Q), :]
                    h = p6[:, 0:Q * 16].rearrange("p (q h) -> p q h", q=Q)
                    h4 = p6[:, 0:Q * 16].rearrange("p (q h e) -> p q h e", q=Q, h=H0)
                    s3 = small[:, :].rearrange("p (q h) -> p q h", q=Q)
                    s4 = small[:, :].rearrange("p (q h e) -> p q h e", q=Q, h=H0)
                    do(c1, vec.tensor_copy(pc[:, :, H0:PW].rearrange("p q (h f) -> p q h f", h=H0)[:, :, :, 1:1 + E0], h4))
                    do(c1, vec.tensor_tensor(s3, h, w["f_asrc"][:, :].unsqueeze(1).broadcast_to([P, Q, H0 * E0]), ALU.mult), bare=True)
                    do(c1, vec.tensor_reduce(pc[:, :, 0:H0], s4, AX, ALU.add))
                    do(c1, vec.tensor_tensor(s3, h, w["f_adst"][:, :].unsqueeze(1).broadcast_to([P, Q, H0 * E0]), ALU.mult), bare=True)
                    do(c1, vec.tensor_reduce(dn[:, bass.ds(c * Q, Q), :], s4, AX, ALU.add), bare=True)
                    do(c1, vec.tensor_reduce(sm[:, 4:8], pc[:, :, 0:H0].rearrange("p q h -> p h q"), AX, ALU.max))
                    sig(V1, c, "pay", vec.tensor_tensor(gmx[:, :], gmx[:, :], sm[:, 4:8], ALU.max))

                return {0: w_xn, 5: w_masked, 6: w_prob, 9: w_zmin, 10: w_x1, 11: w_xn1, 13: w_pay}

            vec.wait_ge(x_in, 16)
            with vec.Fori(0, NCH) as c:
                c1.turn(c)
                vec.wait_ge(chunk_in, 48 * (c + 1))
                do(c1, vec.tensor_single_scalar(tmpi, dstc, 7, op=ALU.arith_shift_right))
                do(c1, vec.tensor_copy(dhi[:, :], tmpi))
                do(c1, vec.tensor_single_scalar(tmpi, dstc, P - 1, op=ALU.bitwise_and))
                do(c1, vec.tensor_copy(rec[:, :, 1].bitcast(F32), tmpi))
                do(c1, vec.tensor_scalar(rec[:, :, 0], srcc, float(M - 1), None, op0=ALU.min))
                do(c1, vec.tensor_scalar(far, dhi[:, :], NB - 0.5, SKIP, op0=ALU.is_gt, op1=ALU.mult))
                work = stage1(c)

                def onehot(g):
                    prev = T1.at(c, f"ranked{g - 2}") if g >= 2 else T1.at(c - 1, f"ranked{SG - 2 + g}")
                    vec.wait_ge(T1.sem, prev)
                    sig(V1, c, f"onehot{g}", vec.tensor_tensor(
                        O[:, g % 2, :, 0:NB], iota[:, 0:NB].unsqueeze(1).broadcast_to([P, ST, NB]),
                        dhi[:, g * ST:(g + 1) * ST].unsqueeze(2).broadcast_to([P, ST, NB]), ALU.is_equal))

                onehot(0)
                for g in range(SG):
                    vec.wait_ge(T1.sem, T1.at(c, f"rank{g}"))
                    sig(V1, c, f"prod{g}", vec.tensor_tensor(big1[:, :, 0:NB], pR[:, :, 0:NB], O[:, g % 2, :, 0:NB], ALU.mult))
                    do(c1, vec.tensor_reduce(pos[:, :], big1[:, :, 0:NB], AX, ALU.add))
                    vec.wait_ge(scattered[g % 2], FILLED + 128 * (c * (SG // 2) + g // 2))
                    do(c1, vec.tensor_tensor(idx[:, g % 2, :], pos[:, :], far[:, g * ST:(g + 1) * ST], ALU.add))
                    sig(V1, c, f"idx{g}", vec.tensor_copy(recs[:, g % 2, :, :], rec[:, g * ST:(g + 1) * ST, :]))
                    if g + 1 < SG:
                        onehot(g + 1)
                    if g in work:
                        work[g]()
                c1.end()

            vec.wait_ge(guard_ready, 1)
            vec.wait_ge(stores_done, NCH + 1)
            dm = yb[:, :, :, :].rearrange("p q e f -> p (q e f)")[:, 0:NB * 2 * H0].rearrange("p (b h) -> p b h", b=NB)
            guard = dm[:, :, H0:2 * H0]
            do(cm, vec.tensor_copy(dm[:, :, 0:H0], dn))
            do(cm, vec.tensor_tensor(guard, dn, gmall[:, :].unsqueeze(1).broadcast_to([P, NB, H0]), ALU.add))
            do(cm, vec.scalar_tensor_tensor(guard, guard, 0.2, guard, ALU.mult, ALU.max))
            do(cm, vec.tensor_scalar(guard, guard, -1.0, None, op0=ALU.mult))
            do(cm, vec.tensor_tensor(dn, dn, pay[:, :, 0:H0], ALU.add))
            do(cm, vec.scalar_tensor_tensor(dn, dn, 0.2, dn, ALU.mult, ALU.max))
            vec.tensor_tensor(dn, dn, guard, ALU.add).then_inc(tables_ready, 1)
            vec.wait_ge(tables_ready, 1)
            do(cm, vec.tensor_copy(dm3[:, :, 0, :], dm))
            do(cm, vec.tensor_tensor(dm, dm, dm3[:, :, 0, :], ALU.subtract))
            do(cm, vec.tensor_copy(dm3[:, :, 1, :], dm))
            do(cm, vec.tensor_tensor(dm3[:, :, 2, :], dm, dm3[:, :, 1, :], ALU.subtract))
            vec.wait_ge(guard_ready, 2)
            weighted = pay[:, :, H0:PW].rearrange("p b (h f) -> p b h f", h=H0)
            do(cm, vec.tensor_tensor(weighted, weighted, dn.unsqueeze(3).broadcast_to([P, NB, H0, 1 + E0]), ALU.mult))
            do(cm, vec.memset(mixw[:, :, :], 1.0))
            for k, steps in enumerate((V2, VB)):
                vec.memset(sm[:, 12 + k:13 + k], 0.0).then_inc(steps.sem, steps.n)
            vec.memset(small2[:, 0:1], 0.0).then_inc(ring_freed, RING)

            def onehot_rows(g):
                dst = ring_dst[:, bass.ds(g % RING, 1), :, :].rearrange("p o k w -> p (o k) w").bitcast(F32)[:, :, 1:2]
                return vec.tensor_tensor(Og[:, bass.ds(g % 2, 1), :, :].rearrange("p o k e -> p (o k) e"),
                                         iota[:, :].unsqueeze(1).broadcast_to([P, GT, P]), dst.broadcast_to([P, GT, P]), ALU.is_equal)

            vec.wait_ge(ring_filled, 1)
            onehot_rows(0).then_inc(VG.sem, VG.n)

            def top2(v, n, sel):
                a, b = cmp1[:, :, 0:n, 0:n], cmp2[:, :, 0:n, 0:n]
                other, own = v.unsqueeze(2).broadcast_to([P, Q, n, n]), v.unsqueeze(3).broadcast_to([P, Q, n, n])
                do(c2, vec.tensor_tensor(a, other, own, ALU.is_gt))
                do(c2, vec.tensor_tensor(b, other, own, ALU.is_equal))
                do(c2, vec.tensor_tensor(b, b, lower[:, 0:n, 0:n].unsqueeze(1).broadcast_to([P, Q, n, n]), ALU.mult))
                do(c2, vec.tensor_tensor(a, a, b, ALU.add))
                do(c2, vec.tensor_reduce(sel, a, AX, ALU.add))
                do(c2, vec.tensor_scalar(sel, sel, 1.5, None, op0=ALU.is_lt))

            def per_q(t):
                return t.unsqueeze(2)

            def back(c, s):
                cb.turn(c)
                cb.n = s * (Q - 1)
                e = order[s]
                xq = lambda q: X[:, bass.ds(c * Q + q, 1), :].rearrange("p o f -> p (o f)")
                xc = X[:, bass.ds(c * Q, Q), :]
                vec.wait_ge(TB.sem, TB.at(c, f"down{e}"))
                if e == 0:
                    sig(VB, c, "mix0", vec.tensor_tensor(xc, cols(p7), xc, ALU.add))
                    return
                for q in qs:
                    m = vec.scalar_tensor_tensor(xq(q), p7[:, q * P:(q + 1) * P], mixw[:, q, e:e + 1], xq(q), ALU.mult, ALU.add)
                    if q < Q - 1:
                        cb.count(m)
                    else:
                        sig(VB, c, f"mix{e}", m)

            def front(c, behind):
                c2.turn(c)
                xq = lambda q: X[:, bass.ds(c * Q + q, 1), :].rearrange("p o f -> p (o f)")
                xc = X[:, bass.ds(c * Q, Q), :]
                for q in qs:
                    g0 = vec.value_load(gstart[0:1, bass.ds(c * Q + q, 1)], min_val=0, max_val=CAP // GE)
                    g1 = vec.value_load(gstart[0:1, bass.ds(c * Q + q + 1, 1)], min_val=1, max_val=CAP // GE)
                    with vec.Fori(g0, g1) as g:
                        cg.turn(g)
                        rows = ring[:, bass.ds(g % RING, 1), :, :].rearrange("p o k f -> p (o k) f")
                        vec.wait_ge(TG.sem, TG.at(g, "dstscore"))
                        d8 = p5[:, 0:GT * 8].rearrange("p (k f) -> p k f", k=GT)
                        do(cg, vec.tensor_tensor(zg[:, :, :], rows[:, :, 0:H0], d8[:, :, 0:H0], ALU.add))
                        do(cg, vec.scalar_tensor_tensor(zg[:, :, :], zg[:, :, :], 0.2, zg[:, :, :], ALU.mult, ALU.max))
                        sig(VG, g, "z", vec.tensor_tensor(zg[:, :, :], zg[:, :, :], d8[:, :, H0:2 * H0], ALU.add))
                        vec.wait_ge(ring_filled, g + 2)
                        vec.wait_ge(TG.sem, TG.at(g - 1, "sums"))
                        onehot_rows(g + 1).then_inc(VG.sem, 1)
                        vec.wait_ge(AG.sem, AG.at(g, "exp"))
                        vec.tensor_tensor(Vg[:, :, :].rearrange("p k (h f) -> p k h f", h=H0),
                                          rows[:, :, H0:PW].rearrange("p k (h f) -> p k h f", h=H0),
                                          eg[:, :, :].unsqueeze(3).broadcast_to([P, GT, H0, 1 + E0]), ALU.mult).then_inc(ring_freed, 1)
                        vec.wait_ge(ring_freed, g + RING + 1)
                        do(cg, vec.tensor_copy(V3[:, :, 0, :], Vg[:, :, :]))
                        do(cg, vec.tensor_tensor(Vg[:, :, :], Vg[:, :, :], V3[:, :, 0, :], ALU.subtract))
                        do(cg, vec.tensor_copy(V3[:, :, 1, :], Vg[:, :, :]))
                        vec.tensor_tensor(V3[:, :, 2, :], Vg[:, :, :], V3[:, :, 1, :], ALU.subtract).then_inc(VG.sem, 1)
                        cg.end()
                vec.wait_ge(TG.sem, TG.at(g1 - 1, "sums"))
                sig(V2, c, "agg", vec.tensor_reduce(agg[:, :, :], p6[:, 0:Q * 3 * VW].rearrange("p (q s f) -> p q f s", q=Q, s=3), AX, ALU.add))
                do(c2, vec.tensor_tensor(agg[:, :, :], agg[:, :, :], pay[:, bass.ds(c * Q, Q), H0:PW], ALU.add))
                a5 = agg[:, :, :].rearrange("p q (h f) -> p q h f", h=H0)
                s3 = small[:, :].rearrange("p (q h) -> p q h", q=Q)
                t3 = small2[:, :].rearrange("p (q h) -> p q h", q=Q)
                s4 = small[:, :].rearrange("p (q h e) -> p q h e", q=Q, h=H0)
                den = sm[:, 0:16].rearrange("p (q h) -> p q h", q=Q)
                do(c2, vec.tensor_scalar(den, a5[:, :, :, 0], 1e-16, None, op0=ALU.add))
                do(c2, vec.reciprocal(den, den))
                do(c2, vec.tensor_tensor(s4, a5[:, :, :, 1:1 + E0], den.unsqueeze(3).broadcast_to([P, Q, H0, E0]), ALU.mult))
                do(c2, vec.tensor_tensor(s3, s3, w["f_bgat"][:, :].unsqueeze(1).broadcast_to([P, Q, 16]), ALU.add))
                do(c2, vec.tensor_reduce(sm[:, 0:Q], s3, AX, ALU.add))
                do(c2, vec.tensor_scalar(sm[:, 0:Q], sm[:, 0:Q], 1.0 / 16, None, op0=ALU.mult))
                do(c2, vec.tensor_tensor(s3, s3, sm[:, 0:Q].unsqueeze(2).broadcast_to([P, Q, 16]), ALU.subtract))
                do(c2, vec.tensor_tensor(t3, s3, s3, ALU.mult))
                do(c2, vec.tensor_reduce(sm[:, 0:Q], t3, AX, ALU.add))
                do(c2, vec.tensor_scalar(sm[:, 0:Q], sm[:, 0:Q], 1.0 / 16, None, op0=ALU.mult))
                inv_sqrt(c2, sm[:, 0:Q])
                do(c2, vec.tensor_tensor(s3, s3, rstd[:, :].unsqueeze(2).broadcast_to([P, Q, 16]), ALU.mult))
                do(c2, vec.tensor_tensor(s3, s3, w["f_gam"][:, :].unsqueeze(1).broadcast_to([P, Q, 16]), ALU.mult))
                do(c2, vec.tensor_tensor(s3, s3, w["f_bet"][:, :].unsqueeze(1).broadcast_to([P, Q, 16]), ALU.add))
                scr, sel4 = gates[:, :, 0:E0], gates[:, :, E0:2 * E0]
                do(c2, vec.tensor_reduce(scr, small[:, :].rearrange("p (q h e) -> p q e h", q=Q, h=H0), AX, ALU.add))
                do(c2, vec.tensor_scalar(scr, scr, 1.0 / H0, None, op0=ALU.mult))
                top2(scr, E0, sel4)
                do(c2, vec.tensor_reduce(sm[:, 0:Q], scr, AX, ALU.max))
                ex0 = small[:, 0:Q * E0].rearrange("p (q e) -> p q e", q=Q)
                g0_ = small2[:, 0:Q * E0].rearrange("p (q e) -> p q e", q=Q)
                sig(V2, c, "gexp0", vec.tensor_tensor(ex0, scr, sm[:, 0:Q].unsqueeze(2).broadcast_to([P, Q, E0]), ALU.subtract))
                behind(0)
                vec.wait_ge(A2.sem, A2.at(c, "gate0"))
                do(c2, vec.tensor_tensor(g0_, g0_, sel4, ALU.mult))
                do(c2, vec.tensor_reduce(sm[:, 0:Q], g0_, AX, ALU.add))
                do(c2, vec.reciprocal(sm[:, 4:8], sm[:, 0:Q]))
                do(c2, vec.tensor_tensor(mix0[:, :, :], g0_, sm[:, 4:8].unsqueeze(2).broadcast_to([P, Q, E0]), ALU.mult))
                vec.wait_ge(y_in, 16 * (c + 1))
                for e in range(E0):
                    for q in qs:
                        m = vec.scalar_tensor_tensor(xq(q), yb[:, q, e, :], mix0[:, q, e:e + 1], xq(q), ALU.mult, ALU.add)
                        if q < Q - 1:
                            c2.count(m)
                        elif e < E0 - 1:
                            do(c2, m)
                        else:
                            sig(V2, c, "x2", m, bare=True)
                norm(c2, xq, lambda q: xn[:, q, :], (V2, c, "xn"))
                behind(1)
                vec.wait_ge(adj_in, 16 * (c + 1))
                sig(V2, c, "mask", vec.tensor_scalar(cols(bufC), adjc[:, :, :], 0.0, None, op0=ALU.is_gt))
                vec.wait_ge(T2.sem, T2.at(c, "maskT"))
                do(c2, vec.tensor_tensor(neg[:, :, :], cols(p6), cols(bufC), ALU.max))
                do(c2, vec.tensor_tensor(neg[:, :, :], neg[:, :, :], ident[:, :].unsqueeze(1).broadcast_to([P, Q, P]), ALU.max))
                sig(V2, c, "allowed", vec.tensor_scalar(neg[:, :, :], neg[:, :, :], FAR, -FAR, op0=ALU.mult, op1=ALU.add))
                behind(2)

                def keys(q):
                    sig(V2, c, f"keys{q}", vec.tensor_tensor(big1[:, :, :], bufB[:, q * P:(q + 1) * P].unsqueeze(1).broadcast_to([P, H1, P]),
                                                            headmask[:, :].unsqueeze(2).broadcast_to([P, H1, P]), ALU.mult))

                vec.wait_ge(A2.sem, A2.at(c, "kT"))
                keys(0)
                for q in qs:
                    vec.wait_ge(T2.sem, T2.at(c, f"scores{q}"))
                    do(c2, vec.tensor_tensor(big2[:, :, :], pS[:, :, :], neg[:, q:q + 1, :].broadcast_to([P, H1, P]), ALU.add))
                    do(c2, vec.tensor_reduce(mxh[:, :], big2[:, :, :], AX, ALU.max))
                    sig(V2, c, f"max{q}", vec.tensor_tensor(big2[:, :, :], big2[:, :, :], mxh[:, :].unsqueeze(2).broadcast_to([P, H1, P]), ALU.subtract))
                    if q < Q - 1:
                        keys(q + 1)
                    vec.wait_ge(T2.sem, T2.at(c, f"ctx{q}"))
                    cx = p5[:, 0:H1 * 17].rearrange("p (h f) -> p h f", h=H1)
                    do(c2, vec.reciprocal(cden[:, :], cx[:, :, HD]))
                    sig(V2, c, f"ctx{q}", vec.tensor_tensor(bufC[:, q * P:(q + 1) * P].rearrange("p (h f) -> p h f", h=H1), cx[:, :, 0:HD],
                                                           cden[:, :].unsqueeze(2).broadcast_to([P, H1, HD]), ALU.mult))
                    behind(3 + q)
                vec.wait_ge(T2.sem, T2.at(c, "attn"))
                bq = lambda t: (lambda q: t[:, q * P:(q + 1) * P])
                do(c2, vec.tensor_tensor(bufD[:, :], p5[:, :], xn[:, :, :].rearrange("p q f -> p (q f)"), ALU.add))
                norm(c2, bq(bufD), bq(bufD))
                do(c2, vec.tensor_tensor(cols(bufD), cols(bufD), w["a_g1"][:, :].unsqueeze(1).broadcast_to([P, Q, P]), ALU.mult))
                sig(V2, c, "y1", vec.tensor_tensor(cols(bufD), cols(bufD), w["a_b1"][:, :].unsqueeze(1).broadcast_to([P, Q, P]), ALU.add))
                behind(7)
                vec.wait_ge(T2.sem, T2.at(c, "ff"))
                do(c2, vec.tensor_tensor(bufC[:, :], p5[:, :], bufD[:, :], ALU.add))
                norm(c2, bq(bufC), bq(bufC))
                do(c2, vec.tensor_tensor(cols(bufC), cols(bufC), w["a_g2"][:, :].unsqueeze(1).broadcast_to([P, Q, P]), ALU.mult))
                do(c2, vec.tensor_tensor(cols(bufC), cols(bufC), w["a_b2"][:, :].unsqueeze(1).broadcast_to([P, Q, P]), ALU.add))
                do(c2, vec.tensor_tensor(xc, cols(bufC), xc, ALU.add), bare=True)
                norm(c2, xq, lambda q: xn[:, q, :], (V2, c, "xn3"))
                vec.wait_ge(T2.sem, T2.at(c, "router"))
                lg = p5[:, 0:Q * E1].rearrange("p (q e) -> p q e", q=Q)
                do(c2, vec.tensor_reduce(sm[:, 0:Q], lg, AX, ALU.max))
                sig(V2, c, "gexp", vec.tensor_tensor(gates[:, :, :], lg, sm[:, 0:Q].unsqueeze(2).broadcast_to([P, Q, E1]), ALU.subtract))
                vec.wait_ge(A2.sem, A2.at(c, "rexp"))
                do(c2, vec.tensor_reduce(sm[:, 0:Q], gates[:, :, :], AX, ALU.add))
                do(c2, vec.reciprocal(sm[:, 4:8], sm[:, 0:Q]))
                do(c2, vec.tensor_tensor(gates[:, :, :], gates[:, :, :], sm[:, 4:8].unsqueeze(2).broadcast_to([P, Q, E1]), ALU.mult))
                sel8 = small[:, 0:Q * E1].rearrange("p (q e) -> p q e", q=Q)
                top2(gates[:, :, :], E1, sel8)
                do(c2, vec.tensor_tensor(gates[:, :, :], gates[:, :, :], sel8, ALU.mult))
                do(c2, vec.tensor_reduce(sm[:, 0:Q], gates[:, :, :], AX, ALU.add))
                do(c2, vec.reciprocal(sm[:, 4:8], sm[:, 0:Q]))
                sig(V2, c, "gate", vec.tensor_tensor(mixw[:, :, 1:1 + E1], gates[:, :, :], sm[:, 4:8].unsqueeze(2).broadcast_to([P, Q, E1]), ALU.mult))
                behind(8)
                c2.end()

            front(0, lambda s: None)
            with vec.Fori(1, NCH) as c:
                front(c, lambda s: back(c - 1, s))
            for s in range(E1 + 1):
                back(NCH - 1, s)


_OUT = ((128, 128, 128), "float32")


def laid_out(i):
    c = np.ascontiguousarray
    rep = lambda v: c(np.broadcast_to(np.asarray(v).reshape(1, -1), (P, np.asarray(v).size)))
    row = lambda v: c(np.asarray(v).reshape(1, -1))
    col = lambda v: c(np.asarray(v).reshape(-1, P).T)
    n = {k: np.asarray(v) for k, v in i.items()}
    m1 = np.concatenate([n["L1_ffn_W1s"][None], n["L1_ffn_W1p"]])
    m2 = np.concatenate([n["L1_ffn_W2s"][None], n["L1_ffn_W2p"]])
    b1 = np.concatenate([n["L1_ffn_b1s"][None], n["L1_ffn_b1p"]])
    b2 = np.concatenate([n["L1_ffn_b2s"][None], n["L1_ffn_b2p"]])
    return {
        "x": c(n["x"]), "adj": c(n["adj"]), "edges": c(n["L0_ffn_edge_index"]),
        "g_W": c(n["L0_gnn_W"]), "g_a12": c(n["L0_gnn_a_12"]), "g_W1": c(n["L0_gnn_W_1"]), "g_W2": c(n["L0_gnn_W_2"]),
        "g_a1": c(n["L0_gnn_a_1"]), "g_a2": c(n["L0_gnn_a_2"]),
        "f_Wgat": c(n["L0_ffn_W_gat"]), "f_asrc": rep(n["L0_ffn_att_src"]), "f_adst": rep(n["L0_ffn_att_dst"]),
        "f_bgat": rep(n["L0_ffn_b_gat"]), "f_gam": rep(n["L0_ffn_ln_gamma"]), "f_bet": rep(n["L0_ffn_ln_beta"]),
        "f_W1": c(n["L0_ffn_W1"].reshape(E0, P, 2, P).transpose(1, 0, 2, 3)),
        "f_b1": c(n["L0_ffn_b1"].reshape(E0, 2, P).transpose(2, 0, 1)),
        "f_W2": c(n["L0_ffn_W2"].reshape(E0, 2, P, P).transpose(2, 0, 1, 3)), "f_b2": row(n["L0_ffn_b2"]),
        "a_Wqkv": c(n["L1_gnn_Wqkv"].T), "a_bqk": col(n["L1_gnn_bqkv"][:2 * P]), "a_bv": row(n["L1_gnn_bqkv"][2 * P:]),
        "a_Wo": c(n["L1_gnn_Wo"].T), "a_bo": row(n["L1_gnn_bo"]),
        "a_g1": rep(n["L1_gnn_ln1_g"]), "a_b1": rep(n["L1_gnn_ln1_b"]), "a_g2": rep(n["L1_gnn_ln2_g"]), "a_b2": rep(n["L1_gnn_ln2_b"]),
        "a_W1": c(n["L1_gnn_W1"].T.reshape(P, FC, P)), "a_c1": col(n["L1_gnn_b1"]),
        "a_W2": c(n["L1_gnn_W2"].T.reshape(FC, P, P).transpose(1, 0, 2)), "a_c2": row(n["L1_gnn_b2"]),
        "m_Wr": c(n["L1_ffn_Wr"]), "m_W1": c(m1.reshape(E1 + 1, P, FC, P).transpose(1, 0, 2, 3)),
        "m_b1": c(b1.reshape(E1 + 1, FC, P).transpose(2, 0, 1)),
        "m_W2": c(m2.reshape(E1 + 1, FC, P, P).transpose(2, 0, 1, 3)), "m_b2": c(b2),
    }


def kernel(**inputs):
    import concourse.bacc as bacc
    from concourse.bass_utils import run_bass_kernel_spmd

    nc = bacc.Bacc("TRN2", target_bir_lowering=False, num_devices=1)
    arrays, aps = {}, {}
    for name, v in laid_out(inputs).items():
        arrays[f"in_{name}"] = v
        aps[name] = nc.dram_tensor(f"in_{name}", v.shape, mybir.dt.from_np(v.dtype), kind="ExternalInput").ap()
    aps["out"] = nc.dram_tensor("out_x", _OUT[0], F32, kind="ExternalOutput").ap()
    program(nc, aps, NB=arrays["in_x"].shape[0], NE=arrays["in_edges"].shape[1])
    r = run_bass_kernel_spmd(nc, [arrays], core_ids=[0])
    return r.results[0]["out_x"]
```

```python
from contextlib import ExitStack

import numpy as np
import concourse.bass as bass
from concourse import mybir
from concourse.alu_op_type import AluOpType as ALU

ACT = mybir.ActivationFunctionType
AX = mybir.AxisListType.X
F32 = mybir.dt.float32
BF16 = mybir.dt.bfloat16
I32 = mybir.dt.int32
U32 = mybir.dt.uint32

P = 128
Q = 4
T = Q * P
GT = 9
GE = GT * P
ST = 8
NINTH = 16
RING = 10
H0, E0 = 4, 4
VW = H0 * (1 + E0)
PW = H0 + VW
H1 = 8
HD = P // H1
E1 = 8
FC = 4
EPS = 1e-5
NEG = 9e15
FAR = 1e30
HI, LO = 16, 8
CT = 64
SKIP = float(2**23)


PER = (100, 179)


class Steps:

    def __init__(self, sem, names):
        self.sem, self.names, self.n = sem, {s: k + 1 for k, s in enumerate(names)}, len(names)
        assert len(self.names) == len(names)

    def at(self, i, name):
        return (i + 1) * self.n + self.names[name]


class Chain:

    def __init__(self, sem, per):
        self.sem, self.per, self.n, self.i = sem, per, 0, 0

    def turn(self, i):
        self.i, self.n = i, 0

    def count(self, ins):
        self.n += 1
        ins.then_inc(self.sem, 1)

    def wait(self, eng):
        eng.wait_ge(self.sem, self.i * self.per + self.n)

    def end(self):
        assert self.n == self.per, (self.n, self.per)


def program(nc, a, NB, NE):
    NCH = NB // Q
    M = NB * P
    CE = NE // P // NCH
    SG = CE // ST
    assert SG * ST == CE and SG % 2 == 0
    FR = P * P * 4
    FILLS = 2 * -(-(NE + (2 * NB + 8) * GE) // (2 * FR))
    CAP = FILLS * FR
    TURNS = (NE // GE + 2 * NB + 4) // 2
    FILLED = 16 * FILLS // 2
    sorted_edges = nc.dram_tensor("sorted_edges", (CAP, 2), U32, kind="Internal").ap()
    node_rows = nc.dram_tensor("node_rows", (M, PW), F32, kind="Internal").ap()
    expert_rows = nc.dram_tensor("expert_rows", (M, E0, P), F32, kind="Internal").ap()

    with ExitStack() as ctx:
        def sb(name, shape, dt=F32):
            return ctx.enter_context(nc.sbuf_tensor(name, shape, dt))

        def psum(name, shape, dt=F32):
            return ctx.enter_context(nc.psum_tensor(name, shape, dt))

        def sem(name):
            return ctx.enter_context(nc.semaphore(name))

        X = sb("X", [P, NB, P])
        pay = sb("pay", [P, NB, PW])
        dnf = sb("dn", [P, max(NB * H0, T)])
        dn = dnf[:, 0:NB * H0].rearrange("p (b h) -> p b h", h=H0)
        mixT = dnf[0:E1 + 1, 0:T]
        dm3 = sb("dm3", [P, NB, 3, 2 * H0], BF16)
        Og = sb("Og", [P, 3, GT, P], BF16)
        ring = sb("ring", [P, RING, GT, PW])
        ringf = ring[:, :, :, :].rearrange("p r k f -> p (r k f)")
        ogf = Og[:, :, :, :].bitcast(F32).rearrange("p o k e -> p (o k e)")
        place = {"f_W1": ringf[:, 0:1024].rearrange("p (e f m) -> p e f m", e=E0, f=2),
                 "f_W2": ringf[:, 1024:2048].rearrange("p (e f m) -> p e f m", e=E0, f=2),
                 "g_W": ogf[:, 0:P], "g_a12": ogf[:, P:2 * P], "g_W1": ogf[:, 2 * P:3 * P], "g_W2": ogf[:, 3 * P:4 * P],
                 "f_b2": ogf[0:1, 4 * P:(4 + E0) * P]}
        w = {}
        wl = []
        for name, shape in (
            ("g_W", [P, P]), ("g_a12", [P, P]), ("g_W1", [P, P]), ("g_W2", [P, P]), ("g_a1", [P, 1]), ("g_a2", [P, 1]),
            ("f_Wgat", [P, H0 * E0]), ("f_asrc", [P, H0 * E0]), ("f_adst", [P, H0 * E0]), ("f_bgat", [P, H0 * E0]),
            ("f_gam", [P, H0 * E0]), ("f_bet", [P, H0 * E0]),
            ("f_W1", [P, E0, 2, P]), ("f_b1", [P, E0, 2]), ("f_W2", [P, E0, 2, P]), ("f_b2", [1, E0 * P]),
            ("a_Wqkv", [P, 3 * P]), ("a_bqk", [P, 2]), ("a_bv", [P, P]), ("a_Wo", [P, P]), ("a_bo", [P, P]),
            ("a_g1", [P, P]), ("a_b1", [P, P]), ("a_g2", [P, P]), ("a_b2", [P, P]),
            ("a_W1", [P, FC, P]), ("a_c1", [P, FC]), ("a_W2", [P, FC, P]), ("a_c2", [P, P]),
            ("m_Wr", [P, E1]), ("m_W1", [P, E1 + 1, FC, P]), ("m_b1", [P, E1 + 1, FC]),
            ("m_W2", [P, E1 + 1, FC, P]), ("m_b2", [E1 + 1, P]),
        ):
            w[name] = place.get(name)
            if w[name] is None:
                w[name] = sb(name, shape)[tuple(slice(None) for _ in shape)]
            wl.append((w[name], a[name]))

        ident = sb("ident", [P, P])
        identb = sb("identb", [P, P], BF16)
        iota = sb("iota", [P, P], BF16)
        before = sb("before", [P, P], BF16)
        notbefore = sb("notbefore", [P, P], BF16)
        onesb = sb("onesb", [P, P], BF16)
        zerob = sb("zerob", [P, ST * LO], BF16)
        zero = sb("zero", [P, P])
        ones1 = sb("ones1", [1, P])
        headmask = sb("headmask", [P, H1])
        lower = sb("lower", [P, E1, E1])

        adjc = sb("adjc", [P, Q, P], I32)
        words = sb("words", [P, max(4 * CE, GT * P // 2)])
        assert CE == P
        srcc, dstc, tmpi = (words[:, k * CE:(k + 1) * CE].bitcast(I32) for k in range(3))
        far = words[:, 3 * CE:4 * CE]
        dhi = sb("dhi", [P, CE], BF16)
        parts = sb("parts", [P, max(2 * CE, GT * 3 * VW // 2)])
        rec = parts[:, 0:2 * CE].bitcast(U32).rearrange("p (c w) -> p c w", w=2)
        pos = sb("pos", [P, ST])
        idx = sb("idx", [P, 2, ST], U32)
        recs = sb("recs", [P, 2, ST, 2], U32)
        neg = sb("neg", [P, Q, P])
        negf = neg[:, :, :].rearrange("p q j -> p (q j)")
        starts, tot, toti = negf[:, 0:NB + 1], negf[:, P + 1:P + 1 + NB], negf[:, 2 * P + 1:2 * P + 3 + NB].bitcast(I32)
        gstart = sb("gstart", [1, NB + 2], I32)
        bst = sb("bst", [P, Q, 6])
        mv = sb("mv", [P, Q, 2])
        nb_ = sb("nb_", [P, Q, 4])
        nbi = sb("nbi", [P, Q], I32)
        rstd = sb("rstd", [P, Q])
        xn = sb("xn", [P, Q, P])
        xT = sb("xT", [P, T])
        bufA = sb("bufA", [P, T])
        bufB = sb("bufB", [P, T])
        bufC = sb("bufC", [P, T])
        bufD = sb("bufD", [P, T])
        sm = sb("sm", [P, 16])
        small = sb("small", [P, Q * H0 * E0])
        small2 = sb("small2", [P, Q * H0 * E0])
        gmx = sb("gmx", [P, H0])
        gmall = sb("gmall", [P, H0])
        yb = sb("yb", [P, Q, E0, P])
        big1 = sb("big1", [P, 8, P])
        big2 = sb("big2", [P, 8, P])
        big3 = sb("big3", [P, 8, P])

        stage = sb("stage", [P, 2, 1, GT, PW])
        gidx = sb("gidx", [P, 2, 1, GT, 2], U32)
        ring_dst = sb("ring_dst", [P, RING, GT, 2], U32)
        OT = words[:, :].bitcast(BF16)[:, 0:GT * P].rearrange("p (k e) -> p k e", k=GT)
        zg = sb("zg", [P, GT, H0])
        eg = sb("eg", [P, GT, H0])
        Vg = sb("Vg", [P, GT, VW])
        V3 = parts[:, 0:GT * 3 * VW // 2].bitcast(BF16).rearrange("p (k s f) -> p k s f", k=GT, s=3)
        agg = sb("agg", [P, Q, VW])
        xTb = sb("xTb", [P, T])
        mix0 = sb("mix0", [P, Q, E0])
        mixw = sb("mixw", [P, Q, E1 + 1])
        ffh = [t[:, 4 * h:4 * h + 4, :].rearrange("p a b -> p (a b)") for t in (big1, big2) for h in range(2)]
        gates = sb("gates", [P, Q, E1])
        pairs = big1[:, 0:4, :].rearrange("p a (b c) -> p (a b) c", c=E1)
        cmp1 = pairs[:, 0:Q * E1, :].rearrange("p (q a) c -> p q a c", q=Q)
        cmp2 = pairs[:, Q * E1:2 * Q * E1, :].rearrange("p (q a) c -> p q a c", q=Q)
        vext = sb("vext", [P, Q, H1, HD + 1])
        cden = sb("cden", [P, H1])
        mxh = sb("mxh", [P, H1])
        hid1 = sb("hid1", [P, FC, T])
        hid = hid1[:, 0:2, :]
        rows_b = yb[:, :, :, :].bitcast(BF16).rearrange("p q e f -> p (q e f)")
        hi1 = rows_b[:, 0:2 * CT * HI].rearrange("p (o n) -> p o n", o=2)
        lo1 = rows_b[:, 2 * CT * HI:2 * CT * (HI + LO)].rearrange("p (o n) -> p o n", o=2)
        O = hid1[:, 2:4, :].bitcast(BF16).rearrange("p o (k b) -> p o k b", k=ST)

        pR = psum("pR", [P, 8, P])
        pS = psum("pS", [P, 8, P])
        p4 = psum("p4", [P, T])
        p4b = p4[:, :].bitcast(BF16).rearrange("p (k e) -> p k e", e=P)
        p5 = psum("p5", [P, T])
        pSb = pS[:, 0, 0:P // 2].bitcast(BF16)
        p6 = psum("p6", [P, T])
        p7 = psum("p7", [P, T])

        weights_in = sem("weights_in")
        edges_in = sem("edges_in")
        x_in = sem("x_in")
        consts = sem("consts")
        counted_onehot = sem("counted_onehot")
        counted = sem("counted")
        bases_ready = sem("bases_ready")
        chunk_in = sem("chunk_in")
        scattered = [sem("scattered0"), sem("scattered1")]
        rows_out = sem("rows_out")
        experts_out = sem("experts_out")
        stores_done = sem("stores_done")
        guard_ready = sem("guard_ready")
        tables_ready = sem("tables_ready")
        passed = sem("passed")
        setup_chain = sem("setup_chain")
        chain1 = sem("chain1")
        chain2 = sem("chain2")
        chaing = sem("chaing")
        chainm = sem("chainm")
        chainb = sem("chainb")
        gidx_in = [sem("gidx_in0"), sem("gidx_in1")]
        gathered = [sem("gathered0"), sem("gathered1")]
        ring_out = sem("ring_out")
        ring_filled = sem("ring_filled")
        ring_freed = sem("ring_freed")
        y_in = sem("y_in")
        adj_in = sem("adj_in")
        mask_ahead = sem("mask_ahead")
        result_out = sem("result_out")

        vwork = {0: ["xn"], 5: ["masked"], 6: ["prob"], 9: ["zmin"], 10: ["x1"], 11: ["xn1"], 13: ["pay"]}
        twork = {1: ["xT"], 2: ["hT"], 3: ["gT", "ay"], 4: ["logits"], 7: ["PT", "hpT"], 8: ["hout"], 12: ["xT1", "hrow"]}
        for e in range(E0):
            twork[12 + e] = twork.get(12 + e, []) + [f"up0_{e}", f"up1_{e}", f"down{e}"]
        ahead = lambda name, g: [f"{name}{g + 1}"] if g + 1 < SG else []
        V1 = Steps(sem("vector_1"), ["onehot0"] + [s for g in range(SG) for s in [f"prod{g}", f"idx{g}"] + ahead("onehot", g) + vwork.get(g, [])])
        T1 = Steps(sem("tensor_1"), ["rank0"] + [s for g in range(SG) for s in [f"ranked{g}"] + ahead("rank", g) + twork.get(g, [])])
        A1 = Steps(sem("scalar_1"), ["xT", "hT", "gT", "ay", "exp", "PT", "hpT", "elu", "xT1"]
                   + [f"{s}{e}" for e in range(E0) for s in ("gelu0_", "gelu1_", "y")])
        VG = Steps(sem("vector_g"), ["z", "parts", "onehot_after_next"])
        TG = Steps(sem("tensor_g"), ["dstscore", "next_T", "sums"])
        AG = Steps(sem("scalar_g"), ["exp", "next_T"])
        qs = range(Q)
        order = list(range(1, E1 + 1)) + [0]
        V2 = Steps(sem("vector_2"), ["agg", "gexp0", "x2", "xn", "keys0", "v", "add0", "max0", "keys1"]
                   + [s for q in qs for s in ([f"add{q + 1}", f"max{q + 1}"] if q < Q - 1 else [])
                      + ([f"keys{q + 2}"] if q < Q - 2 else []) + [f"ctx{q}"]] + ["y1", "mask", "allowed", "xn3", "gexp", "gate"])
        T2 = Steps(sem("tensor_2"), ["xT", "qT", "kT", "v", "scores0"]
                   + [s for q in qs for s in ([f"scores{q + 1}"] if q < Q - 1 else []) + [f"PT{q}", f"ctx{q}"]]
                   + ["ctxT", "attn", "y1T", "maskT"] + [f"ffup{f}" for f in range(FC)] + ["ff", "xT3", "router"])
        A2 = Steps(sem("scalar_2"), ["gate0", "xT", "qT", "kT"]
                   + [f"{s}{q}" for q in qs for s in ("exp", "PT")]
                   + ["ctxT", "y1T"] + [f"relu{f}" for f in range(FC)] + ["xT3", "rexp"])
        VB = Steps(sem("vector_b"), [f"mix{e}" for e in order])
        weights_T = lambda e: [] if e else ["mixT"]
        TB = Steps(sem("tensor_b"), [s for e in order for s in weights_T(e) + [f"up{f}_{e}" for f in range(FC)] + [f"down{e}"]])
        AB = Steps(sem("scalar_b"), [s for e in order for s in weights_T(e) + [f"gelu{f}_{e}" for f in range(FC)]])

        block = ctx.enter_context(nc.Block())

        sorted_tiles = sorted_edges[0:CAP // GE * GE, :].rearrange("(g p k) w -> p g k w", p=P, k=GT)

        CH1, CH2 = PER

        @block.sync
        def _(sp):
            def wait(sm_, value):
                sp.wait_ge(sm_, value)
                sp.sem_inc(passed, 1)

            sp.dma_start(X[:, :, :].bitcast(I32).rearrange("p b f -> p (b f)")[:, 0:NE // P],
                         a["edges"][1].rearrange("(p c) -> p c", p=P)).then_inc(edges_in, 16)
            for tile, src in wl:
                sp.dma_start(tile, src).then_inc(weights_in, 16)

            e_view = [a["edges"][r].rearrange("(p c) -> p c", p=P) for r in range(2)]

            def load_chunk(c):
                sp.dma_start(adjc[:, :, :], a["adj"].rearrange("b i j -> i b j")[:, bass.ds(c * Q, Q), :]).then_inc(chunk_in, 16)
                sp.dma_start(srcc, e_view[0][:, bass.ds(c * CE, CE)]).then_inc(chunk_in, 16)
                sp.dma_start(dstc, e_view[1][:, bass.ds(c * CE, CE)]).then_inc(chunk_in, 16)

            sp.wait_ge(bases_ready, 1)
            sp.dma_start(X[:, :, :], a["x"].rearrange("b n f -> n b f")).then_inc(x_in, 16)
            load_chunk(0)
            sp.sem_inc(stores_done, 1)
            with sp.Fori(0, NCH) as c:
                wait(V1.sem, V1.at(c, "masked"))
                load_chunk((c + 1) % NCH)
                wait(V1.sem, V1.at(c, "pay"))
                sp.dma_start(node_rows.rearrange("(b n) w -> n b w", n=P)[:, bass.ds(c * Q, Q), :],
                             pay[:, bass.ds(c * Q, Q), :]).then_inc(rows_out, 16)
                wait(A1.sem, A1.at(c, f"y{E0 - 1}"))
                sp.dma_start(expert_rows.rearrange("(b n) e f -> n b e f", n=P)[:, bass.ds(c * Q, Q), :, :],
                             yb[:, :, :, :]).then_inc(experts_out, 16)
                wait(rows_out, 16 * (c + 1))
                wait(experts_out, 16 * (c + 1))
                sp.sem_inc(stores_done, 1)
            wait(chunk_in, 48 * (NCH + 1))

            for h in range(2):
                wait(scattered[h], FILLED + 128 * (NCH * SG // 2))

            def load_idx(it, h):
                sp.dma_start(gidx[:, h, :, :, :], sorted_tiles[:, bass.ds(it * 2 + h, 1), :, :]).then_inc(gidx_in[h], 16)

            for h in range(2):
                load_idx(0, h)
            turns = sp.value_load(gstart[0:1, NB + 1:NB + 2], min_val=1, max_val=TURNS)
            with sp.Fori(0, turns) as it:
                for h in range(2):
                    slot = (it % (RING // 2)) * 2 + h
                    wait(gathered[h], 16 * GT * (it + 1))
                    wait(ring_freed, it * 2 + h + 1)
                    sp.dma_start(ring[:, bass.ds(slot, 1), :, :], stage[:, h, :, :, :]).then_inc(ring_out, 16)
                    sp.dma_start(ring_dst[:, bass.ds(slot, 1), :, :], gidx[:, h, :, :, :]).then_inc(ring_out, 16)
                    wait(ring_out, 64 * it + 32 * (h + 1))
                    sp.sem_inc(ring_filled, 1)
                    load_idx(it + 1, h)
            for h in range(2):
                wait(gidx_in[h], 16 * turns + 16)
            sp.wait_ge(result_out, 16 * NCH)


        @block.gpsimd
        def _(pool):
            pool.iota(iota[:, :], pattern=[[1, P]], base=0, channel_multiplier=0,
                      allow_small_or_imprecise_dtypes=True).then_inc(consts, 1)
            pool.memset(onesb[:, :], 1.0).then_inc(consts, 1)
            pool.memset(zero[:, :], 0.0).then_inc(consts, 1)
            pool.memset(zerob[:, :], 0.0).then_inc(consts, 1)
            pool.memset(ones1[:, :], 1.0).then_inc(consts, 1)
            pool.memset(big3[:, :, :], 1.0).then_inc(consts, 1)
            pool.memset(pay[:, :, :], 1.0).then_inc(consts, 1)
            pool.memset(vext[:, :, :, :], 1.0).then_inc(consts, 1)
            fill = big2[:, :, :].rearrange("p a b -> p (a b)").bitcast(U32).rearrange("p (c w) -> p c w", w=2)
            pool.memset(fill[:, :, 0], 0).then_inc(consts, 1)
            pool.memset(fill[:, :, 1].bitcast(F32), -1.0).then_inc(consts, 1)
            pool.wait_ge(consts, 10)
            pool.affine_select(out=before[:, :], in_=onesb[:, :], compare_op=ALU.is_gt, fill=0.0, base=0,
                               pattern=[[1, P]], channel_multiplier=-1).then_inc(consts, 1)
            pool.affine_select(out=notbefore[:, :], in_=onesb[:, :], compare_op=ALU.is_ge, fill=0.0, base=0,
                               pattern=[[-1, P]], channel_multiplier=1).then_inc(consts, 1)
            pool.affine_select(out=ident[:, :], in_=zero[:, :], compare_op=ALU.not_equal, fill=1.0, base=0,
                               pattern=[[-1, P]], channel_multiplier=1).then_inc(consts, 1)
            pool.affine_select(out=headmask[:, :], in_=big3[:, 0, 0:H1], compare_op=ALU.is_ge, fill=0.0, base=0,
                               pattern=[[-HD, H1]], channel_multiplier=1).then_inc(consts, 1)
            pool.affine_select(out=lower[:, :, :], in_=big3[:, 0, 0:E1 * E1].rearrange("p (a b) -> p a b", a=E1),
                               compare_op=ALU.is_gt, fill=0.0, base=0,
                               pattern=[[1, E1], [-1, E1]], channel_multiplier=0).then_inc(consts, 1)
            pool.wait_ge(consts, 15)
            pool.tensor_copy(identb[:, :], ident[:, :]).then_inc(consts, 1)
            pool.affine_select(out=headmask[:, :], in_=headmask[:, :], compare_op=ALU.is_ge, fill=0.0, base=HD - 1,
                               pattern=[[HD, H1]], channel_multiplier=-1).then_inc(consts, 1)
            fills = sorted_edges.rearrange("(r p c) w -> r p c w", p=P, c=4 * P)
            for r in range(FILLS):
                pool.dma_start(fills[r], fill).then_inc(scattered[r % 2], 16)
            for h in range(2):
                pool.wait_ge(scattered[h], FILLED)

            last = pool.to_reg(CAP - 1)
            with pool.Fori(0, NCH) as c:
                for g in range(SG):
                    pool.wait_ge(V1.sem, V1.at(c, f"idx{g}"))
                    pool.sem_inc(passed, 1)
                    for k in range(ST):
                        pool.indirect_dma_start(
                            out=sorted_edges, out_offset=bass.IndirectOffsetOnAxis(ap=idx[:, g % 2, k:k + 1], axis=0),
                            in_=recs[:, g % 2, k, :], in_offset=None, bounds_check=last, oob_is_err=False,
                        ).then_inc(scattered[g % 2], 16)

            pool.wait_ge(V1.sem, V1.at(NCH - 1, "pay"))
            pool.partition_all_reduce(gmall[:, :], gmx[:, :], P, bass.bass_isa.ReduceOp.max).then_inc(guard_ready, 1)

            turns = pool.value_load(gstart[0:1, NB + 1:NB + 2], min_val=1, max_val=TURNS)
            with pool.Fori(0, turns) as it:
                for h in range(2):
                    pool.wait_ge(gidx_in[h], 16 * (it + 1))
                    pool.sem_inc(passed, 1)
                    for k in range(GT):
                        pool.indirect_dma_start(
                            out=stage[:, h, 0, k, :], out_offset=None, in_=node_rows,
                            in_offset=bass.IndirectOffsetOnAxis(ap=gidx[:, h, 0, k, 0:1], axis=0),
                        ).then_inc(gathered[h], 16)

        @block.scalar
        def _(act):
            act.wait_ge(weights_in, 16 * len(wl))
            act.wait_ge(consts, 17)
            act.activation(sm[:, 15:16], zero[:, 0:1], ACT.Copy).then_inc(A1.sem, A1.n)

            def copy(steps, i, name, dst, src, *waits):
                for st, what in waits:
                    act.wait_ge(st.sem, st.at(i, what))
                act.activation(dst, src, ACT.Copy).then_inc(steps.sem, 1)

            with act.Fori(0, NCH) as c:
                copy(A1, c, "xT", xT[:, :], p4[:, :], (T1, "xT"))
                copy(A1, c, "hT", bufA[:, :], p5[:, :], (T1, "hT"))
                act.wait_ge(T1.sem, T1.at(c, "gT"))
                act.activation(bufB[:, :], p4[:, :], ACT.Identity, bias=w["g_a1"][:, 0:1]).then_inc(A1.sem, 1)
                copy(A1, c, "ay", sm[:, 0:Q], p6[:, 0:Q], (T1, "ay"))
                act.wait_ge(V1.sem, V1.at(c, "masked"))
                act.activation(bufC[:, :], bufC[:, :], ACT.Exp).then_inc(A1.sem, 1)
                copy(A1, c, "PT", bufD[:, :], p4[:, :], (T1, "PT"))
                copy(A1, c, "hpT", bufB[:, :], p5[:, :], (T1, "hpT"))
                act.wait_ge(V1.sem, V1.at(c, "zmin"))
                act.activation(bufC[:, :], bufC[:, :], ACT.Exp).then_inc(A1.sem, 1)
                copy(A1, c, "xT1", xT[:, :], p5[:, :], (T1, "xT1"))
                for e in range(E0):
                    for f in range(2):
                        act.wait_ge(T1.sem, T1.at(c, f"up{f}_{e}"))
                        act.activation(hid[:, f, :], pS[:, 4 * f:4 * f + 4, :], ACT.Gelu,
                                       bias=w["f_b1"][:, e, f:f + 1]).then_inc(A1.sem, 1)
                    act.wait_ge(T1.sem, T1.at(c, f"down{e}"))
                    if e == 0:
                        act.wait_ge(stores_done, c + 1)
                    act.activation(yb[:, :, e, :], p7[:, :].rearrange("p (q f) -> p q f", q=Q), ACT.Copy).then_inc(A1.sem, 1)

            act.wait_ge(stores_done, NCH + 1)
            act.wait_ge(chunk_in, 48 * (NCH + 1))
            act.activation(sm[:, 15:16], zero[:, 0:1], ACT.Copy).then_inc(A2.sem, A2.n)

            def load_adj(c):
                act.dma_start(adjc[:, :, :], a["adj"].rearrange("b i j -> i b j")[:, bass.ds(c * Q, Q), :]).then_inc(adj_in, 16)

            load_adj(0)
            act.wait_ge(tables_ready, 1)
            act.activation(dn, dn, ACT.Exp).then_inc(guard_ready, 1)
            act.activation(sm[:, 14:15], zero[:, 0:1], ACT.Copy).then_inc(AB.sem, AB.n)

            def transposed_rows():
                act.activation(OT[:, 0:8, :], p4b, ACT.Copy)
                return act.activation(OT[:, 8, :], pSb, ACT.Copy)

            act.wait_ge(mask_ahead, 1)
            load_adj(1)
            act.wait_ge(TG.sem, TG.at(-1, "next_T"))
            transposed_rows().then_inc(AG.sem, AG.n)

            def load_y(c):
                act.dma_start(yb[:, :, :, :], expert_rows.rearrange("(b n) e f -> n b e f", n=P)[:, bass.ds(c * Q, Q), :, :]).then_inc(y_in, 16)

            load_y(0)

            def back(c, s):
                e = order[s]
                if e == 0:
                    copy(AB, c, "mixT", mixT, p4[0:E1 + 1, :], (TB, "mixT"))
                for f in range(FC):
                    act.wait_ge(TB.sem, TB.at(c, f"up{f}_{e}"))
                    act.activation(hid1[:, f, :], pR[:, 4 * (f % 2):4 * (f % 2) + 4, :], ACT.Gelu,
                                   bias=w["m_b1"][:, e, f:f + 1]).then_inc(AB.sem, 1)

            def store(c):
                act.wait_ge(VB.sem, VB.at(c, "mix0"))
                act.dma_start(a["out"].rearrange("b n f -> n b f")[:, bass.ds(c * Q, Q), :],
                              X[:, bass.ds(c * Q, Q), :]).then_inc(result_out, 16)

            def front(c, behind):
                starts_of = [act.value_load(gstart[0:1, bass.ds(c * Q + q, 1)], min_val=2 * q, max_val=CAP // GE) for q in range(Q + 1)]
                def group(g):
                    act.wait_ge(VG.sem, VG.at(g, "z"))
                    act.activation(eg[:, :, :], zg[:, :, :], ACT.Exp).then_inc(AG.sem, 1)
                    act.wait_ge(TG.sem, TG.at(g, "next_T"))
                    transposed_rows().then_inc(AG.sem, 1)

                for q in qs:
                    group(starts_of[q])
                    if q == 0:
                        behind(0)
                    with act.Fori(starts_of[q] + 1, starts_of[q + 1]) as g:
                        group(g)
                behind(1)
                act.wait_ge(V2.sem, V2.at(c, "gexp0"))
                act.activation(small2[:, 0:Q * E0], small[:, 0:Q * E0], ACT.Exp).then_inc(A2.sem, 1)
                behind(2)
                behind(3)
                act.wait_ge(V2.sem, V2.at(c, "x2"))
                load_y((c + 1) % NCH)
                copy(A2, c, "xT", xT[:, :], p4[:, :], (T2, "xT"))
                act.wait_ge(T2.sem, T2.at(c, "qT"))
                act.activation(bufA[:, :], p5[:, :], ACT.Identity, bias=w["a_bqk"][:, 0:1]).then_inc(A2.sem, 1)
                act.wait_ge(T2.sem, T2.at(c, "kT"))
                act.activation(bufB[:, :], p4[:, :], ACT.Identity, bias=w["a_bqk"][:, 1:2]).then_inc(A2.sem, 1)
                behind(4)
                for q in qs:
                    act.wait_ge(V2.sem, V2.at(c, f"max{q}"))
                    act.activation(big2[:, :, :], big2[:, :, :], ACT.Exp, scale=HD ** -0.5).then_inc(A2.sem, 1)
                    if q in (1, 2):
                        behind(4 + q)
                    act.wait_ge(T2.sem, T2.at(c, f"PT{q}"))
                    act.activation(big3[:, 0:4, :], p4[:, :].rearrange("p (h i) -> p h i", h=4), ACT.Copy)
                    act.activation(big3[:, 4:8, :], p6[:, :].rearrange("p (h i) -> p h i", h=4), ACT.Copy).then_inc(A2.sem, 1)
                behind(7)
                copy(A2, c, "ctxT", bufA[:, :], p4[:, :], (T2, "ctxT"))
                copy(A2, c, "y1T", xT[:, :], p4[:, :], (T2, "y1T"))
                act.wait_ge(V2.sem, V2.at(c, "mask"))
                load_adj((c + 2) % NCH)
                for f in range(FC):
                    act.wait_ge(T2.sem, T2.at(c, f"ffup{f}"))
                    act.activation(ffh[f], pS[:, 4 * (f % 2):4 * (f % 2) + 4, :], ACT.Relu,
                                   bias=w["a_c1"][:, f:f + 1]).then_inc(A2.sem, 1)
                behind(8)
                copy(A2, c, "xT3", xTb[:, :], p4[:, :], (T2, "xT3"))
                act.wait_ge(V2.sem, V2.at(c, "gexp"))
                act.activation(gates[:, :, :], gates[:, :, :], ACT.Exp).then_inc(A2.sem, 1)

            front(0, lambda s: None)
            with act.Fori(1, NCH) as c:
                front(c, lambda s: back(c - 1, s))
                store(c - 1)
            for s_ in range(E1 + 1):
                back(NCH - 1, s_)
            store(NCH - 1)
            act.wait_ge(y_in, 16 * (NCH + 1))
            act.wait_ge(adj_in, 16 * (NCH + 2))

        @block.tensor
        def _(pe):
            pe.wait_ge(weights_in, 16 * len(wl))
            pe.wait_ge(consts, 17)
            pe.matmul(p7[:, 0:ST * LO], onesb[:, :], zerob[:, :], start=True, stop=False, skip_group_check=True).then_inc(counted, 2)
            with pe.Fori(0, NE // P // CT // 2) as i:
                for o in range(2):
                    pe.wait_ge(counted_onehot, 2 * i + o + 1)
                    for s in range(CT // ST):
                        m = pe.matmul(p7[:, 0:ST * LO], hi1[:, o, s * ST * HI:(s + 1) * ST * HI], lo1[:, o, s * ST * LO:(s + 1) * ST * LO],
                                      start=False, stop=False, skip_group_check=True)
                    m.then_inc(counted, 1)
            pe.wait_ge(counted_onehot, NE // P // CT + 1)
            for h in range(2):
                m = pe.matmul(pS[:, 4 * h:4 * h + 4, :], big3[:, 0, :], big1[:, 4 * h:4 * h + 4, :], start=True, stop=True)
            m.then_inc(counted, 1)
            pe.wait_ge(bases_ready, 1)
            for h in range(2):
                m = pe.matmul(pR[:, 4 * h:4 * h + 4, 0:NB], ident[:, :], big1[:, 4 * h:4 * h + 4, 0:NB],
                              start=True, stop=False, skip_group_check=True)
            m.then_inc(T1.sem, T1.n)

            def rank(c, g):
                pe.wait_ge(V1.sem, V1.at(c, f"onehot{g}"))
                for h in range(2):
                    m = pe.matmul(pR[:, 4 * h:4 * h + 4, 0:NB], before[:, :], O[:, g % 2, 4 * h:4 * h + 4, 0:NB],
                                  start=False, stop=False, skip_group_check=True)
                m.then_inc(T1.sem, 1)

            def ranked(c, g):
                pe.wait_ge(V1.sem, V1.at(c, f"prod{g}"))
                for h in range(2):
                    m = pe.matmul(pR[:, 4 * h:4 * h + 4, 0:NB], notbefore[:, :], O[:, g % 2, 4 * h:4 * h + 4, 0:NB],
                                  start=False, stop=False, skip_group_check=True)
                m.then_inc(T1.sem, 1)

            def turn(dst, src, inc):
                for q in qs:
                    m = pe.transpose(dst[:, q * P:(q + 1) * P], src[:, q * P:(q + 1) * P], ident[:, :])
                m.then_inc(inc.sem, 1)

            def flat(t):
                return t[:, :, :].rearrange("p q f -> p (q f)")

            def rows_bias(dst, q, bias, start=False):
                return pe.matmul(dst[:, q * P:(q + 1) * P], ones1[:, :], bias, start=start, stop=True)

            def slices(c):
                def s_xT():
                    pe.wait_ge(V1.sem, V1.at(c, "xn"))
                    turn(p4, flat(xn), T1)

                def s_hT():
                    pe.wait_ge(A1.sem, A1.at(c, "xT"))
                    pe.matmul(p5[:, :], w["g_W"][:, :], xT[:, :], start=True, stop=True).then_inc(T1.sem, 1)

                def s_gT():
                    pe.wait_ge(A1.sem, A1.at(c, "hT"))
                    pe.matmul(p4[:, :], w["g_a12"][:, :], bufA[:, :], start=True, stop=True).then_inc(T1.sem, 1)
                    for q in qs:
                        m = pe.matmul(p6[:, q:q + 1], bufA[:, q * P:(q + 1) * P], w["g_a2"][:, :], start=True, stop=True)
                    m.then_inc(T1.sem, 1)

                def s_logits():
                    pe.wait_ge(A1.sem, A1.at(c, "gT"))
                    for q in qs:
                        m = pe.matmul(p5[:, q * P:(q + 1) * P], bufB[:, q * P:(q + 1) * P], bufA[:, q * P:(q + 1) * P],
                                      start=True, stop=True)
                    m.then_inc(T1.sem, 1)

                def s_PT():
                    pe.wait_ge(V1.sem, V1.at(c, "prob"))
                    turn(p4, bufC, T1)
                    pe.wait_ge(A1.sem, A1.at(c, "PT"))
                    for q in qs:
                        m = pe.matmul(p5[:, q * P:(q + 1) * P], xn[:, q, :], bufD[:, q * P:(q + 1) * P], start=True, stop=True)
                    m.then_inc(T1.sem, 1)

                def s_hout():
                    pe.wait_ge(A1.sem, A1.at(c, "hpT"))
                    for q in qs:
                        pe.matmul(p4[:, q * P:(q + 1) * P], xT[:, q * P:(q + 1) * P], w["g_W1"][:, :], start=True, stop=False)
                        m = pe.matmul(p4[:, q * P:(q + 1) * P], bufB[:, q * P:(q + 1) * P], w["g_W2"][:, :], start=False, stop=True)
                    m.then_inc(T1.sem, 1)

                def s_hrow():
                    pe.wait_ge(V1.sem, V1.at(c, "xn1"))
                    turn(p5, flat(xn), T1)
                    pe.wait_ge(A1.sem, A1.at(c, "xT1"))
                    for q in qs:
                        m = pe.matmul(p6[:, q * 16:(q + 1) * 16], xT[:, q * P:(q + 1) * P], w["f_Wgat"][:, :], start=True, stop=True)
                    m.then_inc(T1.sem, 1)

                def s_expert(e):
                    for f in range(2):
                        if e > 0:
                            pe.wait_ge(A1.sem, A1.at(c, f"gelu{f}_{e - 1}"))
                        pe.matmul(pS[:, 4 * f:4 * f + 4, :], w["f_W1"][:, e, f, :], xT[:, :], start=True, stop=True).then_inc(T1.sem, 1)
                    for f in range(2):
                        pe.wait_ge(A1.sem, A1.at(c, f"gelu{f}_{e}"))
                    if e > 0:
                        pe.wait_ge(A1.sem, A1.at(c, f"y{e - 1}"))
                    for q in qs:
                        for f in range(2):
                            pe.matmul(p7[:, q * P:(q + 1) * P], hid[:, f, q * P:(q + 1) * P], w["f_W2"][:, e, f, :],
                                      start=(f == 0), stop=False)
                        m = rows_bias(p7, q, w["f_b2"][0:1, e * P:(e + 1) * P])
                    m.then_inc(T1.sem, 1)

                return {1: [s_xT], 2: [s_hT], 3: [s_gT], 4: [s_logits], 7: [s_PT], 8: [s_hout],
                        12: [s_hrow, lambda: s_expert(0)]} | {12 + e: [lambda e=e: s_expert(e)] for e in range(1, E0)}

            with pe.Fori(0, NCH) as c:
                work = slices(c)
                rank(c, 0)
                for g in range(SG):
                    ranked(c, g)
                    if g + 1 < SG:
                        rank(c, g + 1)
                    for slice_ in work.get(g, []):
                        slice_()
            pe.wait_ge(A1.sem, A1.at(NCH - 1, f"y{E0 - 1}"))
            for steps in (T2, TB):
                pe.matmul(p7[:, 0:P], ident[:, :], ident[:, :], start=True, stop=True).then_inc(steps.sem, steps.n)

            def transposed_rows(g):
                for k in range(GT):
                    m = pe.transpose(p4b[:, k, :] if k < 8 else pSb, og(g)[:, k, :], identb[:, :])
                return m

            def mask_T():
                for q in qs:
                    m = pe.transpose(p6[:, q * P:(q + 1) * P], big3[:, q, :], ident[:, :])
                return m

            def og(g):
                return Og[:, bass.ds(g % 3, 1), :, :].rearrange("p o k e -> p (o k) e")

            pe.wait_ge(mask_ahead, 1)
            mask_T().then_inc(mask_ahead, 1)
            pe.wait_ge(VG.sem, VG.n)
            transposed_rows(0).then_inc(TG.sem, TG.n)

            def up(c, s):
                e = order[s]
                if e == 0:
                    pe.wait_ge(V2.sem, V2.at(c, "gate"))
                    for q in qs:
                        m = pe.transpose(p4[0:E1 + 1, q * P:(q + 1) * P], mixw[:, q, :], ident[:, :])
                    m.then_inc(TB.sem, 1)
                for f in range(FC):
                    if f >= 2:
                        pe.wait_ge(AB.sem, AB.at(c, f"gelu{f - 2}_{e}"))
                    elif s > 0:
                        pe.wait_ge(AB.sem, AB.at(c, f"gelu{f + 2}_{order[s - 1]}"))
                    pe.matmul(pR[:, 4 * (f % 2):4 * (f % 2) + 4, :], w["m_W1"][:, e, f, :], xTb[:, :], start=True, stop=True).then_inc(TB.sem, 1)

            def down(c, s):
                e = order[s]
                if s > 0:
                    pe.wait_ge(VB.sem, VB.at(c, f"mix{order[s - 1]}"))
                if e == 0:
                    pe.wait_ge(AB.sem, AB.at(c, "mixT"))
                    for q in qs:
                        pe.matmul(p7[:, q * P:(q + 1) * P], mixT[:, q * P:(q + 1) * P], w["m_b2"][:, :], start=(q == 0), stop=False,
                                  skip_group_check=True)
                for f in range(FC):
                    pe.wait_ge(AB.sem, AB.at(c, f"gelu{f}_{e}"))
                    for q in qs:
                        m = pe.matmul(p7[:, q * P:(q + 1) * P], hid1[:, f, q * P:(q + 1) * P], w["m_W2"][:, e, f, :],
                                      start=(e > 0 and f == 0 and q == 0), stop=(f == FC - 1), skip_group_check=True)
                m.then_inc(TB.sem, 1)

            def front(c, up, down):
                starts_of = [pe.value_load(gstart[0:1, bass.ds(c * Q + q, 1)], min_val=2 * q, max_val=CAP // GE) for q in range(Q + 1)]
                pe.wait_ge(A2.sem, A2.at(c - 1, "xT3"))
                pe.wait_ge(V2.sem, V2.at(c - 1, "gexp"))

                def group(q, g, between):
                    pe.wait_ge(AG.sem, AG.at(g - 1, "next_T"))
                    for k in range(GT):
                        for part in range(3):
                            m = pe.matmul(p5[:, k * 8:(k + 1) * 8], OT[:, k, :],
                                          dm3[:, bass.ds(c * Q + q, 1), part, :].rearrange("p o f -> p (o f)"),
                                          start=(part == 0), stop=(part == 2))
                    m.then_inc(TG.sem, 1)
                    pe.wait_ge(VG.sem, VG.at(g - 1, "onehot_after_next"))
                    transposed_rows(g + 1).then_inc(TG.sem, 1)
                    between()
                    pe.wait_ge(VG.sem, VG.at(g, "parts"))
                    for k in range(GT):
                        m = pe.matmul(p6[:, q * 3 * VW:(q + 1) * 3 * VW], og(g)[:, k, :],
                                      V3[:, k, :, :].rearrange("p s f -> p (s f)"), start=False, stop=False,
                                      skip_group_check=True)
                    m.then_inc(TG.sem, 1)

                for q in qs:
                    pe.matmul(p6[:, q * 3 * VW:(q + 1) * 3 * VW], onesb[:, :], zerob[:, 0:3 * VW], start=True, stop=False, skip_group_check=True)
                    group(q, starts_of[q], lambda: up(0) if q == 0 else down(0) if q == 1 else None)
                    with pe.Fori(starts_of[q] + 1, starts_of[q + 1]) as g:
                        group(q, g, lambda: None)
                up(1)
                down(1)
                up(2)
                down(2)
                up(3)
                pe.wait_ge(AG.sem, AG.at(starts_of[Q] - 1, "next_T"))
                pe.sem_inc(passed, 1)
                pe.wait_ge(V2.sem, V2.at(c, "xn"))
                turn(p4, flat(xn), T2)
                pe.wait_ge(A2.sem, A2.at(c, "xT"))
                pe.matmul(p5[:, :], w["a_Wqkv"][:, 0:P], xT[:, :], start=True, stop=True).then_inc(T2.sem, 1)
                pe.matmul(p4[:, :], w["a_Wqkv"][:, P:2 * P], xT[:, :], start=True, stop=True).then_inc(T2.sem, 1)
                pe.wait_ge(A2.sem, A2.at(c, "qT"))
                for q in qs:
                    m = pe.matmul(p5[:, q * P:(q + 1) * P], xT[:, q * P:(q + 1) * P], w["a_Wqkv"][:, 2 * P:3 * P], start=True, stop=True)
                m.then_inc(T2.sem, 1)

                def scores(q):
                    pe.wait_ge(V2.sem, V2.at(c, f"keys{q}"))
                    if q > 0:
                        pe.wait_ge(V2.sem, V2.at(c, f"add{q - 1}"))
                    for h in range(2):
                        m = pe.matmul(pS[:, 4 * h:4 * h + 4, :], bufA[:, q * P:(q + 1) * P], big1[:, 4 * h:4 * h + 4, :],
                                      start=True, stop=True)
                    m.then_inc(T2.sem, 1)

                down(3)
                scores(0)
                up(4)
                for q in qs:
                    if q < Q - 1:
                        scores(q + 1)
                    if q in (1, 2):
                        up(4 + q)
                    pe.wait_ge(A2.sem, A2.at(c, f"exp{q}"))
                    for h in range(H1):
                        m = pe.transpose((p4, p6)[h // 4][:, h % 4 * P:(h % 4 + 1) * P], big2[:, h, :], ident[:, :])
                    m.then_inc(T2.sem, 1)
                    if q < 3:
                        down(4 + q)
                    if q == Q - 1:
                        up(7)
                    pe.wait_ge(A2.sem, A2.at(c, f"PT{q}"))
                    if q == 0:
                        pe.wait_ge(V2.sem, V2.at(c, "v"))
                    if q > 0:
                        pe.wait_ge(V2.sem, V2.at(c, f"ctx{q - 1}"))
                    for h in range(H1):
                        m = pe.matmul(p5[:, h * 17:(h + 1) * 17], big3[:, h, :], vext[:, q, h, :], start=True, stop=True)
                    m.then_inc(T2.sem, 1)
                pe.wait_ge(V2.sem, V2.at(c, f"ctx{Q - 1}"))
                turn(p4, bufC, T2)
                pe.wait_ge(A2.sem, A2.at(c, "ctxT"))
                for q in qs:
                    m = pe.matmul(p5[:, q * P:(q + 1) * P], bufA[:, q * P:(q + 1) * P], w["a_Wo"][:, :], start=True, stop=True)
                m.then_inc(T2.sem, 1)
                down(7)
                pe.wait_ge(V2.sem, V2.at(c, "y1"))
                turn(p4, bufD, T2)
                pe.wait_ge(V2.sem, V2.at(c, "mask"))
                mask_T().then_inc(T2.sem, 1)
                pe.wait_ge(A2.sem, A2.at(c, "y1T"))
                for f in range(FC):
                    if f >= 2:
                        pe.wait_ge(A2.sem, A2.at(c, f"relu{f - 2}"))
                    pe.matmul(pS[:, 4 * (f % 2):4 * (f % 2) + 4, :], w["a_W1"][:, f, :], xT[:, :], start=True, stop=True).then_inc(T2.sem, 1)
                for f in range(FC):
                    pe.wait_ge(A2.sem, A2.at(c, f"relu{f}"))
                    for q in qs:
                        m = pe.matmul(p5[:, q * P:(q + 1) * P], ffh[f][:, q * P:(q + 1) * P], w["a_W2"][:, f, :],
                                      start=(f == 0 and q == 0), stop=(f == FC - 1), skip_group_check=True)
                m.then_inc(T2.sem, 1)
                up(8)
                down(8)
                pe.wait_ge(V2.sem, V2.at(c, "xn3"))
                turn(p4, flat(xn), T2)
                pe.wait_ge(A2.sem, A2.at(c, "xT3"))
                for q in qs:
                    m = pe.matmul(p5[:, q * E1:(q + 1) * E1], xTb[:, q * P:(q + 1) * P], w["m_Wr"][:, :], start=True, stop=True)
                m.then_inc(T2.sem, 1)
            front(0, lambda s: None, lambda s: None)
            with pe.Fori(1, NCH) as c:
                front(c, lambda s: up(c - 1, s), lambda s: down(c - 1, s))
            for s in range(E1 + 1):
                up(NCH - 1, s)
                down(NCH - 1, s)

        @block.vector
        def _(vec):
            def cols(t):
                return t[:, :].rearrange("p (q f) -> p q f", q=Q)

            setup, c1, c2, cg, cm = (Chain(x, per) for x, per in ((setup_chain, 0), (chain1, CH1), (chain2, CH2), (chaing, 5), (chainm, 0)))
            cb = Chain(chainb, E1 * (Q - 1))
            vec.wait_ge(consts, 17)

            def do(chain, ins, bare=False):
                chain.count(ins)
                chain.wait(vec)
                if bare:
                    vec.sem_inc(passed, 1)

            def sig(steps, i, name, ins, bare=False):
                ins.then_inc(steps.sem, 1)
                vec.wait_ge(steps.sem, steps.at(i, name))
                if bare:
                    vec.sem_inc(passed, 1)

            NT = NE // P
            xi = X[:, :, :].bitcast(I32).rearrange("p b f -> p (b f)")
            xf = X[:, :, :].rearrange("p b f -> p (b f)")
            vec.wait_ge(edges_in, 16)
            do(setup, vec.tensor_single_scalar(xi[:, NT:2 * NT], xi[:, 0:NT], 10, op=ALU.arith_shift_right))
            do(setup, vec.tensor_copy(xf[:, 2 * NT:3 * NT], xi[:, NT:2 * NT]))
            do(setup, vec.tensor_single_scalar(xi[:, NT:2 * NT], xi[:, 0:NT], 7, op=ALU.arith_shift_right))
            do(setup, vec.tensor_single_scalar(xi[:, NT:2 * NT], xi[:, NT:2 * NT], LO - 1, op=ALU.bitwise_and))
            do(setup, vec.tensor_copy(xf[:, 3 * NT:4 * NT], xi[:, NT:2 * NT]))
            with vec.Fori(0, NT // CT // 2) as i:
                for o in range(2):
                    vec.wait_ge(counted, 2 * i + o + 1)
                    for row, n, at in ((hi1, HI, 2 * NT), (lo1, LO, 3 * NT)):
                        m = vec.tensor_tensor(row[:, o, :].rearrange("p (t n) -> p t n", n=n), iota[:, 0:n].unsqueeze(1).broadcast_to([P, CT, n]),
                                              xf[:, bass.ds(at + (2 * i + o) * CT, CT)].unsqueeze(2).broadcast_to([P, CT, n]), ALU.is_equal)
                    m.then_inc(counted_onehot, 1)
            vec.wait_ge(counted, 2 + NT // CT)
            do(setup, vec.tensor_copy(small[:, 0:ST * LO], p7[:, 0:ST * LO]))
            vec.tensor_tensor(big1[:, :, :].rearrange("p k (a b) -> p k a b", a=HI),
                              ident[:, :].rearrange("p (k a) -> p k a", k=ST).unsqueeze(3).broadcast_to([P, ST, HI, LO]),
                              small[:, 0:ST * LO].rearrange("p (k b) -> p k b", k=ST).unsqueeze(2).broadcast_to([P, ST, HI, LO]),
                              ALU.mult).then_inc(counted_onehot, 1)
            vec.wait_ge(counted, 3 + NT // CT)
            cnt = yb[:, :, :, :].rearrange("p q e f -> p (q e) f")[:, 0:ST, 0:NB]
            do(setup, vec.tensor_copy(cnt, pS[:, :, 0:NB]))
            do(setup, vec.tensor_reduce(tot, cnt.rearrange("p k b -> p b k"), AX, ALU.add))
            do(setup, vec.tensor_scalar(toti[:, 0:NB], tot, float(GE - 1), None, op0=ALU.add))
            do(setup, vec.tensor_single_scalar(toti[:, 0:NB], toti[:, 0:NB], 7, op=ALU.arith_shift_right))
            do(setup, vec.tensor_scalar(toti[:, 0:NB], toti[:, 0:NB], float(-(-2**16 // GT)), None, op0=ALU.mult))
            do(setup, vec.tensor_single_scalar(toti[:, 0:NB], toti[:, 0:NB], NINTH, op=ALU.arith_shift_right))
            do(setup, vec.tensor_copy(tot, toti[:, 0:NB]))
            do(setup, vec.tensor_scalar(tot, tot, 2.0, None, op0=ALU.max))
            do(setup, vec.memset(starts[:, 0:1], 0.0))
            do(setup, vec.tensor_tensor_scan(starts[:, 1:NB + 1], tot, zero[:, 0:NB], 0.0, ALU.add, ALU.add))
            do(setup, vec.tensor_copy(gstart[0:1, 0:NB + 1], starts[0:1, :]))
            do(setup, vec.tensor_scalar(toti[0:1, 0:1], starts[0:1, NB:NB + 1], 3.0, None, op0=ALU.add))
            do(setup, vec.tensor_single_scalar(gstart[0:1, NB + 1:NB + 2], toti[0:1, 0:1], 1, op=ALU.arith_shift_right))
            do(setup, vec.tensor_scalar(big1[:, 0, 0:NB], starts[:, 0:NB], float(GE), None, op0=ALU.mult))
            for k in range(1, ST):
                do(setup, vec.tensor_tensor(big1[:, k, 0:NB], big1[:, k - 1, 0:NB], cnt[:, k - 1, :], ALU.add))
            do(setup, vec.memset(gmx[:, :], -3e38))
            vec.memset(sm[:, 12:13], 0.0).then_inc(V1.sem, V1.n)
            vec.memset(sm[:, 13:14], 0.0).then_inc(bases_ready, 1)

            def inv_sqrt(chain, var, n=Q):
                v, y, t = nb_[:, 0:n, 0], nb_[:, 0:n, 1], nb_[:, 0:n, 2]
                do(chain, vec.tensor_scalar(v, var, EPS, None, op0=ALU.add))
                do(chain, vec.tensor_single_scalar(nbi[:, 0:n], nb_[:, 0:n, 0].bitcast(I32), 1, op=ALU.arith_shift_right))
                do(chain, vec.tensor_scalar(y.bitcast(I32), nbi[:, 0:n], -1.0, float(0x5F3759DF), op0=ALU.mult, op1=ALU.add))
                for r in range(3):
                    do(chain, vec.tensor_tensor(t, y, y, ALU.mult))
                    do(chain, vec.scalar_tensor_tensor(t, t, -0.5, v, ALU.mult, ALU.mult))
                    do(chain, vec.scalar_tensor_tensor(y if r < 2 else rstd[:, 0:n], t, 1.5, y, ALU.add, ALU.mult))

            def norm(chain, src, dst, last=None):
                for q in qs:
                    chain.count(vec.bn_stats(bst[:, q, :], src(q)))
                chain.wait(vec)
                vec.sem_inc(passed, 1)
                for q in qs:
                    chain.count(vec.bn_aggr(mv[:, q, :], bst[:, q, :]))
                chain.wait(vec)
                inv_sqrt(chain, mv[:, :, 1])
                for q in qs:
                    m = vec.tensor_scalar(dst(q), src(q), mv[:, q, 0:1], rstd[:, q:q + 1], op0=ALU.subtract, op1=ALU.mult)
                    if q < Q - 1:
                        chain.count(m)
                    elif last is None:
                        do(chain, m)
                    else:
                        sig(*last, m)

            def stage1(c):
                xq = lambda q: X[:, bass.ds(c * Q + q, 1), :].rearrange("p o f -> p (o f)")
                xc = X[:, bass.ds(c * Q, Q), :]

                def w_xn():
                    vec.sem_inc(passed, 1)
                    norm(c1, xq, lambda q: xn[:, q, :], (V1, c, "xn"))

                def w_masked():
                    vec.wait_ge(T1.sem, T1.at(c, "logits"))
                    vec.wait_ge(A1.sem, A1.at(c, "ay"))
                    do(c1, vec.tensor_tensor(cols(bufC), cols(p5), sm[:, 0:Q].unsqueeze(2).broadcast_to([P, Q, P]), ALU.add))
                    do(c1, vec.scalar_tensor_tensor(bufC[:, :], bufC[:, :], 0.2, bufC[:, :], ALU.mult, ALU.max))
                    do(c1, vec.tensor_scalar(cols(bufD), adjc[:, :, :], 0.0, None, op0=ALU.is_gt))
                    do(c1, vec.tensor_tensor(bufC[:, :], bufC[:, :], bufD[:, :], ALU.mult))
                    do(c1, vec.tensor_scalar(bufD[:, :], bufD[:, :], NEG, -NEG, op0=ALU.mult, op1=ALU.add))
                    do(c1, vec.tensor_tensor(bufC[:, :], bufC[:, :], bufD[:, :], ALU.add))
                    do(c1, vec.tensor_reduce(sm[:, 4:8], cols(bufC), AX, ALU.max))
                    sig(V1, c, "masked", vec.tensor_tensor(cols(bufC), cols(bufC), sm[:, 4:8].unsqueeze(2).broadcast_to([P, Q, P]), ALU.subtract))

                def w_prob():
                    vec.wait_ge(A1.sem, A1.at(c, "exp"))
                    do(c1, vec.tensor_reduce(sm[:, 4:8], cols(bufC), AX, ALU.add))
                    do(c1, vec.reciprocal(sm[:, 8:12], sm[:, 4:8]))
                    sig(V1, c, "prob", vec.tensor_tensor(cols(bufC), cols(bufC), sm[:, 8:12].unsqueeze(2).broadcast_to([P, Q, P]), ALU.mult))

                def w_zmin():
                    vec.wait_ge(T1.sem, T1.at(c, "hout"))
                    sig(V1, c, "zmin", vec.tensor_scalar(bufC[:, :], p4[:, :], 0.0, None, op0=ALU.min))

                def w_x1():
                    vec.wait_ge(A1.sem, A1.at(c, "elu"))
                    do(c1, vec.scalar_tensor_tensor(bufC[:, :], p4[:, :], 0.0, bufC[:, :], ALU.max, ALU.add))
                    sig(V1, c, "x1", vec.scalar_tensor_tensor(xc, cols(bufC), -1.0, xc, ALU.add, ALU.add))

                def w_xn1():
                    vec.sem_inc(passed, 1)
                    norm(c1, xq, lambda q: xn[:, q, :], (V1, c, "xn1"))

                def w_pay():
                    vec.wait_ge(T1.sem, T1.at(c, "hrow"))
                    pc = pay[:, bass.ds(c * Q, Q), :]
                    h = p6[:, 0:Q * 16].rearrange("p (q h) -> p q h", q=Q)
                    h4 = p6[:, 0:Q * 16].rearrange("p (q h e) -> p q h e", q=Q, h=H0)
                    s3 = small[:, :].rearrange("p (q h) -> p q h", q=Q)
                    s4 = small[:, :].rearrange("p (q h e) -> p q h e", q=Q, h=H0)
                    do(c1, vec.tensor_copy(pc[:, :, H0:PW].rearrange("p q (h f) -> p q h f", h=H0)[:, :, :, 1:1 + E0], h4))
                    do(c1, vec.tensor_tensor(s3, h, w["f_asrc"][:, :].unsqueeze(1).broadcast_to([P, Q, H0 * E0]), ALU.mult), bare=True)
                    do(c1, vec.tensor_reduce(pc[:, :, 0:H0], s4, AX, ALU.add))
                    do(c1, vec.tensor_tensor(s3, h, w["f_adst"][:, :].unsqueeze(1).broadcast_to([P, Q, H0 * E0]), ALU.mult), bare=True)
                    do(c1, vec.tensor_reduce(dn[:, bass.ds(c * Q, Q), :], s4, AX, ALU.add), bare=True)
                    do(c1, vec.tensor_reduce(sm[:, 4:8], pc[:, :, 0:H0].rearrange("p q h -> p h q"), AX, ALU.max))
                    sig(V1, c, "pay", vec.tensor_tensor(gmx[:, :], gmx[:, :], sm[:, 4:8], ALU.max))

                return {0: w_xn, 5: w_masked, 6: w_prob, 9: w_zmin, 10: w_x1, 11: w_xn1, 13: w_pay}

            vec.wait_ge(x_in, 16)
            with vec.Fori(0, NCH) as c:
                c1.turn(c)
                vec.wait_ge(chunk_in, 48 * (c + 1))
                do(c1, vec.tensor_single_scalar(tmpi, dstc, 7, op=ALU.arith_shift_right))
                do(c1, vec.tensor_copy(dhi[:, :], tmpi))
                do(c1, vec.tensor_single_scalar(tmpi, dstc, P - 1, op=ALU.bitwise_and))
                do(c1, vec.tensor_copy(rec[:, :, 1].bitcast(F32), tmpi))
                do(c1, vec.tensor_scalar(rec[:, :, 0], srcc, float(M - 1), None, op0=ALU.min))
                do(c1, vec.tensor_scalar(far, dhi[:, :], NB - 0.5, SKIP, op0=ALU.is_gt, op1=ALU.mult))
                work = stage1(c)

                def onehot(g):
                    prev = T1.at(c, f"ranked{g - 2}") if g >= 2 else T1.at(c - 1, f"ranked{SG - 2 + g}")
                    vec.wait_ge(T1.sem, prev)
                    sig(V1, c, f"onehot{g}", vec.tensor_tensor(
                        O[:, g % 2, :, 0:NB], iota[:, 0:NB].unsqueeze(1).broadcast_to([P, ST, NB]),
                        dhi[:, g * ST:(g + 1) * ST].unsqueeze(2).broadcast_to([P, ST, NB]), ALU.is_equal))

                onehot(0)
                for g in range(SG):
                    vec.wait_ge(T1.sem, T1.at(c, f"rank{g}"))
                    sig(V1, c, f"prod{g}", vec.tensor_tensor(big1[:, :, 0:NB], pR[:, :, 0:NB], O[:, g % 2, :, 0:NB], ALU.mult))
                    do(c1, vec.tensor_reduce(pos[:, :], big1[:, :, 0:NB], AX, ALU.add))
                    vec.wait_ge(scattered[g % 2], FILLED + 128 * (c * (SG // 2) + g // 2))
                    do(c1, vec.tensor_tensor(idx[:, g % 2, :], pos[:, :], far[:, g * ST:(g + 1) * ST], ALU.add))
                    sig(V1, c, f"idx{g}", vec.tensor_copy(recs[:, g % 2, :, :], rec[:, g * ST:(g + 1) * ST, :]))
                    if g + 1 < SG:
                        onehot(g + 1)
                    if g in work:
                        work[g]()
                c1.end()

            vec.wait_ge(guard_ready, 1)
            vec.wait_ge(stores_done, NCH + 1)
            dm = yb[:, :, :, :].rearrange("p q e f -> p (q e f)")[:, 0:NB * 2 * H0].rearrange("p (b h) -> p b h", b=NB)
            guard = dm[:, :, H0:2 * H0]
            do(cm, vec.tensor_copy(dm[:, :, 0:H0], dn))
            do(cm, vec.tensor_tensor(guard, dn, gmall[:, :].unsqueeze(1).broadcast_to([P, NB, H0]), ALU.add))
            do(cm, vec.scalar_tensor_tensor(guard, guard, 0.2, guard, ALU.mult, ALU.max))
            do(cm, vec.tensor_scalar(guard, guard, -1.0, None, op0=ALU.mult))
            do(cm, vec.tensor_tensor(dn, dn, pay[:, :, 0:H0], ALU.add))
            do(cm, vec.scalar_tensor_tensor(dn, dn, 0.2, dn, ALU.mult, ALU.max))
            vec.tensor_tensor(dn, dn, guard, ALU.add).then_inc(tables_ready, 1)
            vec.wait_ge(tables_ready, 1)
            do(cm, vec.tensor_copy(dm3[:, :, 0, :], dm))
            do(cm, vec.tensor_tensor(dm, dm, dm3[:, :, 0, :], ALU.subtract))
            do(cm, vec.tensor_copy(dm3[:, :, 1, :], dm))
            do(cm, vec.tensor_tensor(dm3[:, :, 2, :], dm, dm3[:, :, 1, :], ALU.subtract))
            vec.wait_ge(guard_ready, 2)
            weighted = pay[:, :, H0:PW].rearrange("p b (h f) -> p b h f", h=H0)
            do(cm, vec.tensor_tensor(weighted, weighted, dn.unsqueeze(3).broadcast_to([P, NB, H0, 1 + E0]), ALU.mult))
            do(cm, vec.memset(mixw[:, :, :], 1.0))
            for k, steps in enumerate((V2, VB)):
                vec.memset(sm[:, 12 + k:13 + k], 0.0).then_inc(steps.sem, steps.n)
            vec.memset(small2[:, 0:1], 0.0).then_inc(ring_freed, RING)

            def onehot_rows(g):
                dst = ring_dst[:, bass.ds(g % RING, 1), :, :].rearrange("p o k w -> p (o k) w").bitcast(F32)[:, :, 1:2]
                return vec.tensor_tensor(Og[:, bass.ds(g % 3, 1), :, :].rearrange("p o k e -> p (o k) e"),
                                         iota[:, :].unsqueeze(1).broadcast_to([P, GT, P]), dst.broadcast_to([P, GT, P]), ALU.is_equal)

            def mask():
                return vec.tensor_scalar(big3[:, 0:Q, :], adjc[:, :, :], 0.0, None, op0=ALU.is_gt)

            def allowed(chain):
                do(chain, vec.tensor_tensor(neg[:, :, :], cols(p6), big3[:, 0:Q, :], ALU.max))
                do(chain, vec.tensor_tensor(neg[:, :, :], neg[:, :, :], ident[:, :].unsqueeze(1).broadcast_to([P, Q, P]), ALU.max))
                return vec.tensor_scalar(neg[:, :, :], neg[:, :, :], FAR, -FAR, op0=ALU.mult, op1=ALU.add)

            vec.wait_ge(adj_in, 16)
            mask().then_inc(mask_ahead, 1)
            vec.wait_ge(mask_ahead, 2)
            do(cm, allowed(cm))
            vec.wait_ge(ring_filled, 1)
            onehot_rows(0)
            vec.wait_ge(ring_filled, 2)
            onehot_rows(1).then_inc(VG.sem, VG.n)

            def top2(v, n, sel):
                a, b = cmp1[:, :, 0:n, 0:n], cmp2[:, :, 0:n, 0:n]
                other, own = v.unsqueeze(2).broadcast_to([P, Q, n, n]), v.unsqueeze(3).broadcast_to([P, Q, n, n])
                do(c2, vec.tensor_tensor(a, other, own, ALU.is_gt))
                do(c2, vec.tensor_tensor(b, other, own, ALU.is_equal))
                do(c2, vec.tensor_tensor(b, b, lower[:, 0:n, 0:n].unsqueeze(1).broadcast_to([P, Q, n, n]), ALU.mult))
                do(c2, vec.tensor_tensor(a, a, b, ALU.add))
                do(c2, vec.tensor_reduce(sel, a, AX, ALU.add))
                do(c2, vec.tensor_scalar(sel, sel, 1.5, None, op0=ALU.is_lt))

            def back(c, s):
                cb.turn(c)
                cb.n = s * (Q - 1)
                e = order[s]
                xq = lambda q: X[:, bass.ds(c * Q + q, 1), :].rearrange("p o f -> p (o f)")
                xc = X[:, bass.ds(c * Q, Q), :]
                vec.wait_ge(TB.sem, TB.at(c, f"down{e}"))
                if e == 0:
                    sig(VB, c, "mix0", vec.tensor_tensor(xc, cols(p7), xc, ALU.add))
                    return
                for q in qs:
                    m = vec.scalar_tensor_tensor(xq(q), p7[:, q * P:(q + 1) * P], mixw[:, q, e:e + 1], xq(q), ALU.mult, ALU.add)
                    if q < Q - 1:
                        cb.count(m)
                    else:
                        sig(VB, c, f"mix{e}", m)

            def front(c, behind):
                c2.turn(c)
                start_of = lambda q: vec.value_load(gstart[0:1, bass.ds(c * Q + q, 1)], min_val=2 * q, max_val=CAP // GE)
                xq = lambda q: X[:, bass.ds(c * Q + q, 1), :].rearrange("p o f -> p (o f)")
                xc = X[:, bass.ds(c * Q, Q), :]

                def group(g):
                    cg.turn(g)
                    rows = ring[:, bass.ds(g % RING, 1), :, :].rearrange("p o k f -> p (o k) f")
                    vec.wait_ge(TG.sem, TG.at(g, "dstscore"))
                    d8 = p5[:, 0:GT * 8].rearrange("p (k f) -> p k f", k=GT)
                    do(cg, vec.tensor_tensor(zg[:, :, :], rows[:, :, 0:H0], d8[:, :, 0:H0], ALU.add))
                    do(cg, vec.scalar_tensor_tensor(zg[:, :, :], zg[:, :, :], 0.2, zg[:, :, :], ALU.mult, ALU.max))
                    sig(VG, g, "z", vec.tensor_tensor(zg[:, :, :], zg[:, :, :], d8[:, :, H0:2 * H0], ALU.add))
                    vec.wait_ge(TG.sem, TG.at(g - 1, "sums"))
                    vec.wait_ge(AG.sem, AG.at(g, "exp"))
                    vec.tensor_tensor(Vg[:, :, :].rearrange("p k (h f) -> p k h f", h=H0),
                                      rows[:, :, H0:PW].rearrange("p k (h f) -> p k h f", h=H0),
                                      eg[:, :, :].unsqueeze(3).broadcast_to([P, GT, H0, 1 + E0]), ALU.mult).then_inc(ring_freed, 1)
                    vec.wait_ge(ring_freed, g + RING + 1)
                    do(cg, vec.tensor_copy(V3[:, :, 0, :], Vg[:, :, :]))
                    do(cg, vec.tensor_tensor(Vg[:, :, :], Vg[:, :, :], V3[:, :, 0, :], ALU.subtract))
                    do(cg, vec.tensor_copy(V3[:, :, 1, :], Vg[:, :, :]))
                    vec.tensor_tensor(V3[:, :, 2, :], Vg[:, :, :], V3[:, :, 1, :], ALU.subtract).then_inc(VG.sem, 1)
                    vec.wait_ge(ring_filled, g + 3)
                    onehot_rows(g + 2).then_inc(VG.sem, 1)
                    cg.end()

                g1 = start_of(0)
                for q in qs:
                    g0 = g1
                    group(g0)
                    g1 = start_of(q + 1)
                    with vec.Fori(g0 + 1, g1) as g:
                        group(g)
                vec.wait_ge(TG.sem, TG.at(g1 - 1, "sums"))
                sig(V2, c, "agg", vec.tensor_reduce(agg[:, :, :], p6[:, 0:Q * 3 * VW].rearrange("p (q s f) -> p q f s", q=Q, s=3), AX, ALU.add))
                behind(0)
                do(c2, vec.tensor_tensor(agg[:, :, :], agg[:, :, :], pay[:, bass.ds(c * Q, Q), H0:PW], ALU.add))
                a5 = agg[:, :, :].rearrange("p q (h f) -> p q h f", h=H0)
                s3 = small[:, :].rearrange("p (q h) -> p q h", q=Q)
                t3 = small2[:, :].rearrange("p (q h) -> p q h", q=Q)
                s4 = small[:, :].rearrange("p (q h e) -> p q h e", q=Q, h=H0)
                den = sm[:, 0:16].rearrange("p (q h) -> p q h", q=Q)
                do(c2, vec.tensor_scalar(den, a5[:, :, :, 0], 1e-16, None, op0=ALU.add))
                do(c2, vec.reciprocal(den, den))
                do(c2, vec.tensor_tensor(s4, a5[:, :, :, 1:1 + E0], den.unsqueeze(3).broadcast_to([P, Q, H0, E0]), ALU.mult))
                do(c2, vec.tensor_tensor(s3, s3, w["f_bgat"][:, :].unsqueeze(1).broadcast_to([P, Q, 16]), ALU.add))
                do(c2, vec.tensor_reduce(sm[:, 0:Q], s3, AX, ALU.add))
                do(c2, vec.tensor_scalar(sm[:, 0:Q], sm[:, 0:Q], 1.0 / 16, None, op0=ALU.mult))
                do(c2, vec.tensor_tensor(s3, s3, sm[:, 0:Q].unsqueeze(2).broadcast_to([P, Q, 16]), ALU.subtract))
                do(c2, vec.tensor_tensor(t3, s3, s3, ALU.mult))
                do(c2, vec.tensor_reduce(sm[:, 0:Q], t3, AX, ALU.add))
                do(c2, vec.tensor_scalar(sm[:, 0:Q], sm[:, 0:Q], 1.0 / 16, None, op0=ALU.mult))
                inv_sqrt(c2, sm[:, 0:Q])
                do(c2, vec.tensor_tensor(s3, s3, rstd[:, :].unsqueeze(2).broadcast_to([P, Q, 16]), ALU.mult))
                do(c2, vec.tensor_tensor(s3, s3, w["f_gam"][:, :].unsqueeze(1).broadcast_to([P, Q, 16]), ALU.mult))
                do(c2, vec.tensor_tensor(s3, s3, w["f_bet"][:, :].unsqueeze(1).broadcast_to([P, Q, 16]), ALU.add))
                scr, sel4 = gates[:, :, 0:E0], gates[:, :, E0:2 * E0]
                do(c2, vec.tensor_reduce(scr, small[:, :].rearrange("p (q h e) -> p q e h", q=Q, h=H0), AX, ALU.add))
                do(c2, vec.tensor_scalar(scr, scr, 1.0 / H0, None, op0=ALU.mult))
                top2(scr, E0, sel4)
                do(c2, vec.tensor_reduce(sm[:, 0:Q], scr, AX, ALU.max))
                ex0 = small[:, 0:Q * E0].rearrange("p (q e) -> p q e", q=Q)
                g0_ = small2[:, 0:Q * E0].rearrange("p (q e) -> p q e", q=Q)
                sig(V2, c, "gexp0", vec.tensor_tensor(ex0, scr, sm[:, 0:Q].unsqueeze(2).broadcast_to([P, Q, E0]), ALU.subtract))
                behind(1)
                vec.wait_ge(A2.sem, A2.at(c, "gate0"))
                do(c2, vec.tensor_tensor(g0_, g0_, sel4, ALU.mult))
                do(c2, vec.tensor_reduce(sm[:, 0:Q], g0_, AX, ALU.add))
                do(c2, vec.reciprocal(sm[:, 4:8], sm[:, 0:Q]))
                do(c2, vec.tensor_tensor(mix0[:, :, :], g0_, sm[:, 4:8].unsqueeze(2).broadcast_to([P, Q, E0]), ALU.mult))
                vec.wait_ge(y_in, 16 * (c + 1))
                for e in range(E0):
                    for q in qs:
                        m = vec.scalar_tensor_tensor(xq(q), yb[:, q, e, :], mix0[:, q, e:e + 1], xq(q), ALU.mult, ALU.add)
                        if q < Q - 1:
                            c2.count(m)
                        elif e < E0 - 1:
                            do(c2, m)
                        else:
                            sig(V2, c, "x2", m, bare=True)
                norm(c2, xq, lambda q: xn[:, q, :], (V2, c, "xn"))
                behind(2)

                def keys(q):
                    sig(V2, c, f"keys{q}", vec.tensor_tensor(big1[:, :, :], bufB[:, q * P:(q + 1) * P].unsqueeze(1).broadcast_to([P, H1, P]),
                                                            headmask[:, :].unsqueeze(2).broadcast_to([P, H1, P]), ALU.mult))

                vec.wait_ge(A2.sem, A2.at(c, "kT"))
                keys(0)
                vec.wait_ge(T2.sem, T2.at(c, "v"))
                sig(V2, c, "v", vec.tensor_tensor(vext[:, :, :, 0:HD], p5[:, :].rearrange("p (q h d) -> p q h d", q=Q, h=H1),
                                                  w["a_bv"][:, :].rearrange("p (h d) -> p h d", h=H1).unsqueeze(1).broadcast_to([P, Q, H1, HD]), ALU.add))
                behind(3)

                def shifted(q):
                    vec.wait_ge(T2.sem, T2.at(c, f"PT{q - 1}" if q > 0 else "scores0"))
                    sig(V2, c, f"add{q}", vec.tensor_tensor(big2[:, :, :], pS[:, :, :], neg[:, q:q + 1, :].broadcast_to([P, H1, P]), ALU.add))
                    do(c2, vec.tensor_reduce(mxh[:, :], big2[:, :, :], AX, ALU.max))
                    sig(V2, c, f"max{q}", vec.tensor_tensor(big2[:, :, :], big2[:, :, :], mxh[:, :].unsqueeze(2).broadcast_to([P, H1, P]), ALU.subtract))

                shifted(0)
                keys(1)
                for q in qs:
                    if q < Q - 1:
                        shifted(q + 1)
                    if q < Q - 2:
                        keys(q + 2)
                    vec.wait_ge(T2.sem, T2.at(c, f"ctx{q}"))
                    cx = p5[:, 0:H1 * 17].rearrange("p (h f) -> p h f", h=H1)
                    do(c2, vec.reciprocal(cden[:, :], cx[:, :, HD]))
                    sig(V2, c, f"ctx{q}", vec.tensor_tensor(bufC[:, q * P:(q + 1) * P].rearrange("p (h f) -> p h f", h=H1), cx[:, :, 0:HD],
                                                           cden[:, :].unsqueeze(2).broadcast_to([P, H1, HD]), ALU.mult))
                    if q < 3:
                        behind(4 + q)
                    if q == 2:
                        do(c2, vec.tensor_tensor(xn[:, :, :], xn[:, :, :], w["a_bo"][:, :].unsqueeze(1).broadcast_to([P, Q, P]), ALU.add))
                vec.wait_ge(T2.sem, T2.at(c, "attn"))
                bq = lambda t: (lambda q: t[:, q * P:(q + 1) * P])
                do(c2, vec.tensor_tensor(bufD[:, :], p5[:, :], xn[:, :, :].rearrange("p q f -> p (q f)"), ALU.add))
                norm(c2, bq(bufD), bq(bufD))
                do(c2, vec.tensor_tensor(cols(bufD), cols(bufD), w["a_g1"][:, :].unsqueeze(1).broadcast_to([P, Q, P]), ALU.mult))
                sig(V2, c, "y1", vec.tensor_tensor(cols(bufD), cols(bufD), w["a_b1"][:, :].unsqueeze(1).broadcast_to([P, Q, P]), ALU.add))
                vec.wait_ge(adj_in, 16 * (c + 2))
                sig(V2, c, "mask", mask())
                behind(7)
                vec.wait_ge(T2.sem, T2.at(c, "maskT"))
                sig(V2, c, "allowed", allowed(c2))
                do(c2, vec.tensor_tensor(cols(bufD), cols(bufD), w["a_c2"][:, :].unsqueeze(1).broadcast_to([P, Q, P]), ALU.add))
                do(c2, vec.tensor_tensor(xc, xc, w["a_b2"][:, :].unsqueeze(1).broadcast_to([P, Q, P]), ALU.add))
                vec.wait_ge(T2.sem, T2.at(c, "ff"))
                do(c2, vec.tensor_tensor(bufC[:, :], p5[:, :], bufD[:, :], ALU.add))
                norm(c2, bq(bufC), bq(bufC))
                do(c2, vec.tensor_tensor(cols(bufC), cols(bufC), w["a_g2"][:, :].unsqueeze(1).broadcast_to([P, Q, P]), ALU.mult))
                do(c2, vec.tensor_tensor(xc, cols(bufC), xc, ALU.add), bare=True)
                norm(c2, xq, lambda q: xn[:, q, :], (V2, c, "xn3"))
                behind(8)
                vec.wait_ge(T2.sem, T2.at(c, "router"))
                lg = p5[:, 0:Q * E1].rearrange("p (q e) -> p q e", q=Q)
                do(c2, vec.tensor_reduce(sm[:, 0:Q], lg, AX, ALU.max))
                sig(V2, c, "gexp", vec.tensor_tensor(gates[:, :, :], lg, sm[:, 0:Q].unsqueeze(2).broadcast_to([P, Q, E1]), ALU.subtract))
                vec.wait_ge(A2.sem, A2.at(c, "rexp"))
                do(c2, vec.tensor_reduce(sm[:, 0:Q], gates[:, :, :], AX, ALU.add))
                do(c2, vec.reciprocal(sm[:, 4:8], sm[:, 0:Q]))
                do(c2, vec.tensor_tensor(gates[:, :, :], gates[:, :, :], sm[:, 4:8].unsqueeze(2).broadcast_to([P, Q, E1]), ALU.mult))
                sel8 = small[:, 0:Q * E1].rearrange("p (q e) -> p q e", q=Q)
                top2(gates[:, :, :], E1, sel8)
                do(c2, vec.tensor_tensor(gates[:, :, :], gates[:, :, :], sel8, ALU.mult))
                do(c2, vec.tensor_reduce(sm[:, 0:Q], gates[:, :, :], AX, ALU.add))
                do(c2, vec.reciprocal(sm[:, 4:8], sm[:, 0:Q]))
                sig(V2, c, "gate", vec.tensor_tensor(mixw[:, :, 1:1 + E1], gates[:, :, :], sm[:, 4:8].unsqueeze(2).broadcast_to([P, Q, E1]), ALU.mult))
                c2.end()

            front(0, lambda s: None)
            with vec.Fori(1, NCH) as c:
                front(c, lambda s: back(c - 1, s))
            for s in range(E1 + 1):
                back(NCH - 1, s)


_OUT = ((128, 128, 128), "float32")


def laid_out(i):
    c = np.ascontiguousarray
    rep = lambda v: c(np.broadcast_to(np.asarray(v).reshape(1, -1), (P, np.asarray(v).size)))
    row = lambda v: c(np.asarray(v).reshape(1, -1))
    col = lambda v: c(np.asarray(v).reshape(-1, P).T)
    n = {k: np.asarray(v) for k, v in i.items()}
    m1 = np.concatenate([n["L1_ffn_W1s"][None], n["L1_ffn_W1p"]])
    m2 = np.concatenate([n["L1_ffn_W2s"][None], n["L1_ffn_W2p"]])
    b1 = np.concatenate([n["L1_ffn_b1s"][None], n["L1_ffn_b1p"]])
    b2 = np.concatenate([n["L1_ffn_b2s"][None], n["L1_ffn_b2p"]])
    return {
        "x": c(n["x"]), "adj": c(n["adj"]), "edges": c(n["L0_ffn_edge_index"]),
        "g_W": c(n["L0_gnn_W"]), "g_a12": c(n["L0_gnn_a_12"]), "g_W1": c(n["L0_gnn_W_1"]), "g_W2": c(n["L0_gnn_W_2"]),
        "g_a1": c(n["L0_gnn_a_1"]), "g_a2": c(n["L0_gnn_a_2"]),
        "f_Wgat": c(n["L0_ffn_W_gat"]), "f_asrc": rep(n["L0_ffn_att_src"]), "f_adst": rep(n["L0_ffn_att_dst"]),
        "f_bgat": rep(n["L0_ffn_b_gat"]), "f_gam": rep(n["L0_ffn_ln_gamma"]), "f_bet": rep(n["L0_ffn_ln_beta"]),
        "f_W1": c(n["L0_ffn_W1"].reshape(E0, P, 2, P).transpose(1, 0, 2, 3)),
        "f_b1": c(n["L0_ffn_b1"].reshape(E0, 2, P).transpose(2, 0, 1)),
        "f_W2": c(n["L0_ffn_W2"].reshape(E0, 2, P, P).transpose(2, 0, 1, 3)), "f_b2": row(n["L0_ffn_b2"]),
        "a_Wqkv": c(n["L1_gnn_Wqkv"].T), "a_bqk": col(n["L1_gnn_bqkv"][:2 * P]), "a_bv": rep(n["L1_gnn_bqkv"][2 * P:]),
        "a_Wo": c(n["L1_gnn_Wo"].T), "a_bo": rep(n["L1_gnn_bo"]),
        "a_g1": rep(n["L1_gnn_ln1_g"]), "a_b1": rep(n["L1_gnn_ln1_b"]), "a_g2": rep(n["L1_gnn_ln2_g"]), "a_b2": rep(n["L1_gnn_ln2_b"]),
        "a_W1": c(n["L1_gnn_W1"].T.reshape(P, FC, P)), "a_c1": col(n["L1_gnn_b1"]),
        "a_W2": c(n["L1_gnn_W2"].T.reshape(FC, P, P).transpose(1, 0, 2)), "a_c2": rep(n["L1_gnn_b2"]),
        "m_Wr": c(n["L1_ffn_Wr"]), "m_W1": c(m1.reshape(E1 + 1, P, FC, P).transpose(1, 0, 2, 3)),
        "m_b1": c(b1.reshape(E1 + 1, FC, P).transpose(2, 0, 1)),
        "m_W2": c(m2.reshape(E1 + 1, FC, P, P).transpose(2, 0, 1, 3)), "m_b2": c(b2),
    }


def kernel(**inputs):
    import concourse.bacc as bacc
    from concourse.bass_utils import run_bass_kernel_spmd

    nc = bacc.Bacc("TRN2", target_bir_lowering=False, num_devices=1)
    arrays, aps = {}, {}
    for name, v in laid_out(inputs).items():
        arrays[f"in_{name}"] = v
        aps[name] = nc.dram_tensor(f"in_{name}", v.shape, mybir.dt.from_np(v.dtype), kind="ExternalInput").ap()
    aps["out"] = nc.dram_tensor("out_x", _OUT[0], F32, kind="ExternalOutput").ap()
    program(nc, aps, NB=arrays["in_x"].shape[0], NE=arrays["in_edges"].shape[1])
    r = run_bass_kernel_spmd(nc, [arrays], core_ids=[0])
    return r.results[0]["out_x"]
```
